# Optimizing a Trainium2 kernel written in Bass

```python
import numpy as np
import jax
import jax.numpy as jnp

def _softmax(x, axis=-1):
    return jax.nn.softmax(x, axis=axis)

def _gelu(x):
    return jax.nn.gelu(x, approximate=True)

def _silu(x):
    return jax.nn.silu(x)

def _sigmoid(x):
    return jax.nn.sigmoid(x)

def _layernorm(x, axis=-1, eps=1e-05):
    m = jnp.mean(x, axis=axis, keepdims=True)
    v = jnp.var(x, axis=axis, keepdims=True)
    return (x - m) / jnp.sqrt(v + eps)

def _scatter_add(tgt, idx, src, axis=0):
    return tgt.at[idx].add(src)

def _segment_sum(src, seg, n):
    return jax.ops.segment_sum(src, seg, n)
kernel_name = 'mk_hybrid_d1_jaxref_r8_fbdbdb'

def setup_inputs(seed: int=0):
    np.random.seed(seed)
    _w = jnp.asarray

    def _L0_attn_a_setup():
        import jax, jax.numpy as jnp
        import numpy as np
        D_MODEL = 256
        D_STATE = 128
        D_CONV = 4
        EXPAND = 2
        D_HEAD = 64
        D_INNER = EXPAND * D_MODEL
        N_HEADS = D_INNER // D_HEAD
        CONV_DIM = D_INNER + 2 * D_STATE
        D_IN_PROJ = 2 * D_INNER + 2 * D_STATE + N_HEADS
        CHUNK = 32
        EPS = 1e-05

        def _forward(u, W_in, conv_w, conv_b, dt_bias, A_log, Dp, norm_w, W_out):
            b, l, _ = u.shape
            zxbcdt = u @ W_in.T
            z = zxbcdt[..., :D_INNER]
            xBC = zxbcdt[..., D_INNER:D_INNER + CONV_DIM]
            dt = zxbcdt[..., D_INNER + CONV_DIM:]
            xpad = jnp.pad(xBC, ((0, 0), (D_CONV - 1, 0), (0, 0)))
            xBC = sum((xpad[:, w:w + l, :] * conv_w[:, w] for w in range(D_CONV))) + conv_b
            xBC = jax.nn.silu(xBC)
            x = xBC[..., :D_INNER]
            Bm = xBC[..., D_INNER:D_INNER + D_STATE]
            Cm = xBC[..., D_INNER + D_STATE:]
            dt = jax.nn.softplus(dt + dt_bias)
            A = -jnp.exp(A_log)
            c = l // CHUNK
            dtc = dt.reshape(b, c, CHUNK, (h_ := N_HEADS))
            dA_cs = jnp.cumsum(dtc * A, axis=2)
            xc = x.reshape(b, c, CHUNK, N_HEADS, D_HEAD)
            Bc = Bm.reshape(b, c, CHUNK, D_STATE)
            Cc = Cm.reshape(b, c, CHUNK, D_STATE)
            mask = jnp.tril(jnp.ones((CHUNK, CHUNK), bool))
            diff = dA_cs[:, :, :, None, :] - dA_cs[:, :, None, :, :]
            L = jnp.exp(jnp.where(mask[None, None, :, :, None], diff, -jnp.inf))
            CB = jnp.einsum('bcin,bcjn->bcij', Cc, Bc)
            M = CB[..., None] * L * dtc[:, :, None, :, :]
            y_diag = jnp.einsum('bcijh,bcjhp->bcihp', M, xc)
            decay_last = jnp.exp(dA_cs[:, :, -1:, :] - dA_cs)
            states = jnp.einsum('bcsh,bcsn,bcshp->bchpn', decay_last * dtc, Bc, xc)
            chunk_decay = jnp.exp(dA_cs[:, :, -1, :])

            def step(s, inp):
                st, dec = inp
                return (s * dec[:, :, None, None] + st, s)
            s0 = jnp.zeros((b, N_HEADS, D_HEAD, D_STATE), u.dtype)
            _, prev = jax.lax.scan(step, s0, (states.transpose(1, 0, 2, 3, 4), chunk_decay.transpose(1, 0, 2)))
            prev = prev.transpose(1, 0, 2, 3, 4)
            y_off = jnp.einsum('bcin,bchpn,bcih->bcihp', Cc, prev, jnp.exp(dA_cs))
            y = y_diag + y_off + Dp[None, None, None, :, None] * xc
            y = y.reshape(b, l, D_INNER)
            yg = y * jax.nn.silu(z)
            yg = yg * jax.lax.rsqrt(jnp.mean(yg * yg, axis=-1, keepdims=True) + EPS)
            y = yg * norm_w
            return y @ W_out.T
        key = jax.random.key(seed)
        ks = jax.random.split(key, 8)
        B, L = (2, 512)
        u = jax.random.normal(ks[0], (B, L, D_MODEL), jnp.float32)
        W_in = 0.02 * jax.random.normal(ks[1], (D_IN_PROJ, D_MODEL), jnp.float32)
        conv_w = 0.1 * jax.random.normal(ks[2], (CONV_DIM, D_CONV), jnp.float32)
        conv_b = jnp.zeros((CONV_DIM,), jnp.float32)
        dt = jnp.exp(jax.random.uniform(ks[3], (N_HEADS,)) * (np.log(0.1) - np.log(0.001)) + np.log(0.001))
        dt = jnp.clip(dt, 0.0001, None)
        dt_bias = dt + jnp.log(-jnp.expm1(-dt))
        A_log = jnp.log(jax.random.uniform(ks[4], (N_HEADS,), minval=1.0, maxval=16.0))
        Dp = jnp.ones((N_HEADS,), jnp.float32)
        norm_w = jnp.ones((D_INNER,), jnp.float32)
        W_out = 0.02 * jax.random.normal(ks[5], (D_MODEL, D_INNER), jnp.float32)
        return {'u': u, 'W_in': W_in, 'conv_w': conv_w, 'conv_b': conv_b, 'dt_bias': dt_bias, 'A_log': A_log, 'Dp': Dp, 'norm_w': norm_w, 'W_out': W_out}
    _L0_attn_a_in = _L0_attn_a_setup()

    def _L0_attn_b_setup():
        import jax, jax.numpy as jnp
        import numpy as np
        EPS = 1e-08
        C_RGLRU = 8.0

        def rmsnorm(x, w):
            rms = jnp.sqrt(jnp.mean(x * x, axis=-1, keepdims=True) + EPS)
            return w * (x / rms)

        def causal_depthwise_conv(x, conv_w, conv_b):
            K = conv_w.shape[0]
            S = x.shape[1]
            xp = jnp.pad(x, ((0, 0), (K - 1, 0), (0, 0)))
            y = sum((conv_w[k] * xp[:, k:k + S, :] for k in range(K)))
            return y + conv_b

        def rg_lru(x, ga_W, ga_b, gx_W, gx_b, a_param):
            r = jax.nn.sigmoid(x @ ga_W + ga_b)
            i = jax.nn.sigmoid(x @ gx_W + gx_b)
            log_a = -C_RGLRU * jax.nn.softplus(a_param) * r
            a = jnp.exp(log_a)
            mult = jnp.sqrt(-jnp.expm1(2.0 * log_a))
            b = mult * (i * x)

            def combine(c1, c2):
                a1, b1 = c1
                a2, b2 = c2
                return (a1 * a2, a2 * b1 + b2)
            _, h = jax.lax.associative_scan(combine, (a, b), axis=1)
            return h
        D, H, F, K, B, S = (256, 256, 768, 4, 2, 256)
        key = jax.random.key(seed)
        ks = jax.random.split(key, 16)

        def lin(k, fan_in, shape):
            return jax.random.normal(k, shape, jnp.float32) * fan_in ** (-0.5)
        return {'x': jax.random.normal(ks[0], (B, S, D), jnp.float32), 'norm1_w': jnp.ones((D,), jnp.float32), 'left_W': lin(ks[1], D, (D, H)), 'left_b': jnp.zeros((H,), jnp.float32), 'right_W': lin(ks[2], D, (D, H)), 'right_b': jnp.zeros((H,), jnp.float32), 'conv_w': lin(ks[3], K, (K, H)), 'conv_b': jnp.zeros((H,), jnp.float32), 'ga_W': lin(ks[4], H, (H, H)), 'ga_b': jnp.zeros((H,), jnp.float32), 'gx_W': lin(ks[5], H, (H, H)), 'gx_b': jnp.zeros((H,), jnp.float32), 'a_param': jax.random.uniform(ks[6], (H,), jnp.float32, 0.5, 3.0), 'out_W': lin(ks[7], H, (H, D)), 'out_b': jnp.zeros((D,), jnp.float32), 'norm2_w': jnp.ones((D,), jnp.float32), 'up1_W': lin(ks[8], D, (D, F)), 'up1_b': jnp.zeros((F,), jnp.float32), 'up2_W': lin(ks[9], D, (D, F)), 'up2_b': jnp.zeros((F,), jnp.float32), 'down_W': lin(ks[10], F, (F, D)), 'down_b': jnp.zeros((D,), jnp.float32)}
    _L0_attn_b_in = _L0_attn_b_setup()

    def _L0_ffn_setup():
        import jax, jax.numpy as jnp
        import numpy as np
        H, I, E = (256, 512, 8)
        B, S = (2, 256)
        key = jax.random.key(seed)
        ks = jax.random.split(key, 5)
        scale = 0.02
        return {'hidden_states': jax.random.normal(ks[0], (B, S, H), dtype=jnp.float32), 'router_w': jax.random.normal(ks[1], (H, E), dtype=jnp.float32) * scale, 'gate_w': jax.random.normal(ks[2], (E, H, I), dtype=jnp.float32) * scale, 'up_w': jax.random.normal(ks[3], (E, H, I), dtype=jnp.float32) * scale, 'down_w': jax.random.normal(ks[4], (E, I, H), dtype=jnp.float32) * scale}
    _L0_ffn_in = _L0_ffn_setup()
    _d = {'L0_attn_a_u': _L0_attn_a_in['u'], 'L0_attn_a_W_in': _L0_attn_a_in['W_in'], 'L0_attn_a_conv_w': _L0_attn_a_in['conv_w'], 'L0_attn_a_conv_b': _L0_attn_a_in['conv_b'], 'L0_attn_a_dt_bias': _L0_attn_a_in['dt_bias'], 'L0_attn_a_A_log': _L0_attn_a_in['A_log'], 'L0_attn_a_Dp': _L0_attn_a_in['Dp'], 'L0_attn_a_norm_w': _L0_attn_a_in['norm_w'], 'L0_attn_a_W_out': _L0_attn_a_in['W_out'], 'L0_attn_b_norm1_w': _L0_attn_b_in['norm1_w'], 'L0_attn_b_left_W': _L0_attn_b_in['left_W'], 'L0_attn_b_left_b': _L0_attn_b_in['left_b'], 'L0_attn_b_right_W': _L0_attn_b_in['right_W'], 'L0_attn_b_right_b': _L0_attn_b_in['right_b'], 'L0_attn_b_conv_w': _L0_attn_b_in['conv_w'], 'L0_attn_b_conv_b': _L0_attn_b_in['conv_b'], 'L0_attn_b_ga_W': _L0_attn_b_in['ga_W'], 'L0_attn_b_ga_b': _L0_attn_b_in['ga_b'], 'L0_attn_b_gx_W': _L0_attn_b_in['gx_W'], 'L0_attn_b_gx_b': _L0_attn_b_in['gx_b'], 'L0_attn_b_a_param': _L0_attn_b_in['a_param'], 'L0_attn_b_out_W': _L0_attn_b_in['out_W'], 'L0_attn_b_out_b': _L0_attn_b_in['out_b'], 'L0_attn_b_norm2_w': _L0_attn_b_in['norm2_w'], 'L0_attn_b_up1_W': _L0_attn_b_in['up1_W'], 'L0_attn_b_up1_b': _L0_attn_b_in['up1_b'], 'L0_attn_b_up2_W': _L0_attn_b_in['up2_W'], 'L0_attn_b_up2_b': _L0_attn_b_in['up2_b'], 'L0_attn_b_down_W': _L0_attn_b_in['down_W'], 'L0_attn_b_down_b': _L0_attn_b_in['down_b'], 'L0_ffn_router_w': _L0_ffn_in['router_w'], 'L0_ffn_gate_w': _L0_ffn_in['gate_w'], 'L0_ffn_up_w': _L0_ffn_in['up_w'], 'L0_ffn_down_w': _L0_ffn_in['down_w']}
    _x0 = _d['L0_attn_a_u']
    _d['L0_attn_a_u'] = jax.random.normal(jax.random.fold_in(jax.random.key(seed), 1), (1, 2048, 256), dtype=_x0.dtype)
    del _x0
    return _d

def reference(L0_attn_a_u, L0_attn_a_W_in, L0_attn_a_conv_w, L0_attn_a_conv_b, L0_attn_a_dt_bias, L0_attn_a_A_log, L0_attn_a_Dp, L0_attn_a_norm_w, L0_attn_a_W_out, L0_attn_b_norm1_w, L0_attn_b_left_W, L0_attn_b_left_b, L0_attn_b_right_W, L0_attn_b_right_b, L0_attn_b_conv_w, L0_attn_b_conv_b, L0_attn_b_ga_W, L0_attn_b_ga_b, L0_attn_b_gx_W, L0_attn_b_gx_b, L0_attn_b_a_param, L0_attn_b_out_W, L0_attn_b_out_b, L0_attn_b_norm2_w, L0_attn_b_up1_W, L0_attn_b_up1_b, L0_attn_b_up2_W, L0_attn_b_up2_b, L0_attn_b_down_W, L0_attn_b_down_b, L0_ffn_router_w, L0_ffn_gate_w, L0_ffn_up_w, L0_ffn_down_w):

    def _L0_attn_a_ref(u, W_in, conv_w, conv_b, dt_bias, A_log, Dp, norm_w, W_out):
        import jax, jax.numpy as jnp
        import numpy as np
        D_MODEL = 256
        D_STATE = 128
        D_CONV = 4
        EXPAND = 2
        D_HEAD = 64
        D_INNER = EXPAND * D_MODEL
        N_HEADS = D_INNER // D_HEAD
        CONV_DIM = D_INNER + 2 * D_STATE
        D_IN_PROJ = 2 * D_INNER + 2 * D_STATE + N_HEADS
        CHUNK = 32
        EPS = 1e-05

        def _forward(u, W_in, conv_w, conv_b, dt_bias, A_log, Dp, norm_w, W_out):
            b, l, _ = u.shape
            zxbcdt = u @ W_in.T
            z = zxbcdt[..., :D_INNER]
            xBC = zxbcdt[..., D_INNER:D_INNER + CONV_DIM]
            dt = zxbcdt[..., D_INNER + CONV_DIM:]
            xpad = jnp.pad(xBC, ((0, 0), (D_CONV - 1, 0), (0, 0)))
            xBC = sum((xpad[:, w:w + l, :] * conv_w[:, w] for w in range(D_CONV))) + conv_b
            xBC = jax.nn.silu(xBC)
            x = xBC[..., :D_INNER]
            Bm = xBC[..., D_INNER:D_INNER + D_STATE]
            Cm = xBC[..., D_INNER + D_STATE:]
            dt = jax.nn.softplus(dt + dt_bias)
            A = -jnp.exp(A_log)
            c = l // CHUNK
            dtc = dt.reshape(b, c, CHUNK, (h_ := N_HEADS))
            dA_cs = jnp.cumsum(dtc * A, axis=2)
            xc = x.reshape(b, c, CHUNK, N_HEADS, D_HEAD)
            Bc = Bm.reshape(b, c, CHUNK, D_STATE)
            Cc = Cm.reshape(b, c, CHUNK, D_STATE)
            mask = jnp.tril(jnp.ones((CHUNK, CHUNK), bool))
            diff = dA_cs[:, :, :, None, :] - dA_cs[:, :, None, :, :]
            L = jnp.exp(jnp.where(mask[None, None, :, :, None], diff, -jnp.inf))
            CB = jnp.einsum('bcin,bcjn->bcij', Cc, Bc)
            M = CB[..., None] * L * dtc[:, :, None, :, :]
            y_diag = jnp.einsum('bcijh,bcjhp->bcihp', M, xc)
            decay_last = jnp.exp(dA_cs[:, :, -1:, :] - dA_cs)
            states = jnp.einsum('bcsh,bcsn,bcshp->bchpn', decay_last * dtc, Bc, xc)
            chunk_decay = jnp.exp(dA_cs[:, :, -1, :])

            def step(s, inp):
                st, dec = inp
                return (s * dec[:, :, None, None] + st, s)
            s0 = jnp.zeros((b, N_HEADS, D_HEAD, D_STATE), u.dtype)
            _, prev = jax.lax.scan(step, s0, (states.transpose(1, 0, 2, 3, 4), chunk_decay.transpose(1, 0, 2)))
            prev = prev.transpose(1, 0, 2, 3, 4)
            y_off = jnp.einsum('bcin,bchpn,bcih->bcihp', Cc, prev, jnp.exp(dA_cs))
            y = y_diag + y_off + Dp[None, None, None, :, None] * xc
            y = y.reshape(b, l, D_INNER)
            yg = y * jax.nn.silu(z)
            yg = yg * jax.lax.rsqrt(jnp.mean(yg * yg, axis=-1, keepdims=True) + EPS)
            y = yg * norm_w
            return y @ W_out.T
        return _forward(u, W_in, conv_w, conv_b, dt_bias, A_log, Dp, norm_w, W_out)

    def _L0_attn_b_ref(x, norm1_w, left_W, left_b, right_W, right_b, conv_w, conv_b, ga_W, ga_b, gx_W, gx_b, a_param, out_W, out_b, norm2_w, up1_W, up1_b, up2_W, up2_b, down_W, down_b):
        import jax, jax.numpy as jnp
        import numpy as np
        EPS = 1e-08
        C_RGLRU = 8.0

        def rmsnorm(x, w):
            rms = jnp.sqrt(jnp.mean(x * x, axis=-1, keepdims=True) + EPS)
            return w * (x / rms)

        def causal_depthwise_conv(x, conv_w, conv_b):
            K = conv_w.shape[0]
            S = x.shape[1]
            xp = jnp.pad(x, ((0, 0), (K - 1, 0), (0, 0)))
            y = sum((conv_w[k] * xp[:, k:k + S, :] for k in range(K)))
            return y + conv_b

        def rg_lru(x, ga_W, ga_b, gx_W, gx_b, a_param):
            r = jax.nn.sigmoid(x @ ga_W + ga_b)
            i = jax.nn.sigmoid(x @ gx_W + gx_b)
            log_a = -C_RGLRU * jax.nn.softplus(a_param) * r
            a = jnp.exp(log_a)
            mult = jnp.sqrt(-jnp.expm1(2.0 * log_a))
            b = mult * (i * x)

            def combine(c1, c2):
                a1, b1 = c1
                a2, b2 = c2
                return (a1 * a2, a2 * b1 + b2)
            _, h = jax.lax.associative_scan(combine, (a, b), axis=1)
            return h
        gelu = lambda t: jax.nn.gelu(t, approximate=False)
        xn = rmsnorm(x, norm1_w)
        left = gelu(xn @ left_W + left_b)
        right = rg_lru(causal_depthwise_conv(xn @ right_W + right_b, conv_w, conv_b), ga_W, ga_b, gx_W, gx_b, a_param)
        x1 = left * right @ out_W + out_b + x
        x1n = rmsnorm(x1, norm2_w)
        mlp = gelu(x1n @ up1_W + up1_b) * (x1n @ up2_W + up2_b) @ down_W + down_b
        return mlp + x1

    def _L0_ffn_ref(hidden_states, router_w, gate_w, up_w, down_w):
        import jax, jax.numpy as jnp
        import numpy as np
        H, I, E = (256, 512, 8)
        B, S = (2, 256)
        hidden_shape = hidden_states.shape
        x = hidden_states.reshape(-1, hidden_shape[-1])
        route = jax.nn.sigmoid(x @ router_w)
        max_ind = jnp.argmax(route, axis=1)
        max_prob = jnp.take_along_axis(route, max_ind[:, None], axis=1)
        out = jnp.zeros_like(x)
        num_experts = gate_w.shape[0]
        for e in range(num_experts):
            mask = (max_ind == e)[:, None]
            h = jax.nn.silu(x @ gate_w[e]) * (x @ up_w[e])
            out = out + jnp.where(mask, h @ down_w[e], 0.0)
        out = out * max_prob
        return out.reshape(hidden_shape)
    x = L0_attn_a_u
    x = x + _L0_attn_a_ref(_layernorm(x, axis=-1), L0_attn_a_W_in, L0_attn_a_conv_w, L0_attn_a_conv_b, L0_attn_a_dt_bias, L0_attn_a_A_log, L0_attn_a_Dp, L0_attn_a_norm_w, L0_attn_a_W_out)
    x = x + _L0_ffn_ref(_layernorm(x, axis=-1), L0_ffn_router_w, L0_ffn_gate_w, L0_ffn_up_w, L0_ffn_down_w)
    x = x + _L0_attn_b_ref(_layernorm(x, axis=-1), L0_attn_b_norm1_w, L0_attn_b_left_W, L0_attn_b_left_b, L0_attn_b_right_W, L0_attn_b_right_b, L0_attn_b_conv_w, L0_attn_b_conv_b, L0_attn_b_ga_W, L0_attn_b_ga_b, L0_attn_b_gx_W, L0_attn_b_gx_b, L0_attn_b_a_param, L0_attn_b_out_W, L0_attn_b_out_b, L0_attn_b_norm2_w, L0_attn_b_up1_W, L0_attn_b_up1_b, L0_attn_b_up2_W, L0_attn_b_up2_b, L0_attn_b_down_W, L0_attn_b_down_b)
    x = x + _L0_ffn_ref(_layernorm(x, axis=-1), L0_ffn_router_w, L0_ffn_gate_w, L0_ffn_up_w, L0_ffn_down_w)
    return x

_drawn_inputs = setup_inputs


def setup_inputs(seed=0):
    import zlib

    import numpy as np

    out = dict(_drawn_inputs(seed))
    spreads = {'L0_attn_a_conv_b': (0.0, 0.1),
     'L0_attn_a_Dp': (1.0, 0.2),
     'L0_attn_a_norm_w': (1.0, 0.2),
     'L0_attn_b_norm1_w': (1.0, 0.2),
     'L0_attn_b_left_b': (0.0, 0.33),
     'L0_attn_b_right_b': (0.0, 0.329),
     'L0_attn_b_conv_b': (0.0, 0.316),
     'L0_attn_b_ga_b': (0.0, 0.8),
     'L0_attn_b_gx_b': (0.0, 0.8),
     'L0_attn_b_out_b': (0.0, 0.1),
     'L0_attn_b_norm2_w': (1.0, 0.2),
     'L0_attn_b_up1_b': (0.0, 0.1),
     'L0_attn_b_up2_b': (0.0, 0.1),
     'L0_attn_b_down_b': (0.0, 0.1)}
    factors = {'L0_attn_a_dt_bias': 8.0,
     'L0_attn_a_A_log': 8.0,
     'L0_attn_b_ga_W': 3.818,
     'L0_attn_b_a_param': 8.0,
     'L0_ffn_router_w': 3.185,
     'L0_ffn_gate_w': 2.98,
     'L0_ffn_up_w': 2.952,
     'L0_ffn_down_w': 2.946}
    for name, (base, spread) in spreads.items():
        noise = np.random.default_rng([zlib.crc32(name.encode()), seed]).standard_normal(out[name].shape)
        drawn = base * np.exp(spread * noise) if base else spread * noise
        out[name] = jnp.asarray(drawn.astype(out[name].dtype))
    for name, factor in factors.items():
        out[name] = (out[name] * factor).astype(out[name].dtype)
    return out
```

```python
from contextlib import ExitStack

import concourse.bass as bass
from concourse import mybir

F32 = mybir.dt.float32
I32 = mybir.dt.int32
U32 = mybir.dt.uint32
ALU = mybir.AluOpType
ACT = mybir.ActivationFunctionType
AX = mybir.AxisListType

P = 128
TOKENS, D = 2048, 256
KD = D // P
NT = TOKENS // P
NS = NT // 2
ST = 2 * P

DI, DS, NH, DH, TAPS = 512, 128, 8, 64, 4
KI = DI // P
CB = (DI + 2 * DS) // P
XBC0 = DI
DT0 = DI + CB * P
DPROJ = DT0 + NH
ATANH = (2.000000007877749, 0.6666631593507903, 0.40024853723562315, 0.2796141883332212, 0.28174657270344106)

E, FI = 8, 512
KF = FI // P
F, KU = 768, 768 // P
C_RGLRU = 8.0
MAXT = NT + E + 1


START = 2


def after(n):
    return START + (max(n, 0) if isinstance(n, int) else n)


def at(s, per, k=None):
    return after(s * per + (per if k is None else k))


def wait_apart(e, passed, sem, value):
    e.wait_ge(sem, value)
    e.sem_inc(passed, 1)


class Memory:

    def __init__(self, nc, ctx):
        self.nc, self.ctx = nc, ctx

    def sb(self, name, shape, dt=F32):
        return self.ctx.enter_context(self.nc.sbuf_tensor(name, shape, dt))

    def banks(self, name):
        return [self.ctx.enter_context(self.nc.psum_tensor(f"{name}{i}", [P, 512], F32)) for i in range(8)]

    def sem(self, name):
        return self.ctx.enter_context(self.nc.semaphore(name))


class Phase(Memory):

    def __init__(self, nc, ctx):
        super().__init__(nc, ctx)
        self.sems, self.loop_sems = [], []

    def sem(self, name):
        self.sems.append(super().sem(name))
        return self.sems[-1]

    def loop_sem(self, name):
        self.loop_sems.append(self.sem(name))
        return self.loop_sems[-1]

    def start_loop_sems(self):
        with self.nc.Block() as block:
            for n, on in enumerate((block.sync, block.scalar, block.vector, block.tensor)):
                def _(e, n=n):
                    for s in self.loop_sems[n::4]:
                        e.sem_inc(s, START)
                on(_)

    def clear(self):
        with self.nc.Block() as block:

            @block.gpsimd
            def _(g):
                for s in self.sems:
                    g.sem_clear(s)


def make_constants(nc, m, zeros, zeros_made):
    c = {
        "ident": m.sb("ident", [P, P]),
        "tri_le": m.sb("tri_le", [P, P]),
        "tri_gt": m.sb("tri_gt", [P, P]),
        "tri_lt": m.sb("tri_lt", [P, P]),
        "ones": m.sb("ones", [P, P]),
        "half_neg": m.sb("half_neg", [P, 2]),
        "eps": m.sb("eps", [P, 2]),
    }
    ready, filled = m.sem("const_ready"), m.sem("const_filled")
    with nc.Block() as block:

        @block.gpsimd
        def _(g):
            g.memset(c["ident"][:, :], 0.0).then_inc(filled, 1)
            for name in ("tri_le", "tri_gt", "tri_lt"):
                g.memset(c[name][:, :], 1.0).then_inc(filled, 1)
            g.memset(c["ones"][:, :], 1.0)
            g.memset(c["half_neg"][:, :], -0.5)
            g.memset(c["eps"][:, :], 1e-5)
            g.memset(zeros[:, :], 0.0).then_inc(zeros_made, 1)
            g.wait_ge(filled, 4)
            for name, op, row, col, fill in (("ident", ALU.not_equal, 1, -1, 1.0), ("tri_le", ALU.is_ge, -1, 1, 0.0),
                                             ("tri_gt", ALU.is_gt, 1, -1, 0.0), ("tri_lt", ALU.is_gt, -1, 1, 0.0)):
                g.affine_select(out=c[name][:, :], in_=c[name][:, :], compare_op=op, fill=fill, base=0,
                                pattern=[[col, P]], channel_multiplier=row).then_inc(ready, 1)
            g.wait_ge(ready, 4)
    return c


def mamba_phase(nc, m0, a, c, x, x_loaded, prefetch):
    ident, tri_le, tri_gt, ones = c["ident"], c["tri_le"], c["tri_gt"], c["ones"]
    with ExitStack() as ctx:
        m = Phase(nc, ctx)
        sb, sem = m.sb, m.sem
        b = m.banks("mb")
        winT = sb("winT", [P, KD, DPROJ])
        woutT = sb("woutT", [P, KI, D])
        conv_w, conv_b = sb("conv_w", [P, CB, TAPS]), sb("conv_b", [P, CB])
        norm_w = sb("norm_w", [P, KI])
        dt_bias, neg_a, d_skip = sb("dt_bias", [P, NH]), sb("neg_a", [P, NH]), sb("d_skip", [P, NH])
        stats, mv, rstd = sb("stats", [P, 2, 6]), sb("mv", [P, 2, 2]), sb("rstd", [P, 2, 1])
        veps = sb("veps", [P, 2, 1])
        xn = sb("xn", [P, 2, D])
        xnT = [sb(f"xnT{q}", [P, KD, ST]) for q in range(2)]
        xpre = sb("xpre", [P, CB, TAPS - 1 + ST])
        hth = sb("hth", [P, 2 * CB, ST])
        h, th = hth[:, 0:CB, :], hth[:, CB:2 * CB, :]
        xc = [sb(f"xc{q}", [P, CB, ST]) for q in range(2)]
        dtw = sb("dtw", [P, 8, 2 * NH])
        dt = [sb(f"dt{q}", [P, 2 * NH]) for q in range(2)]
        dA = sb("dA", [P, 2 * NH])
        decay = [sb(f"decay{q}", [P, 2, 2 * NH]) for q in range(2)]
        dA_tri = [sb(f"dA_tri{k}", [P, NH, P]) for k in range(2)]
        L, M = sb("L", [P, NH, P]), sb("M", [P, NH, P])
        cbm, bt = sb("cbm", [P, P]), sb("bt", [P, P])
        xt, xdt, xw, xD = (sb(n, [P, DI]) for n in ("xt", "xdt", "xw", "xD"))
        state, sdec = sb("state", [P, DI]), sb("sdec", [P, DI])
        tz, zs, y, yg = (sb(n, [P, DI]) for n in ("tz", "zs", "y", "yg"))
        ygT = sb("ygT", [P, KI, P])
        ms, mse, rs = sb("ms", [P, 1]), sb("mse", [P, 1]), sb("rs", [P, 1])
        win_raw = hth[:, :, :].rearrange("p b t -> p (b t)")[:, 0:11 * D].rearrange("p (r d) -> p r d", d=D)
        wout_raw = L[:, :, :].rearrange("p h t -> p (h t)")[:, 0:2 * DI].rearrange("p (r i) -> p r i", i=DI)

        win_loaded = [sem(f"win_loaded{k}") for k in range(3)]
        win_ps, win_done = sem("win_ps"), sem("win_done")
        wout_loaded, wout_ps, wout_done = sem("wout_loaded"), sem("wout_ps"), sem("wout_done")
        par_loaded, par_done, waits_passed = sem("par_loaded"), sem("par_done"), sem("waits_passed")
        (stats_done, mv_done, veps_done, rstd_done, xn_done, xnT_ps, xnT_done, xbc_ps, xpre_done, tap0_done, conv_step,
         halo_done, tanh_done, xc_done, dt_ps, dt_raw_done, dt_exp_done, dt_step, tri_done, small_ps,
         decay_done) = (m.loop_sem("a_" + n) for n in (
             "stats_done mv_done veps_done rstd_done xn_done xnT_ps xnT_done xbc_ps xpre_done tap0_done conv_step "
             "halo_done tanh_done xc_done dt_ps dt_raw_done dt_exp_done dt_step tri_done small_ps decay_done").split())
        (xt_ps, cb_ps, D_ps, xt_done, bt_done, cbm_done, L_done, M_done, xdt_done, xw_done, xD_done, sdec_done,
         yoff_ps, z_ps, tz_done, zs_done, yd_ps, st_ps, S_done, y1_done, y2_done, y3_done, yg_done, sq_done, mse_done,
         rs_done, ygT_ps, ygT_done, out_ps, x_done) = (m.loop_sem("b_" + n) for n in (
             "xt_ps cb_ps D_ps xt_done bt_done cbm_done L_done M_done xdt_done xw_done xD_done sdec_done "
             "yoff_ps z_ps tz_done zs_done yd_ps st_ps S_done y1_done y2_done y3_done yg_done sq_done mse_done "
             "rs_done ygT_ps ygT_done out_ps x_done").split())
        NDT = 13

        def heads(ap, n):
            return ap.unsqueeze(2).to_broadcast([P, NH, n])

        def pe_setup(pe):
            for g, (r0, r1) in enumerate(((0, 4), (4, 8), (8, 11))):
                pe.wait_ge(win_loaded[g], 16 * (1 + (g == 2)))
                for k in range(KD):
                    for r in range(r0, r1):
                        n = min(P, DPROJ - r * P)
                        t = pe.transpose(b[1 + 2 * g + k][:, (r - r0) * P:(r - r0) * P + n],
                                         win_raw[0:n, r, k * P:(k + 1) * P], ident[0:n, 0:n])
                    t.then_inc(win_ps, 1)
            pe.wait_ge(wout_loaded, 16)
            for g, bank in enumerate((b[0], b[7])):
                for i in range(2):
                    for r in range(2):
                        ib = 2 * g + i
                        t = pe.transpose(bank[:, (2 * i + r) * P:(2 * i + r + 1) * P],
                                         wout_raw[:, r, ib * P:(ib + 1) * P], ident[:, :])
                t.then_inc(wout_ps, 1)
            pe.wait_ge(win_done, 6)
            pe.wait_ge(wout_done, 4)

        def pe_A1(pe, s, q):
            pe.wait_ge(x_done, after(2 * s - 2))
            pe.wait_ge(xn_done, at(s, 2))
            for t in range(2):
                for k in range(KD):
                    last = pe.transpose(b[0][:, k * ST + t * P:k * ST + (t + 1) * P], xn[:, t, k * P:(k + 1) * P],
                                        ident[:, :])
            last.then_inc(xnT_ps, 1)

        def pe_xbc(pe, s, q, g):
            if g == 0:
                pe.wait_ge(xnT_done, at(s, 1))
                pe.wait_ge(tap0_done, at(s, 3, 0))
            elif g == 1:
                pe.wait_ge(decay_done, after(s))
            else:
                pe.wait_ge(tap0_done, at(s, 3, 1))
            bank = b[1 + g % 2]
            for j in range(2):
                col = XBC0 + (2 * g + j) * P
                for k in range(KD):
                    last = pe.matmul(bank[:, j * ST:(j + 1) * ST], winT[:, k, col:col + P], xnT[q][:, k, :],
                                     start=(k == 0), stop=(k == KD - 1))
            last.then_inc(xbc_ps, 1)

        def pe_dt(pe, s, q):
            pe.wait_ge(tap0_done, at(s, 3, 2))
            for t in range(2):
                for k in range(KD):
                    last = pe.matmul(b[2][:, t * NH:(t + 1) * NH], xnT[q][:, k, t * P:(t + 1) * P],
                                     winT[:, k, DT0:DPROJ], start=(k == 0), stop=(k == KD - 1))
            last.then_inc(dt_ps, 1)

        def pe_small(pe, s, q):
            pe.wait_ge(dt_step, at(s, NDT))
            pe.matmul(b[2][:, 32:48], tri_le[:, :], dA[:, :], start=True, stop=True)
            pe.matmul(b[2][:, 48:64], ones[:, :], dA[:, :], start=True, stop=True).then_inc(small_ps, 1)

        def pe_B1(pe, s, q, t):
            g = 2 * s + t
            pe.wait_ge(xc_done, at(s, 3))
            pe.wait_ge(zs_done, after(g))
            pe.wait_ge(ygT_done, after(g - t))
            if t:
                pe.wait_ge(bt_done, after(g))
                pe.wait_ge(cbm_done, after(g))
            for k in range(KI):
                last = pe.transpose(b[5][:, k * P:(k + 1) * P], xc[q][:, k, t * P:(t + 1) * P], ident[:, :])
            last.then_inc(xt_ps, 1)
            pe.transpose(b[6][:, 0:P], xc[q][:, KI, t * P:(t + 1) * P], ident[:, :])
            pe.matmul(b[6][:, P:2 * P], xc[q][:, KI, t * P:(t + 1) * P], xc[q][:, KI + 1, t * P:(t + 1) * P],
                      start=True, stop=True).then_inc(cb_ps, 1)
            pe.wait_ge(tri_done, after(g + 1))
            pe.wait_ge(y2_done, after(g))
            pe.wait_ge(S_done, after(g + 1))
            for k in range(2):
                last = pe.matmul(b[3 + k][:, :], tri_gt[:, :], dA_tri[t][:, 4 * k:4 * k + 4, :].rearrange("p h t -> p (h t)"),
                                 start=True, stop=True)
            last.then_inc(D_ps, 1)

        def pe_B2(pe, s, q, t):
            g = 2 * s + t
            pe.wait_ge(y1_done, after(g))
            pe.matmul(b[7][:, :], xc[q][:, KI + 1, t * P:(t + 1) * P], state[:, :], start=True,
                      stop=True).then_inc(yoff_ps, 1)
            pe.wait_ge(xt_done, after(g + 1))
            for k in range(KD):
                last = pe.matmul(b[5][:, :], xnT[q][:, k, t * P:(t + 1) * P], winT[:, k, 0:DI],
                                 start=(k == 0), stop=(k == KD - 1))
            last.then_inc(z_ps, 1)

        def pe_B3(pe, s, q, t):
            g = 2 * s + t
            pe.wait_ge(M_done, after(g + 1))
            pe.wait_ge(xdt_done, after(g + 1))
            for hd in range(NH):
                last = pe.matmul(b[3][:, hd * DH:(hd + 1) * DH], M[:, hd, :], xdt[:, hd * DH:(hd + 1) * DH],
                                 start=True, stop=True)
            last.then_inc(yd_ps, 1)
            pe.wait_ge(xw_done, after(g + 1))
            pe.wait_ge(bt_done, after(g + 1))
            pe.matmul(b[4][:, :], bt[:, :], xw[:, :], start=True, stop=True).then_inc(st_ps, 1)

        def pe_B4(pe, s, q, t):
            g = 2 * s + t
            pe.wait_ge(yg_done, after(g + 1))
            if t == 0:
                pe.wait_ge(bt_done, after(g + 2))
                pe.wait_ge(cbm_done, after(g + 2))
            for k in range(KI):
                last = pe.transpose(b[6][:, k * P:(k + 1) * P], yg[:, k * P:(k + 1) * P], ident[:, :])
            last.then_inc(ygT_ps, 1)
            pe.wait_ge(ygT_done, after(g + 1))
            if t == 0 and not (isinstance(s, int) and s == NS - 1):
                pe.wait_ge(xnT_done, after(s + 2))
            if t:
                pe.wait_ge(x_done, after(g))
            for k in range(KI):
                last = pe.matmul(b[0][:, t * D:(t + 1) * D], ygT[:, k, :], woutT[:, k, :], start=(k == 0),
                                 stop=(k == KI - 1))
            last.then_inc(out_ps, 1)

        def act_setup(act):
            act.wait_ge(par_loaded, 16 * 6)
            act.activation(neg_a[:, :], neg_a[:, :], ACT.Exp).then_inc(par_done, 1)
            for i in (0, 2, 4):
                act.wait_ge(win_ps, i + 1)
                act_copy_win(act, i)
            for g in range(2):
                act.wait_ge(wout_ps, g + 1)
                act.wait_ge(par_done, 2)
                for i in range(2):
                    act.activation(woutT[:, 2 * g + i, :], (b[0], b[7])[g][:, i * D:(i + 1) * D], ACT.Copy,
                                   scale=norm_w[:, 2 * g + i:2 * g + i + 1]).then_inc(wout_done, 1)

        def win_group(i):
            g, k = i // 2, i % 2
            n = (4 * P, 4 * P, DPROJ - 8 * P)[g]
            return winT[:, k, g * 4 * P:g * 4 * P + n], b[1 + i][:, 0:n]

        def act_copy_win(act, i):
            act.activation(*win_group(i), ACT.Copy).then_inc(win_done, 1)

        def act_A1(act, s, q):
            act.wait_ge(xnT_ps, at(s, 1))
            act.wait_ge(z_ps, after(2 * s - 2))
            act.activation(xnT[q][:, :, :].rearrange("p k t -> p (k t)"), b[0][:, :], ACT.Copy).then_inc(xnT_done, 1)

        def act_xbc(act, s, q, g):
            act.wait_ge(xbc_ps, at(s, 3, g + 1))
            act.wait_ge(halo_done, at(s, 3, g + 1))
            act.wait_ge(xc_done, at(s, 3, 0))
            bank = b[1 + g % 2][:, :].rearrange("p (j t) -> p j t", j=2)
            act.activation(xpre[:, 2 * g:2 * g + 2, TAPS - 1:], bank, ACT.Copy).then_inc(xpre_done, 1)
            for j in range(2):
                i = act.activation(h[:, 2 * g + j, :], bank[:, j, :], ACT.Identity,
                                   scale=conv_w[:, 2 * g + j, TAPS - 1:TAPS], bias=conv_b[:, 2 * g + j:2 * g + j + 1])
            i.then_inc(tap0_done, 1)

        def act_tanh(act, s, q, g):
            act.wait_ge(conv_step, at(s, 18, 6 * g + 6))
            act.activation(th[:, 2 * g:2 * g + 2, :], h[:, 2 * g:2 * g + 2, :], ACT.Tanh).then_inc(tanh_done, 1)

        def act_dt(act, s, q):
            act.wait_ge(dt_step, at(s, NDT, 2))
            act.activation(dtw[:, 2, :], dtw[:, 1, :], ACT.Exp).then_inc(dt_exp_done, 1)

        def act_decay(act, s, q):
            act.wait_ge(small_ps, at(s, 1))
            act.wait_ge(y1_done, after(2 * s - 2))
            act.wait_ge(sdec_done, after(2 * s - 2))
            act.activation(decay[q][:, :, :].rearrange("p a b -> p (a b)"), b[2][:, 32:64], ACT.Exp).then_inc(
                decay_done, 1)

        def act_B1(act, s, q, t):
            g = 2 * s + t
            act.wait_ge(xt_ps, after(g + 1))
            act.wait_ge(xdt_done, after(g))
            act.wait_ge(xD_done, after(g))
            act.activation(xt[:, :], b[5][:, :], ACT.Copy).then_inc(xt_done, 1)
            act.wait_ge(cb_ps, after(g + 1))
            act.wait_ge(st_ps, after(g))
            act.activation(bt[:, :], b[6][:, 0:P], ACT.Copy).then_inc(bt_done, 1)
            act.wait_ge(D_ps, after(g + 1))
            act.wait_ge(M_done, after(g))
            act.wait_ge(xw_done, after(g))
            for k in range(2):
                i = act.activation(L[:, 4 * k:4 * k + 4, :].rearrange("p h t -> p (h t)"), b[3 + k][:, :], ACT.Exp)
            i.then_inc(L_done, 1)

        def act_B2(act, s, q, t):
            g = 2 * s + t
            act.wait_ge(z_ps, after(g + 1))
            act.wait_ge(zs_done, after(g))
            act.activation(tz[:, :], b[5][:, :], ACT.Tanh, scale=0.5).then_inc(tz_done, 1)

        def act_B3(act, s, q, t):
            g = 2 * s + t
            act.wait_ge(yg_done, after(g + 1))
            act.wait_ge(mse_done, after(g))
            act.activation(tz[:, :], yg[:, :], ACT.Square, scale=0.5 * DI ** -0.5, accum_out=ms[:, :]).then_inc(
                sq_done, 1)

        def act_B4(act, s, q, t):
            g = 2 * s + t
            act.wait_ge(ygT_ps, after(g + 1))
            act.wait_ge(out_ps, after(g))
            act.activation(ygT[:, :, :].rearrange("p k t -> p (k t)"), b[6][:, :], ACT.Copy).then_inc(ygT_done, 1)

        def dve_setup(v):
            v.memset(state[:, :], 0.0).then_inc(S_done, 1)
            v.memset(xpre[:, :, 0:TAPS - 1], 0.0).then_inc(halo_done, 3)
            v.wait_ge(par_loaded, 16 * 6)
            v.tensor_scalar(conv_w[:, :, :], conv_w[:, :, :], 0.5, None, ALU.mult)
            v.tensor_scalar(conv_b[:, :], conv_b[:, :], 0.5, None, ALU.mult)
            v.tensor_scalar(norm_w[:, :], norm_w[:, :], 0.5, None, ALU.mult).then_inc(par_done, 1)
            v.wait_ge(par_done, 2)
            v.tensor_scalar(neg_a[:, :], neg_a[:, :], -1.0, None, ALU.mult).then_inc(par_done, 1)
            for i in (1, 3, 5):
                v.wait_ge(win_ps, i + 1)
                v.tensor_copy(*win_group(i)).then_inc(win_done, 1)
            v.wait_ge(par_done, 3)

        def dve_A1(v, s, q):
            for t in range(2):
                v.wait_ge(rstd_done, after(s))
                v.bn_stats(stats[:, t, :], x[:, bass.ds(2 * s + t, 1), :].rearrange("p a d -> p (a d)")).then_inc(
                    stats_done, 1)
            for t in range(2):
                wait_apart(v, waits_passed, stats_done, at(s, 2, t + 1))
                v.bn_aggr(mv[:, t, :], stats[:, t, :]).then_inc(mv_done, 1)
            v.wait_ge(rstd_done, after(s + 1))
            v.wait_ge(xnT_ps, after(s))
            for t in range(2):
                v.tensor_scalar(xn[:, t, :], x[:, bass.ds(2 * s + t, 1), :].rearrange("p a d -> p (a d)"),
                                mv[:, t, 0:1], rstd[:, t, :], ALU.subtract, ALU.mult).then_inc(xn_done, 1)

        def dve_conv(v, s, q, g):
            v.wait_ge(tap0_done, at(s, 3, g + 1))
            for n, tap in enumerate((2, 1, 0)):
                for j in range(2):
                    if n:
                        v.wait_ge(conv_step, at(s, 18, 6 * g + 2 * n + j - 1))
                    blk = 2 * g + j
                    v.scalar_tensor_tensor(out=h[:, blk, :], in0=xpre[:, blk, tap:tap + ST], scalar=conv_w[:, blk, tap:tap + 1],
                                           in1=h[:, blk, :], op0=ALU.mult, op1=ALU.add).then_inc(conv_step, 1)
            v.wait_ge(conv_step, at(s, 18, 6 * g + 6))
            v.tensor_copy(xpre[:, 2 * g:2 * g + 2, 0:TAPS - 1], xpre[:, 2 * g:2 * g + 2, ST:ST + TAPS - 1]).then_inc(
                halo_done, 1)

        def dve_silu(v, s, q, g):
            v.wait_ge(tanh_done, at(s, 3, g + 1))
            v.wait_ge(yoff_ps, after(2 * s - 2))
            v.scalar_tensor_tensor(out=xc[q][:, 2 * g:2 * g + 2, :], in0=th[:, 2 * g:2 * g + 2, :], scalar=1.0,
                                   in1=h[:, 2 * g:2 * g + 2, :], op0=ALU.add, op1=ALU.mult).then_inc(xc_done, 1)

        def dve_dt(v, s, q):
            vv, nv, e, den, r, z, z2, p = (dtw[:, i, :] for i in range(8))
            k = [0]

            def step(instruction):
                k[0] += 1
                instruction.then_inc(dt_step, 1)
                v.wait_ge(dt_step, at(s, NDT, k[0]))

            v.wait_ge(dt_ps, at(s, 1))
            two = lambda ap: ap.unsqueeze(1).to_broadcast([P, 2, NH])
            split = lambda ap: ap.rearrange("p (a b) -> p a b", a=2)
            step(v.tensor_tensor(split(vv), split(b[2][:, 0:2 * NH]), two(dt_bias[:, :]), ALU.add))
            step(v.scalar_tensor_tensor(out=nv, in0=vv, scalar=-1.0, in1=vv, op0=ALU.mult, op1=ALU.min))
            v.wait_ge(dt_exp_done, at(s, 1))
            step(v.tensor_scalar(den, e, 2.0, None, ALU.add))
            step(v.reciprocal(r, den))
            step(v.tensor_tensor(z, e, r, ALU.mult))
            step(v.tensor_tensor(z2, z, z, ALU.mult))
            step(v.tensor_scalar(p, z2, ATANH[4], ATANH[3], ALU.mult, ALU.add))
            step(v.scalar_tensor_tensor(out=p, in0=p, scalar=0.0, in1=z2, op0=ALU.add, op1=ALU.mult))
            step(v.scalar_tensor_tensor(out=p, in0=p, scalar=ATANH[2], in1=z2, op0=ALU.add, op1=ALU.mult))
            step(v.scalar_tensor_tensor(out=p, in0=p, scalar=ATANH[1], in1=z2, op0=ALU.add, op1=ALU.mult))
            step(v.scalar_tensor_tensor(out=p, in0=p, scalar=ATANH[0], in1=z, op0=ALU.add, op1=ALU.mult))
            v.wait_ge(xdt_done, after(2 * s - 2))
            step(v.scalar_tensor_tensor(out=dt[q][:, :], in0=vv, scalar=0.0, in1=p, op0=ALU.max, op1=ALU.add))
            v.wait_ge(small_ps, after(s))
            v.wait_ge(tri_done, after(2 * s))
            step(v.tensor_tensor(split(dA[:, :]), split(dt[q][:, :]), two(neg_a[:, :]), ALU.mult))

        def dve_cbm(v, s, q, t):
            g = 2 * s + t
            v.wait_ge(bt_done, after(g + 1))
            v.tensor_tensor(cbm[:, :], b[6][:, P:2 * P], tri_le[:, :], ALU.mult).then_inc(cbm_done, 1)

        def dve_M(v, s, q, t):
            g = 2 * s + t
            v.wait_ge(L_done, after(g + 1))
            v.wait_ge(cbm_done, after(g + 1))
            v.wait_ge(yd_ps, after(g))
            v.tensor_tensor(M[:, :, :], L[:, :, :], cbm[:, :].unsqueeze(1).to_broadcast([P, NH, P]),
                            ALU.mult).then_inc(M_done, 1)

        def dve_z(v, s, q, t):
            g = 2 * s + t
            v.wait_ge(tz_done, after(g + 1))
            v.scalar_tensor_tensor(out=zs[:, :], in0=tz[:, :], scalar=1.0, in1=b[5][:, :], op0=ALU.add,
                                   op1=ALU.mult).then_inc(zs_done, 1)

        def dve_y(v, s, q, t):
            g = 2 * s + t
            byhead = lambda ap: ap.rearrange("p (h d) -> p h d", h=NH)
            v.wait_ge(yoff_ps, after(g + 1))
            v.wait_ge(decay_done, after(s + 1))
            v.tensor_tensor(byhead(y[:, :]), byhead(b[7][:, :]), heads(decay[q][:, 0, t * NH:(t + 1) * NH], DH),
                            ALU.mult).then_inc(y1_done, 1)
            v.wait_ge(st_ps, after(g + 1))
            v.wait_ge(sdec_done, after(g + 1))
            v.tensor_tensor(state[:, :], sdec[:, :], b[4][:, :], ALU.add).then_inc(S_done, 1)
            v.wait_ge(y1_done, after(g + 1))
            v.wait_ge(yd_ps, after(g + 1))
            v.tensor_tensor(y[:, :], y[:, :], b[3][:, :], ALU.add).then_inc(y2_done, 1)
            v.wait_ge(y2_done, after(g + 1))
            v.wait_ge(xD_done, after(g + 1))
            v.tensor_tensor(y[:, :], y[:, :], xD[:, :], ALU.add).then_inc(y3_done, 1)
            v.wait_ge(y3_done, after(g + 1))
            v.wait_ge(zs_done, after(g + 1))
            v.wait_ge(sq_done, after(g))
            v.wait_ge(ygT_ps, after(g))
            v.tensor_tensor(yg[:, :], y[:, :], zs[:, :], ALU.mult).then_inc(yg_done, 1)

        def dve_x(v, s, q, t):
            g = 2 * s + t
            v.wait_ge(out_ps, after(g + 1))
            v.wait_ge(rs_done, after(g + 1))
            xs = x[:, bass.ds(g, 1), :].rearrange("p a d -> p (a d)")
            v.scalar_tensor_tensor(out=xs, in0=b[0][:, t * D:(t + 1) * D], scalar=rs[:, :], in1=xs, op0=ALU.mult,
                                   op1=ALU.add).then_inc(x_done, 1)

        def pool_A1(g_, s, q):
            g_.wait_ge(mv_done, at(s, 2))
            g_.tensor_tensor(veps[:, :, :], mv[:, :, 1:2], c["eps"][:, :].unsqueeze(2), ALU.add).then_inc(veps_done, 1)
            g_.wait_ge(veps_done, after(s + 1))
            g_.wait_ge(xn_done, after(2 * s))
            g_.tensor_tensor(rstd[:, :, :], veps[:, :, :], c["half_neg"][:, :].unsqueeze(2), ALU.pow).then_inc(
                rstd_done, 1)

        def pool_tri(g_, s, q):
            g_.wait_ge(dt_step, at(s, NDT))
            for t in range(2):
                g_.wait_ge(D_ps, after(2 * s - 1 + t))
                g_.tensor_tensor(dA_tri[t][:, :, :], tri_le[:, :].unsqueeze(1).to_broadcast([P, NH, P]),
                                 heads(dA[:, t * NH:(t + 1) * NH], P), ALU.mult).then_inc(tri_done, 1)

        def pool_B2(g_, s, q, t):
            g = 2 * s + t
            byhead = lambda ap: ap.rearrange("p (h d) -> p h d", h=NH)
            g_.wait_ge(xt_done, after(g + 1))
            g_.wait_ge(dt_step, at(s, NDT))
            g_.wait_ge(yd_ps, after(g))
            g_.tensor_tensor(byhead(xdt[:, :]), byhead(xt[:, :]), heads(dt[q][:, t * NH:(t + 1) * NH], DH),
                             ALU.mult).then_inc(xdt_done, 1)
            g_.wait_ge(L_done, after(g + 1))
            g_.wait_ge(xdt_done, after(g + 1))
            g_.wait_ge(st_ps, after(g))
            g_.tensor_tensor(byhead(xw[:, :]), byhead(xdt[:, :]), L[:, :, P - 1:P].to_broadcast([P, NH, DH]),
                             ALU.mult).then_inc(xw_done, 1)
            g_.wait_ge(S_done, after(g + 1))
            g_.wait_ge(decay_done, after(s + 1))
            g_.tensor_tensor(byhead(sdec[:, :]), byhead(state[:, :]), heads(decay[q][:, 1, t * NH:(t + 1) * NH], DH),
                             ALU.mult).then_inc(sdec_done, 1)
            g_.wait_ge(y3_done, after(g))
            g_.tensor_tensor(byhead(xD[:, :]), byhead(xt[:, :]), heads(d_skip[:, :], DH), ALU.mult).then_inc(
                xD_done, 1)

        def pool_B3(g_, s, q, t):
            g = 2 * s + t
            g_.wait_ge(sq_done, after(g + 1))
            g_.tensor_tensor(mse[:, :], ms[:, :], c["eps"][:, 0:1], ALU.add).then_inc(mse_done, 1)
            g_.wait_ge(mse_done, after(g + 1))
            g_.wait_ge(x_done, after(g))
            g_.tensor_tensor(rs[:, :], mse[:, :], c["half_neg"][:, 0:1], ALU.pow).then_inc(rs_done, 1)

        def program(e, stage_a, stage_b, before_loop=lambda: None):
            A1, A2a, A2b, A3 = stage_a
            B1, B2, B3, B4 = stage_b

            def run_a(s, q):
                for piece in (A1, A2a, A2b, A3):
                    piece(e, s, q)

            def body(s, q, ahead=True):
                B1(e, s, q, 0)
                if ahead:
                    A1(e, s + 1, 1 - q)
                B2(e, s, q, 0)
                B3(e, s, q, 0)
                if ahead:
                    A2a(e, s + 1, 1 - q)
                B1(e, s, q, 1)
                B2(e, s, q, 1)
                B4(e, s, q, 0)
                if ahead:
                    A2b(e, s + 1, 1 - q)
                B3(e, s, q, 1)
                if ahead:
                    A3(e, s + 1, 1 - q)
                B4(e, s, q, 1)

            run_a(0, 0)
            before_loop()
            with e.Fori(0, NS // 2 - 1) as i:
                body(2 * i, 0)
                body(2 * i + 1, 1)
            body(NS - 2, 0)
            body(NS - 1, 1, ahead=False)

        def nothing(*_):
            pass

        def both(*pieces):
            def piece(*args):
                for p in pieces:
                    p(*args)
            return piece

        def group(fn, g):
            return lambda e, s, q: fn(e, s, q, g)

        m.start_loop_sems()
        with nc.Block() as block:

            @block.sync
            def _(sp):
                for g, (r0, r1) in ((1, (4, 8)), (2, (8, 10)), (0, (0, 4))):
                    sp.dma_start(win_raw[:, r0:r1, :],
                                 a["W_in"][r0 * P:r1 * P, :].rearrange("(r p) d -> p r d", p=P)).then_inc(win_loaded[g], 16)
                sp.dma_start(win_raw[0:NH, 10, :], a["W_in"][DT0:DPROJ, :]).then_inc(win_loaded[2], 16)
                sp.dma_start(wout_raw, a["W_out"].rearrange("(r p) i -> p r i", p=P)).then_inc(wout_loaded, 16)
                for k in range(3):
                    sp.wait_ge(win_loaded[k], 16 * (1 + (k == 2)))
                sp.wait_ge(wout_loaded, 16)
                for t in range(4):
                    sp.wait_ge(x_loaded[t], 16)
                sp.wait_ge(par_loaded, 16 * 6)
                prefetch(sp)

            @block.tensor
            def _(pe):
                pe_setup(pe)
                program(pe, (pe_A1, both(group(pe_xbc, 0), group(pe_xbc, 1)), both(group(pe_xbc, 2), pe_dt), pe_small),
                        (pe_B1, pe_B2, pe_B3, pe_B4))

            @block.scalar
            def _(act):
                act.dma_start(conv_w[:, :, :], a["conv_w"].rearrange("(r p) w -> p r w", p=P)).then_inc(par_loaded, 16)
                for dst, src in ((conv_b, "conv_b"), (norm_w, "norm_w")):
                    act.dma_start(dst[:, :], a[src].rearrange("(r p) -> p r", p=P), allow_slow_non_contiguous=True).then_inc(par_loaded, 16)
                for dst, src in ((dt_bias, "dt_bias"), (neg_a, "A_log"), (d_skip, "Dp")):
                    act.dma_start(dst[:, :], a[src].partition_broadcast(P)).then_inc(par_loaded, 16)
                for t in range(4):
                    act.dma_start(x[:, 4 * t:4 * t + 4, :], a["u"][0, 4 * t * P:(4 * t + 4) * P, :].rearrange(
                        "(r p) d -> p r d", p=P)).then_inc(x_loaded[t], 16)
                act_setup(act)
                act.wait_ge(par_done, 3)

                program(act, (act_A1, both(group(act_xbc, 0), group(act_xbc, 1), group(act_tanh, 0), group(act_tanh, 1)),
                              both(group(act_xbc, 2), group(act_tanh, 2)), both(act_dt, act_decay)), (act_B1, act_B2, act_B3, act_B4))

            @block.vector
            def _(v):
                dve_setup(v)
                v.wait_ge(x_loaded[0], 16)

                def rest_of_x():
                    for t in range(1, 4):
                        v.wait_ge(x_loaded[t], 16)
                program(v, (dve_A1, both(group(dve_conv, 0), group(dve_conv, 1), group(dve_silu, 0), group(dve_silu, 1)),
                            both(group(dve_conv, 2), group(dve_silu, 2)), dve_dt),
                        (dve_cbm, both(dve_M, dve_z), dve_y, dve_x), rest_of_x)

            @block.gpsimd
            def _(g_):
                g_.wait_ge(par_loaded, 16 * 6)
                program(g_, (pool_A1, nothing, nothing, pool_tri), (nothing, pool_B2, pool_B3, nothing))
        m.clear()


def moe_phase(nc, c, w, slots, slots_zeroed, x, tag, prefetch):
    ident, tri_lt, ones = c["ident"], c["tri_lt"], c["ones"]
    slots_in, slots_out = slots
    with ExitStack() as ctx:
        m = Phase(nc, ctx)
        m.tag = tag
        sb, sem, loop_sem = m.sb, m.sem, m.loop_sem
        b = m.banks(tag + "b")
        stats, mv, rstd, veps = (sb(tag + n, s) for n, s in (
            ("stats", [P, 2, 6]), ("mv", [P, 2, 2]), ("rstd", [P, 2, 1]), ("veps", [P, 2, 1])))
        xn = sb(tag + "xn", [P, NT, D])
        xs = [sb(f"{tag}xs{q}", [P, 2, D]) for q in range(2)]
        xnT = [sb(f"{tag}xnT{q}", [P, KD, ST]) for q in range(2)]
        route = sb(tag + "route", [P, NT, E])
        prio, thresh, tile_no = sb(tag + "prio", [P, E]), sb(tag + "thresh", [P, NT]), sb(tag + "tile_no", [P, MAXT])
        seg = sb(tag + "seg", [P, E, NT])
        prob, best = sb(tag + "prob", [P, NT]), sb(tag + "best", [P, NT])
        eq, onehot = sb(tag + "eq", [P, NT, E]), sb(tag + "onehot", [P, NT, E])
        tot, cum, place = (sb(tag + n, [P, E, NT]) for n in ("tot", "cum", "place"))
        pos, pos_i = sb(tag + "pos", [P, NT]), sb(tag + "pos_i", [P, NT], U32)
        over = sb(tag + "over", [P, E, NT])
        need, ends, first = sb(tag + "need", [P, E]), sb(tag + "ends", [P, E]), sb(tag + "first", [P, E])
        past, expert = sb(tag + "past", [P, MAXT, E]), sb(tag + "expert", [P, MAXT])
        table = sb(tag + "table", [1, MAXT], I32)
        small_i = sb(tag + "small_i", [1, 3], I32)
        xin, xT = sb(tag + "xin", [P, D]), sb(tag + "xT", [P, KD, P])
        sg, h, yout = (sb(tag + n, [P, s]) for n, s in (("sg", FI), ("h", FI), ("y", D)))
        hT = sb(tag + "hT", [P, KF, P])

        (stats_done, mv_done, veps_done, rstd_done, xs_done, xn_done, xnT_ps, xnT_done, logit_ps, route_done) = (
            loop_sem(tag + n) for n in
            "stats_done mv_done veps_done rstd_done xs_done xn_done xnT_ps xnT_done logit_ps route_done".split())
        tables_made, onehot_done, prefix_ps, group_step, scattered, waits_passed, waits_passed_g = (
            sem(tag + n) for n in "tables_made onehot_done prefix_ps group_step scattered waits_passed waits_passed_g".split())
        xin_loaded, y_stored = loop_sem(tag + "xin_loaded"), loop_sem(tag + "y_stored")
        xT_ps, xT_done, gu_ps, sg_done, h_done, hT_ps, hT_done, y_ps, y_done = (
            loop_sem(tag + n) for n in "xT_ps xT_done gu_ps sg_done h_done hT_ps hT_done y_ps y_done".split())
        gathered = [sem(f"{tag}gathered{k}") for k in range(4)]
        combined = sem(tag + "combined")
        NGROUP, NPOS = 20, 16

        def supertiles(e, step):
            with e.Fori(0, NS // 2) as i:
                step(e, 2 * i, 0)
                step(e, 2 * i + 1, 1)

        def pe_front(pe, s, q):
            pe.wait_ge(xs_done, at(s, 2))
            for t in range(2):
                for k in range(KD):
                    last = pe.transpose(b[q][:, k * ST + t * P:k * ST + (t + 1) * P],
                                        xs[q][:, t, k * P:(k + 1) * P], ident[:, :])
            last.then_inc(xnT_ps, 1)
            pe.wait_ge(xnT_done, after(s + 1))
            for t in range(2):
                for k in range(KD):
                    last = pe.matmul(b[2 + q][:, t * E:(t + 1) * E], xnT[q][:, k, t * P:(t + 1) * P], w["router"][:, k, :],
                                     start=(k == 0), stop=(k == KD - 1))
            last.then_inc(logit_ps, 1)

        def act_front(act, s, q):
            act.wait_ge(xnT_ps, after(s + 1))
            act.activation(xnT[q][:, :, :].rearrange("p k t -> p (k t)"), b[q][:, :], ACT.Copy).then_inc(xnT_done, 1)
            act.wait_ge(logit_ps, after(s + 1))
            act.activation(route[:, bass.ds(2 * s, 2), :].rearrange("p t e -> p (t e)"), b[2 + q][:, 0:2 * E],
                           ACT.Sigmoid).then_inc(route_done, 1)

        def dve_front(v, s, q):
            for t in range(2):
                v.wait_ge(rstd_done, after(s))
                v.bn_stats(stats[:, t, :], x[:, bass.ds(2 * s + t, 1), :].rearrange("p a d -> p (a d)")).then_inc(
                    stats_done, 1)
            for t in range(2):
                wait_apart(v, waits_passed, stats_done, at(s, 2, t + 1))
                v.bn_aggr(mv[:, t, :], stats[:, t, :]).then_inc(mv_done, 1)
            v.wait_ge(rstd_done, after(s + 1))
            v.wait_ge(xnT_ps, after(s - 1))
            v.wait_ge(xn_done, after(s - 1))
            for t in range(2):
                v.tensor_scalar(xs[q][:, t, :],
                                x[:, bass.ds(2 * s + t, 1), :].rearrange("p a d -> p (a d)"),
                                mv[:, t, 0:1], rstd[:, t, :], ALU.subtract, ALU.mult).then_inc(xs_done, 1)

        def pool_front(g, s, q):
            g.wait_ge(mv_done, at(s, 2))
            g.tensor_tensor(veps[:, :, :], mv[:, :, 1:2], c["eps"][:, :].unsqueeze(2), ALU.add).then_inc(veps_done, 1)
            g.wait_ge(veps_done, after(s + 1))
            g.wait_ge(xs_done, after(2 * s))
            g.tensor_tensor(rstd[:, :, :], veps[:, :, :], c["half_neg"][:, :].unsqueeze(2), ALU.pow).then_inc(
                rstd_done, 1)
            wait_apart(g, waits_passed_g, xs_done, at(s, 2))
            g.tensor_copy(xn[:, bass.ds(2 * s, 2), :], xs[q][:, :, :]).then_inc(xn_done, 1)

        def dve_group(v):
            n = [0]

            def step(instruction):
                n[0] += 1
                instruction.then_inc(group_step, 1)
                v.wait_ge(group_step, n[0])

            te = lambda ap: ap.rearrange("p e t -> p t e")
            v.wait_ge(route_done, after(NS))
            v.wait_ge(tables_made, 1)
            step(v.tensor_reduce(prob[:, :], route[:, :, :], AX.X, ALU.max))
            step(v.tensor_tensor(eq[:, :, :], route[:, :, :], prob[:, :].unsqueeze(2).to_broadcast([P, NT, E]), ALU.is_equal))
            prio_t = prio[:, :].unsqueeze(1).to_broadcast([P, NT, E])
            step(v.tensor_tensor(eq[:, :, :], eq[:, :, :], prio_t, ALU.mult))
            step(v.tensor_reduce(best[:, :], eq[:, :, :], AX.X, ALU.max))
            v.tensor_tensor(onehot[:, :, :], prio_t, best[:, :].unsqueeze(2).to_broadcast([P, NT, E]),
                            ALU.is_equal).then_inc(onehot_done, 1)
            v.wait_ge(prefix_ps, 1)
            step(v.tensor_copy(tot[:, :, :], b[5][:, 0:NT * E].rearrange("p (t e) -> p e t", e=E)))
            flat = lambda ap: ap.rearrange("p e t -> p (e t)")
            step(v.tensor_tensor_scan(flat(cum[:, :, :]), flat(seg[:, :, :]), flat(tot[:, :, :]), 0.0, ALU.mult, ALU.add))
            counts = cum[:, :, NT - 1:NT]
            step(v.tensor_tensor(over[:, :, :], counts.to_broadcast([P, E, NT]),
                                 thresh[:, :].unsqueeze(1).to_broadcast([P, E, NT]), ALU.is_gt))
            step(v.tensor_reduce(need[:, :], over[:, :, :], AX.X, ALU.add))
            step(v.tensor_tensor_scan(ends[:, :], ones[:, 0:E], need[:, :], 0.0, ALU.mult, ALU.add))
            step(v.tensor_tensor(first[:, :], ends[:, :], need[:, :], ALU.subtract))
            step(v.tensor_tensor(place[:, :, :], cum[:, :, :], tot[:, :, :], ALU.subtract))
            step(v.tensor_tensor(place[:, :, :], place[:, :, :], b[4][:, 0:NT * E].rearrange("p (t e) -> p e t", e=E), ALU.add))
            step(v.scalar_tensor_tensor(out=place[:, :, :], in0=first[:, :].unsqueeze(2).to_broadcast([P, E, NT]), scalar=float(P),
                                        in1=place[:, :, :], op0=ALU.mult, op1=ALU.add))
            step(v.tensor_tensor(eq[:, :, :], te(place[:, :, :]), onehot[:, :, :], ALU.mult))
            step(v.tensor_reduce(pos[:, :], eq[:, :, :], AX.X, ALU.add))
            step(v.tensor_copy(pos_i[:, :], pos[:, :]))
            assert n[0] == NPOS, n[0]
            step(v.tensor_tensor(past[:, :, :], tile_no[:, :].unsqueeze(2).to_broadcast([P, MAXT, E]),
                                 ends[:, :].unsqueeze(1).to_broadcast([P, MAXT, E]), ALU.is_ge))
            step(v.tensor_reduce(expert[:, :], past[:, :, :], AX.X, ALU.add))
            v.tensor_copy(small_i[:, 0:1], ends[0:1, E - 1:E])
            v.tensor_scalar(small_i[:, 2:3], ends[0:1, E - 1:E], -1.0, None, ALU.add)
            step(v.tensor_scalar(table[:, :], expert[0:1, :], float(E - 1), None, ALU.min))
            step(v.tensor_scalar(small_i[:, 1:2], ends[0:1, E - 1:E], 16.0, float(START), ALU.mult, ALU.add))
            assert n[0] == NGROUP, n[0]

        def load_count(e):
            e.wait_ge(group_step, NGROUP)
            return e.value_load(small_i[0:1, 0:1], min_val=NT, max_val=NT + E - 1)

        def tiles(e, up, down):
            up(e, 0)
            count = load_count(e)
            with e.Fori(1, count) as s:
                up(e, s, lambda: down(e, s - 1))
            down(e, e.value_load(small_i[0:1, 2:3], min_val=NT - 1, max_val=NT + E - 2))

        def expert_of(e, s):
            return e.value_load(table[0:1, bass.ds(s, 1)], min_val=0, max_val=E - 1)

        def sp_load(sp, s):
            sp.wait_ge(xT_ps, after(s))
            sp.dma_start(xin[:, :], slots_in[bass.ds(s * P, P), :]).then_inc(xin_loaded, 16)

        def sp_store(sp, s):
            sp.wait_ge(y_done, after(s + 1))
            sp.dma_start(slots_out[bass.ds(s * P, P), :], yout[:, :]).then_inc(y_stored, 16)

        def pe_x(pe, s):
            pe.wait_ge(xin_loaded, after(s * 16 + 16))
            pe.wait_ge(xT_done, after(s))
            for k in range(KD):
                last = pe.transpose(b[0][:, k * P:(k + 1) * P], xin[:, k * P:(k + 1) * P], ident[:, :])
            last.then_inc(xT_ps, 1)

        def pe_up(pe, s, between=lambda: None):
            ex = expert_of(pe, s)
            pe.wait_ge(xT_done, after(s + 1))
            for bank, name in ((b[1], "gate"), (b[2], "up")):
                for k in range(KD):
                    last = pe.matmul(bank[:, :], xT[:, k, :], w[name][:, bass.ds(ex, 1), k, :].rearrange("p a f -> p (a f)"),
                                     start=(k == 0), stop=(k == KD - 1))
                last.then_inc(gu_ps, 1)
            pe_x(pe, s + 1)
            between()
            pe.wait_ge(h_done, after(s + 1))
            for k in range(KF):
                last = pe.transpose(b[3][:, k * P:(k + 1) * P], h[:, k * P:(k + 1) * P], ident[:, :])
            last.then_inc(hT_ps, 1)

        def pe_down(pe, s):
            ex = expert_of(pe, s)
            pe.wait_ge(hT_done, after(s + 1))
            pe.wait_ge(y_done, after(s))
            for k in range(KF):
                last = pe.matmul(b[4][:, 0:D], hT[:, k, :], w["down"][:, bass.ds(ex, 1), k, :].rearrange("p a f -> p (a f)"),
                                 start=(k == 0), stop=(k == KF - 1))
            last.then_inc(y_ps, 1)

        def act_x(act, s):
            act.wait_ge(xT_ps, after(s + 1))
            act.activation(xT[:, :, :].rearrange("p k t -> p (k t)"), b[0][:, 0:D], ACT.Copy).then_inc(xT_done, 1)

        def act_up(act, s, between=lambda: None):
            act.wait_ge(gu_ps, after(2 * s + 1))
            act.wait_ge(h_done, after(s))
            act.activation(sg[:, :], b[1][:, :], ACT.Silu).then_inc(sg_done, 1)
            act_x(act, s + 1)
            between()

        def act_down(act, s):
            act.wait_ge(y_ps, after(s + 1))
            act.wait_ge(y_stored, after(s * 16))
            act.activation(yout[:, :], b[4][:, 0:D], ACT.Copy).then_inc(y_done, 1)

        def dve_up(v, s, between=lambda: None):
            v.wait_ge(sg_done, after(s + 1))
            v.wait_ge(gu_ps, after(2 * s + 2))
            v.wait_ge(hT_ps, after(s))
            v.tensor_tensor(h[:, :], sg[:, :], b[2][:, :], ALU.mult).then_inc(h_done, 1)
            v.wait_ge(hT_ps, after(s + 1))
            v.tensor_copy(hT[:, :, :].rearrange("p k t -> p (k t)"), b[3][:, :]).then_inc(hT_done, 1)

        m.start_loop_sems()
        with nc.Block() as block:

            @block.tensor
            def _(pe):
                pe.wait_ge(w["loaded"][0], 16)
                supertiles(pe, pe_front)
                pe.wait_ge(onehot_done, 1)
                hot = onehot[:, :, :].rearrange("p t e -> p (t e)")
                pe.matmul(b[4][:, 0:NT * E], tri_lt[:, :], hot, start=True, stop=True)
                pe.matmul(b[5][:, 0:NT * E], ones[:, :], hot, start=True, stop=True).then_inc(prefix_ps, 1)
                for s in w["loaded"][1:]:
                    pe.wait_ge(s, 16)
                pe.wait_ge(group_step, NGROUP)
                pe_x(pe, 0)
                tiles(pe, pe_up, pe_down)

            @block.scalar
            def _(act):
                supertiles(act, act_front)
                act_x(act, 0)
                tiles(act, act_up, act_down)

            @block.vector
            def _(v):
                supertiles(v, dve_front)
                dve_group(v)
                tiles(v, dve_up, lambda *_: None)
                for k in range(4):
                    v.wait_ge(gathered[k], 16 * 4)
                    for t in range(4 * k, 4 * k + 4):
                        v.scalar_tensor_tensor(out=x[:, t, :], in0=xn[:, t, :], scalar=prob[:, t:t + 1], in1=x[:, t, :],
                                               op0=ALU.mult, op1=ALU.add).then_inc(combined, 1)
                v.wait_ge(combined, NT)

            @block.gpsimd
            def _(g):
                for t in range(E):
                    g.memset(prio[:, t:t + 1], float(E - t))
                for t in range(NT):
                    g.memset(thresh[:, t:t + 1], float(t * P))
                for t in range(MAXT):
                    g.memset(tile_no[:, t:t + 1], float(t))
                g.memset(seg[:, :, 1:NT], 1.0)
                g.memset(seg[:, :, 0:1], 0.0).then_inc(tables_made, 1)
                supertiles(g, pool_front)
                g.wait_ge(group_step, NPOS)
                g.wait_ge(xn_done, after(NS))
                g.wait_ge(slots_zeroed, 16 * 2)
                for t in range(NT):
                    g.indirect_dma_start(slots_in[:, :], bass.IndirectOffsetOnAxis(pos_i[:, t:t + 1], 0), xn[:, t, :],
                                         None).then_inc(scattered, 16)
                g.wait_ge(group_step, NGROUP)
                stores = g.value_load(small_i[0:1, 1:2], min_val=START + 16 * NT, max_val=START + 16 * (NT + E - 1))
                wait_apart(g, waits_passed_g, y_stored, stores)
                for t in range(NT):
                    g.indirect_dma_start(xn[:, t, :], None, slots_out[:, :],
                                         bass.IndirectOffsetOnAxis(pos_i[:, t:t + 1], 0)).then_inc(gathered[t // 4], 16)

            @block.sync
            def _(sp):
                prefetch(sp)
                sp.wait_ge(scattered, 16 * NT)
                count = load_count(sp)
                sp_load(sp, 0)
                sp_load(sp, 1)
                with sp.Fori(0, count) as s:
                    sp_load(sp, s + 2)
                    sp_store(sp, s)
        m.clear()


def griffin_weights(nc, m, a):
    w, loads = {}, []
    for name, rows, cols in (("left_W", D, D), ("right_W", D, D), ("ga_W", D, D), ("gx_W", D, D), ("out_W", D, D),
                             ("up1_W", D, F), ("up2_W", D, F), ("down_W", F, D)):
        w[name] = m.sb("g_" + name, [P, rows // P, cols])
        loads.append((w[name][:, :, :], a[name].rearrange("(k p) f -> p k f", p=P)))
    for name, n in (("norm1_w", KD), ("left_b", KD), ("right_b", KD), ("g_conv_b", KD), ("ga_b", KD), ("gx_b", KD),
                    ("a_param", KD), ("norm2_w", KD), ("up1_b", KU), ("up2_b", KU)):
        w[name] = m.sb("g_" + name, [P, n])
        loads.append((w[name][:, :], a[name].rearrange("(k p) -> p k", p=P)))
    w["g_conv_w"] = m.sb("g_conv_w", [P, TAPS, KD])
    loads.append((w["g_conv_w"][:, :, :], a["g_conv_w"].rearrange("t (k p) -> p t k", p=P)))
    for name in ("out_b", "down_b"):
        w[name] = m.sb("g_" + name, [P, D])
        loads.append((w[name][:, :], a[name].partition_broadcast(P)))
    return w, loads


def griffin_phase(nc, c, w, n_loads, loaded, x):
    ident = c["ident"]
    with ExitStack() as ctx:
        m = Phase(nc, ctx)
        sb, sem, loop_sem = m.sb, m.sem, m.loop_sem
        b = m.banks("gb")
        stats, mv, rstd, veps = (sb("g_" + n, s) for n, s in (
            ("stats", [P, 2, 6]), ("mv", [P, 2, 2]), ("rstd", [P, 2, 1]), ("veps", [P, 2, 1])))
        unit, s1, eps8 = sb("g_unit", [P, 2, 1]), sb("g_s1", [P, 2, 1]), sb("g_eps8", [P, 2])
        xl, xlb = sb("g_xl", [P, 2, D]), [sb(f"g_xlb{q}", [P, 2, D]) for q in range(2)]
        xn, xnT = sb("g_xn", [P, 2, D]), sb("g_xnT", [P, KD, ST])
        left = sb("g_left", [P, KD, ST])
        rpre, xcv = sb("g_rpre", [P, KD, TAPS - 1 + ST]), sb("g_xcv", [P, KD, ST])
        tr, ti, a, tl, a2, qn, root, u, bb, hs = (sb("g_" + n, [P, KD, ST]) for n in "tr ti a tl a2 qn root u bb hs".split())
        carry = sb("g_carry", [P, KD])
        prod = [sb(f"g_prod{q}", [P, KD, ST]) for q in range(2)]
        tap_b, sp4, soft = sb("g_tap_b", [P, KD]), sb("g_sp4", [P, KD]), sb("g_soft", [P, 8, KD])
        x1, x1n, x1nT = sb("g_x1", [P, 2, D]), sb("g_x1n", [P, 2, D]), sb("g_x1nT", [P, KD, ST])
        ms, mse, s2 = sb("g_ms", [P, 2]), sb("g_mse", [P, 2]), sb("g_s2", [P, 2])
        sq = sb("g_sq", [P, 2, D])
        gl = [sb(f"g_gl{j}", [P, ST]) for j in range(2)]
        mT = sb("g_mT", [P, KU, ST])

        names = ("stats_done mv_done norm_step xl_done xn_done xlb_done xdb_done xnT_ps xnT_done lr_ps left_done "
                 "rpre_done tap0_done conv_step halo_done gate_ps gates_done a_done tl_done a2_done q_done root_done "
                 "u_done b_done scan_done carry_done prod_done out_ps x1_done sq_done mse_done s2_done x1n_done "
                 "xadd_done x1nT_ps x1nT_done up_ps gl_done m_done down_ps x_done").split()
        S = {n: loop_sem("g_" + n) for n in names}
        setup, exp_done, eps_made, passed_v, passed_g = (sem("g_" + n) for n in "setup exp_done eps_made passed_v passed_g".split())
        N_SETUP = 24
        xt2 = lambda s: x[:, bass.ds(2 * s, 2), :]
        row2 = lambda ap: ap.unsqueeze(1).to_broadcast([P, 2, D])

        def pe_transposes(pe, bank, src, done):
            for t in range(2):
                for k in range(KD):
                    last = pe.transpose(bank[:, k * ST + t * P:k * ST + (t + 1) * P], src[:, t, k * P:(k + 1) * P], ident[:, :])
            last.then_inc(done, 1)

        def pe_features(pe, bank, weight, rhs):
            for j in range(KD):
                for k in range(KD):
                    last = pe.matmul(bank[:, j * ST:(j + 1) * ST], w[weight][:, k, j * P:(j + 1) * P], rhs[:, k, :],
                                     start=(k == 0), stop=(k == KD - 1))
            return last

        def pe_A1(pe, s, q):
            pe.wait_ge(S["xn_done"], at(s, 2))
            pe_transposes(pe, b[0], xn, S["xnT_ps"])
            pe.wait_ge(S["xnT_done"], after(s + 1))
            pe.wait_ge(S["left_done"], after(2 * s))
            pe_features(pe, b[1], "left_W", xnT).then_inc(S["lr_ps"], 1)
            pe.wait_ge(S["tap0_done"], after(2 * s))
            pe_features(pe, b[2], "right_W", xnT).then_inc(S["lr_ps"], 1)

        def pe_A2(pe, s, q):
            pe.wait_ge(S["conv_step"], at(s, 6))
            pe.wait_ge(S["gates_done"], after(4 * s))
            pe_features(pe, b[3], "ga_W", xcv).then_inc(S["gate_ps"], 1)
            pe_features(pe, b[4], "gx_W", xcv).then_inc(S["gate_ps"], 1)

        def pe_Bo(pe, s, q):
            pe.wait_ge(S["prod_done"], after(s + 1))
            pe.wait_ge(S["x_done"], after(s))
            for t in range(2):
                for k in range(KD):
                    last = pe.matmul(b[5][:, t * D:(t + 1) * D], prod[q][:, k, t * P:(t + 1) * P], w["out_W"][:, k, :],
                                     start=(k == 0), stop=(k == KD - 1))
            last.then_inc(S["out_ps"], 1)

        def pe_Bn(pe, s, q):
            pe.wait_ge(S["x1n_done"], at(s, 2))
            pe_transposes(pe, b[5], x1n, S["x1nT_ps"])
            pe.wait_ge(S["x1nT_done"], after(s + 1))

        def pe_Bu(pe, s, q, f0):
            for f in range(f0, f0 + KU // 2):
                pe.wait_ge(S["m_done"], after(KU * s + f - 1))
                for half, name in enumerate(("up1_W", "up2_W")):
                    for k in range(KD):
                        last = pe.matmul(b[6 + f % 2][:, half * ST:(half + 1) * ST], w[name][:, k, f * P:(f + 1) * P],
                                         x1nT[:, k, :], start=(k == 0), stop=(k == KD - 1))
                last.then_inc(S["up_ps"], 1)

        def pe_Bd(pe, s, q):
            pe.wait_ge(S["m_done"], at(s, KU))
            for t in range(2):
                for k in range(KU):
                    last = pe.matmul(b[5][:, t * D:(t + 1) * D], mT[:, k, t * P:(t + 1) * P], w["down_W"][:, k, :],
                                     start=(k == 0), stop=(k == KU - 1))
            last.then_inc(S["down_ps"], 1)

        def act_A1(act, s, q):
            act.wait_ge(S["xnT_ps"], after(s + 1))
            act.wait_ge(S["lr_ps"], after(2 * s))
            act.activation(xnT[:, :, :].rearrange("p k t -> p (k t)"), b[0][:, :], ACT.Copy).then_inc(S["xnT_done"], 1)
            act.wait_ge(S["lr_ps"], at(s, 2, 1))
            act.wait_ge(S["prod_done"], after(s))
            for j in range(KD):
                act.activation(left[:, j, :], b[1][:, j * ST:(j + 1) * ST], ACT.Gelu, bias=w["left_b"][:, j:j + 1]).then_inc(
                    S["left_done"], 1)
            act.wait_ge(S["lr_ps"], at(s, 2, 2))
            act.wait_ge(S["halo_done"], after(s + 1))
            act.wait_ge(S["gate_ps"], after(2 * s))
            act.wait_ge(S["u_done"], after(s))
            for j in range(KD):
                act.activation(rpre[:, j, TAPS - 1:], b[2][:, j * ST:(j + 1) * ST], ACT.Identity,
                               bias=w["right_b"][:, j:j + 1]).then_inc(S["rpre_done"], 1)
                act.activation(xcv[:, j, :], b[2][:, j * ST:(j + 1) * ST], ACT.Identity,
                               scale=w["g_conv_w"][:, TAPS - 1, j:j + 1], bias=tap_b[:, j:j + 1]).then_inc(S["tap0_done"], 1)

        def act_A2(act, s, q):
            act.wait_ge(S["tl_done"], after(2 * s))
            act.wait_ge(S["u_done"], after(s))
            for n, (dst, bias) in enumerate(((tr, "ga_b"), (ti, "gx_b"))):
                act.wait_ge(S["gate_ps"], at(s, 2, n + 1))
                for j in range(KD):
                    act.activation(dst[:, j, :], b[3 + n][:, j * ST:(j + 1) * ST], ACT.Tanh, scale=0.5,
                                   bias=w[bias][:, j:j + 1]).then_inc(S["gates_done"], 1)

        def act_A3(act, s, q):
            act.wait_ge(S["gates_done"], at(s, 4, 2))
            act.wait_ge(S["scan_done"], after(s))
            act.wait_ge(S["q_done"], after(s))
            for dst, func, done in ((a, ACT.Exp, "a_done"), (tl, ACT.Tanh, "tl_done")):
                for j in range(KD):
                    act.activation(dst[:, j, :], tr[:, j, :], func, scale=sp4[:, j:j + 1], bias=sp4[:, j:j + 1]).then_inc(
                        S[done], 1)
            act.wait_ge(S["q_done"], after(s + 1))
            act.wait_ge(S["b_done"], after(s))
            act.activation(root[:, :, :], qn[:, :, :], ACT.Sqrt, scale=-0.25).then_inc(S["root_done"], 1)

        def act_Bo(act, s, q):
            act.wait_ge(S["x1_done"], after(s + 1))
            act.wait_ge(S["mse_done"], after(s))
            for t in range(2):
                act.activation(sq[:, t, :], x1[:, t, :], ACT.Square, scale=D ** -0.5, accum_out=ms[:, t:t + 1]).then_inc(
                    S["sq_done"], 1)

        def act_Bn(act, s, q):
            act.wait_ge(S["x1nT_ps"], after(s + 1))
            act.wait_ge(S["up_ps"], after(KU * s))
            act.activation(x1nT[:, :, :].rearrange("p k t -> p (k t)"), b[5][:, :], ACT.Copy).then_inc(S["x1nT_done"], 1)

        def act_Bu(act, s, q, f0):
            for f in range(f0, f0 + KU // 2):
                act.wait_ge(S["up_ps"], at(s, KU, f + 1))
                act.wait_ge(S["m_done"], after(KU * s + f - 1))
                act.activation(gl[f % 2][:, :], b[6 + f % 2][:, 0:ST], ACT.Gelu, bias=w["up1_b"][:, f:f + 1]).then_inc(
                    S["gl_done"], 1)

        def dve_setup(v):
            n = [0]

            def step(instruction):
                n[0] += 1
                instruction.then_inc(setup, 1)
                v.wait_ge(setup, n[0])

            v.wait_ge(loaded, 16 * n_loads)
            v.memset(carry[:, :], 0.0).then_inc(S["carry_done"], 1)
            v.memset(rpre[:, :, 0:TAPS - 1], 0.0).then_inc(S["halo_done"], 1)
            vv, nv, e, den, r, z, z2, p = (soft[:, i, :] for i in range(8))
            vv = w["a_param"][:, :]
            step(v.scalar_tensor_tensor(out=nv, in0=vv, scalar=-1.0, in1=vv, op0=ALU.mult, op1=ALU.min))
            v.wait_ge(exp_done, 1)
            step(v.tensor_scalar(den, e, 2.0, None, ALU.add))
            step(v.reciprocal(r, den))
            step(v.tensor_tensor(z, e, r, ALU.mult))
            step(v.tensor_tensor(z2, z, z, ALU.mult))
            step(v.tensor_scalar(p, z2, ATANH[4], ATANH[3], ALU.mult, ALU.add))
            step(v.scalar_tensor_tensor(out=p, in0=p, scalar=0.0, in1=z2, op0=ALU.add, op1=ALU.mult))
            step(v.scalar_tensor_tensor(out=p, in0=p, scalar=ATANH[2], in1=z2, op0=ALU.add, op1=ALU.mult))
            step(v.scalar_tensor_tensor(out=p, in0=p, scalar=ATANH[1], in1=z2, op0=ALU.add, op1=ALU.mult))
            step(v.scalar_tensor_tensor(out=p, in0=p, scalar=ATANH[0], in1=z, op0=ALU.add, op1=ALU.mult))
            step(v.scalar_tensor_tensor(out=p, in0=vv, scalar=0.0, in1=p, op0=ALU.max, op1=ALU.add))
            step(v.tensor_scalar(sp4[:, :], p, -C_RGLRU / 2, None, ALU.mult))
            step(v.tensor_tensor(tap_b[:, :], w["g_conv_w"][:, TAPS - 1, :], w["right_b"][:, :], ALU.mult))
            step(v.tensor_tensor(tap_b[:, :], tap_b[:, :], w["g_conv_b"][:, :], ALU.add))
            for name in ("ga_b", "gx_b"):
                step(v.tensor_scalar(w[name][:, :], w[name][:, :], 0.5, None, ALU.mult))
            for name, norm in (("left_W", "norm1_w"), ("right_W", "norm1_w"), ("up1_W", "norm2_w"), ("up2_W", "norm2_w")):
                for k in range(KD):
                    step(v.tensor_scalar(w[name][:, k, :], w[name][:, k, :], w[norm][:, k:k + 1], None, ALU.mult))
            assert n[0] == N_SETUP, n[0]

        def dve_A0(v, s, q):
            v.wait_ge(S["norm_step"], at(s, 6, 0))
            for t in range(2):
                v.bn_stats(stats[:, t, :], x[:, bass.ds(2 * s + t, 1), :].rearrange("p a d -> p (a d)")).then_inc(
                    S["stats_done"], 1)
            for t in range(2):
                wait_apart(v, passed_v, S["stats_done"], at(s, 2, t + 1))
                v.bn_aggr(mv[:, t, :], stats[:, t, :]).then_inc(S["mv_done"], 1)
            v.wait_ge(S["norm_step"], at(s, 6, 2))
            v.wait_ge(S["xlb_done"], after(s))
            for t in range(2):
                v.tensor_scalar(xl[:, t, :], x[:, bass.ds(2 * s + t, 1), :].rearrange("p a d -> p (a d)"),
                                mv[:, t, 0:1], rstd[:, t, :], ALU.subtract, ALU.mult).then_inc(S["xl_done"], 1)
            v.wait_ge(S["xl_done"], at(s, 2))
            v.wait_ge(S["norm_step"], at(s, 6, 6))
            v.wait_ge(S["xnT_ps"], after(s))
            for t in range(2):
                v.tensor_scalar(xn[:, t, :], xl[:, t, :], s1[:, t, :], None, ALU.mult).then_inc(S["xn_done"], 1)

        def dve_A1(v, s, q):
            for n, tap in enumerate((2, 1, 0)):
                for j in range(KD):
                    if n:
                        v.wait_ge(S["conv_step"], at(s, 6, 2 * n + j - 1))
                    else:
                        v.wait_ge(S["tap0_done"], at(s, 2, j + 1))
                    v.scalar_tensor_tensor(out=xcv[:, j, :], in0=rpre[:, j, tap:tap + ST], scalar=w["g_conv_w"][:, tap, j:j + 1],
                                           in1=xcv[:, j, :], op0=ALU.mult, op1=ALU.add).then_inc(S["conv_step"], 1)
            v.wait_ge(S["conv_step"], at(s, 6))
            v.tensor_copy(rpre[:, :, 0:TAPS - 1], rpre[:, :, ST:ST + TAPS - 1]).then_inc(S["halo_done"], 1)

        def dve_A3(v, s, q):
            v.wait_ge(S["gates_done"], at(s, 4))
            v.wait_ge(S["b_done"], after(s))
            v.scalar_tensor_tensor(out=u[:, :, :], in0=ti[:, :, :], scalar=1.0, in1=xcv[:, :, :], op0=ALU.add,
                                   op1=ALU.mult).then_inc(S["u_done"], 1)
            v.wait_ge(S["a_done"], at(s, 2))
            v.tensor_tensor(a2[:, :, :], a[:, :, :], a[:, :, :], ALU.mult).then_inc(S["a2_done"], 1)
            v.wait_ge(S["a2_done"], after(s + 1))
            v.wait_ge(S["tl_done"], at(s, 2))
            v.wait_ge(S["root_done"], after(s))
            v.scalar_tensor_tensor(out=qn[:, :, :], in0=a2[:, :, :], scalar=1.0, in1=tl[:, :, :], op0=ALU.add,
                                   op1=ALU.mult).then_inc(S["q_done"], 1)
            v.wait_ge(S["root_done"], after(s + 1))
            v.tensor_tensor(bb[:, :, :], u[:, :, :], root[:, :, :], ALU.mult).then_inc(S["b_done"], 1)
            v.wait_ge(S["b_done"], after(s + 1))
            v.wait_ge(S["carry_done"], after(s + 1))
            for j in range(KD):
                last = v.tensor_tensor_scan(hs[:, j, :], a[:, j, :], bb[:, j, :], carry[:, j:j + 1], ALU.mult, ALU.add)
            last.then_inc(S["scan_done"], 1)
            v.wait_ge(S["scan_done"], after(s + 1))
            v.tensor_copy(carry[:, :], hs[:, :, ST - 1]).then_inc(S["carry_done"], 1)
            v.wait_ge(S["left_done"], at(s, 2))
            v.wait_ge(S["out_ps"], after(s - 1))
            v.tensor_tensor(prod[q][:, :, :], left[:, :, :], hs[:, :, :], ALU.mult).then_inc(S["prod_done"], 1)

        def dve_Bo(v, s, q):
            v.wait_ge(S["out_ps"], after(s + 1))
            v.wait_ge(S["xlb_done"], after(s + 1))
            v.wait_ge(S["xadd_done"], after(s))
            v.tensor_tensor(x1[:, :, :].rearrange("p t d -> p (t d)"), b[5][:, :], xlb[q][:, :, :].rearrange("p t d -> p (t d)"),
                            ALU.add).then_inc(S["x1_done"], 1)
            v.wait_ge(S["s2_done"], after(s + 1))
            v.wait_ge(S["x1_done"], after(s + 1))
            v.wait_ge(S["x1nT_ps"], after(s))
            for t in range(2):
                v.tensor_scalar(x1n[:, t, :], x1[:, t, :], s2[:, t:t + 1], None, ALU.mult).then_inc(S["x1n_done"], 1)

        def dve_Bu(v, s, q, f0):
            for f in range(f0, f0 + KU // 2):
                v.wait_ge(S["gl_done"], at(s, KU, f + 1))
                v.wait_ge(S["down_ps"], after(s))
                v.scalar_tensor_tensor(out=mT[:, f, :], in0=b[6 + f % 2][:, ST:2 * ST], scalar=w["up2_b"][:, f:f + 1],
                                       in1=gl[f % 2][:, :], op0=ALU.add, op1=ALU.mult).then_inc(S["m_done"], 1)

        def dve_Bd(v, s, q):
            v.wait_ge(S["down_ps"], after(s + 1))
            v.wait_ge(S["xadd_done"], after(s + 1))
            v.tensor_tensor(xt2(s).rearrange("p t d -> p (t d)"), b[5][:, :], xt2(s).rearrange("p t d -> p (t d)"),
                            ALU.add).then_inc(S["x_done"], 1)

        def pool_A0(g, s, q):
            half_neg = c["half_neg"][:, :].unsqueeze(2)
            g.wait_ge(S["mv_done"], at(s, 2))
            g.wait_ge(S["xn_done"], after(2 * s))
            for n, (out, in0, in1, op) in enumerate((
                    (veps, mv[:, :, 1:2], c["eps"][:, :].unsqueeze(2), ALU.add),
                    (rstd, veps[:, :, :], half_neg, ALU.pow),
                    (unit, rstd[:, :, :], rstd[:, :, :], ALU.mult),
                    (unit, unit[:, :, :], mv[:, :, 1:2], ALU.mult),
                    (unit, unit[:, :, :], eps8[:, :].unsqueeze(2), ALU.add),
                    (s1, unit[:, :, :], half_neg, ALU.pow))):
                if n:
                    g.wait_ge(S["norm_step"], at(s, 6, n))
                g.tensor_tensor(out[:, :, :], in0, in1, op).then_inc(S["norm_step"], 1)
            g.wait_ge(S["xl_done"], at(s, 2))
            g.wait_ge(S["x1_done"], after(s - 1))
            g.tensor_tensor(xlb[q][:, :, :], xl[:, :, :], row2(w["out_b"][:, :]), ALU.add).then_inc(S["xlb_done"], 1)
            wait_apart(g, passed_g, S["xl_done"], at(s, 2))
            g.tensor_tensor(xt2(s), xt2(s), row2(w["down_b"][:, :]), ALU.add).then_inc(S["xdb_done"], 1)

        def pool_Bo(g, s, q):
            g.wait_ge(S["sq_done"], at(s, 2))
            g.tensor_tensor(mse[:, :], ms[:, :], eps8[:, :], ALU.add).then_inc(S["mse_done"], 1)
            g.wait_ge(S["mse_done"], after(s + 1))
            g.wait_ge(S["x1n_done"], after(2 * s))
            g.tensor_tensor(s2[:, :], mse[:, :], c["half_neg"][:, :], ALU.pow).then_inc(S["s2_done"], 1)
            wait_apart(g, passed_g, S["xdb_done"], after(s + 1))
            g.tensor_tensor(xt2(s), xt2(s), x1[:, :, :], ALU.add).then_inc(S["xadd_done"], 1)

        def program(e, A0, A1, A2, A3, Bo, Bn, Bu, Bd):
            def body(s, q, ahead=True):
                n, nq = s + 1, 1 - q
                if ahead:
                    A0(e, n, nq)
                Bo(e, s, q)
                if ahead:
                    A1(e, n, nq)
                Bn(e, s, q)
                Bu(e, s, q, 0)
                if ahead:
                    A2(e, n, nq)
                Bu(e, s, q, KU // 2)
                if ahead:
                    A3(e, n, nq)
                Bd(e, s, q)

            for piece in (A0, A1, A2, A3):
                piece(e, 0, 0)
            with e.Fori(0, NS // 2 - 1) as i:
                body(2 * i, 0)
                body(2 * i + 1, 1)
            body(NS - 2, 0)
            body(NS - 1, 1, ahead=False)

        def no(*_):
            pass

        m.start_loop_sems()
        with nc.Block() as block:

            @block.tensor
            def _(pe):
                pe.wait_ge(setup, N_SETUP)
                program(pe, no, pe_A1, pe_A2, no, pe_Bo, pe_Bn, pe_Bu, pe_Bd)

            @block.scalar
            def _(act):
                act.wait_ge(setup, 1)
                act.activation(soft[:, 2, :], soft[:, 1, :], ACT.Exp).then_inc(exp_done, 1)
                act.wait_ge(setup, N_SETUP)
                program(act, no, act_A1, act_A2, act_A3, act_Bo, act_Bn, act_Bu, no)

            @block.vector
            def _(v):
                dve_setup(v)
                program(v, dve_A0, dve_A1, no, dve_A3, dve_Bo, no, dve_Bu, dve_Bd)

            @block.gpsimd
            def _(g):
                g.memset(eps8[:, :], 1e-8).then_inc(eps_made, 1)
                g.wait_ge(eps_made, 1)
                g.wait_ge(setup, N_SETUP)
                program(g, pool_A0, no, no, no, pool_Bo, no, no, no)
        m.clear()


_PARTS = {"u": "L0_attn_a_u", "W_in": "L0_attn_a_W_in", "conv_w": "L0_attn_a_conv_w", "conv_b": "L0_attn_a_conv_b",
          "dt_bias": "L0_attn_a_dt_bias", "A_log": "L0_attn_a_A_log", "Dp": "L0_attn_a_Dp",
          "norm_w": "L0_attn_a_norm_w", "W_out": "L0_attn_a_W_out",
          "router": "L0_ffn_router_w", "gate": "L0_ffn_gate_w", "up": "L0_ffn_up_w", "down": "L0_ffn_down_w", "g_conv_w": "L0_attn_b_conv_w", "g_conv_b": "L0_attn_b_conv_b"}
_PARTS.update({n: "L0_attn_b_" + n for n in (
    "norm1_w left_W left_b right_W right_b ga_W ga_b gx_W gx_b a_param out_W out_b norm2_w up1_W up1_b up2_W up2_b "
    "down_W down_b").split()})


def build(nc, a, out):
    with ExitStack() as ctx:
        m = Memory(nc, ctx)
        x = m.sb("x", [P, NT, D])
        x_loaded = [m.sem(f"x_loaded{t}") for t in range(4)]
        stored = m.sem("stored")
        zeros, zeros_made, slots_zeroed = m.sb("zeros", [P, D]), m.sem("zeros_made"), m.sem("slots_zeroed")
        c = make_constants(nc, m, zeros, zeros_made)
        w = {"router": m.sb("router", [P, KD, E]), "gate": m.sb("gate", [P, E, KD, FI]), "up": m.sb("up", [P, E, KD, FI]),
             "down": m.sb("down", [P, E, KF, D]), "loaded": [m.sem(f"experts_loaded{k}") for k in range(4)]}
        slots = [nc.dram_tensor(n, (MAXT * P, D), F32).ap() for n in ("slots_in", "slots_out")]

        def load_experts(sp):
            sp.wait_ge(zeros_made, 1)
            for s in slots:
                sp.dma_start(s.rearrange("(t p) d -> p t d", p=P), zeros[:, :].unsqueeze(1).to_broadcast([P, MAXT, D])).then_inc(
                    slots_zeroed, 16)
            sp.dma_start(w["router"][:, :, :], a["router"].rearrange("(k p) e -> p k e", p=P)).then_inc(w["loaded"][0], 16)
            for k, name in enumerate(("gate", "up", "down")):
                sp.dma_start(w[name][:, :, :, :], a[name].rearrange("e (k p) f -> p e k f", p=P)).then_inc(w["loaded"][k + 1], 16)

        mamba_phase(nc, m, a, c, x, x_loaded, load_experts)
        gw, loads = griffin_weights(nc, m, a)
        griffin_loaded = m.sem("griffin_loaded")

        def load_griffin(sp):
            for dst, src in loads:
                sp.dma_start(dst, src, allow_slow_non_contiguous=True).then_inc(griffin_loaded, 16)

        moe_phase(nc, c, w, slots, slots_zeroed, x, "f1_", load_griffin)
        griffin_phase(nc, c, gw, len(loads), griffin_loaded, x)
        moe_phase(nc, c, w, slots, slots_zeroed, x, "f2_", lambda sp: None)
        with nc.Block() as block:

            @block.sync
            def _(sp):
                sp.dma_start(out[0].rearrange("(r p) d -> p r d", p=P), x[:, :, :]).then_inc(stored, 16)
                sp.wait_ge(stored, 16)


def kernel(**inputs):
    import numpy as _np
    import concourse.bacc as _bacc
    from concourse import mybir as _mybir
    from concourse.bass_utils import run_bass_kernel_spmd as _run

    nc = _bacc.Bacc("TRN2", target_bir_lowering=False, num_devices=1)
    arrays, args = {}, {}
    for short, name in _PARTS.items():
        v = _np.ascontiguousarray(inputs[name])
        arrays[f"in_{name}_dram"] = v
        args[short] = nc.dram_tensor(f"in_{name}_dram", v.shape, _mybir.dt.from_np(v.dtype), kind="ExternalInput").ap()
    out = nc.dram_tensor("out_0_dram", (1, TOKENS, D), _mybir.dt.float32, kind="ExternalOutput").ap()
    build(nc, args, out)
    r = _run(nc, [arrays], core_ids=[0])
    return r.results[0]["out_0_dram"]
```

```python
from contextlib import ExitStack

import concourse.bass as bass
from concourse import mybir

F32 = mybir.dt.float32
I32 = mybir.dt.int32
U32 = mybir.dt.uint32
ALU = mybir.AluOpType
ACT = mybir.ActivationFunctionType
AX = mybir.AxisListType

P = 128
TOKENS, D = 2048, 256
KD = D // P
NT = TOKENS // P
NS = NT // 2
ST = 2 * P

DI, DS, NH, DH, TAPS = 512, 128, 8, 64, 4
KI = DI // P
CB = (DI + 2 * DS) // P
XBC0 = DI
DT0 = DI + CB * P
DPROJ = DT0 + NH
ATANH = (2.000000007877749, 0.6666631593507903, 0.40024853723562315, 0.2796141883332212, 0.28174657270344106)

E, FI = 8, 512
KF = FI // P
F, KU = 768, 768 // P
C_RGLRU = 8.0
MAXT = NT + E + 1
ROOM = NT + 1


START = 2


def after(n):
    return START + (max(n, 0) if isinstance(n, int) else n)


def at(s, per, k=None):
    return after(s * per + (per if k is None else k))


def wait_apart(e, passed, sem, value):
    e.wait_ge(sem, value)
    e.sem_inc(passed, 1)


class Memory:

    def __init__(self, nc, ctx):
        self.nc, self.ctx = nc, ctx

    def sb(self, name, shape, dt=F32):
        return self.ctx.enter_context(self.nc.sbuf_tensor(name, shape, dt))

    def banks(self, name):
        return [self.ctx.enter_context(self.nc.psum_tensor(f"{name}{i}", [P, 512], F32)) for i in range(8)]

    def sem(self, name):
        return self.ctx.enter_context(self.nc.semaphore(name))


class Phase(Memory):

    def __init__(self, nc, ctx):
        super().__init__(nc, ctx)
        self.sems, self.loop_sems = [], []

    def sem(self, name):
        self.sems.append(super().sem(name))
        return self.sems[-1]

    def loop_sem(self, name):
        self.loop_sems.append(self.sem(name))
        return self.loop_sems[-1]

    def start_loop_sems(self):
        with self.nc.Block() as block:
            for n, on in enumerate((block.sync, block.scalar, block.vector, block.tensor)):
                def _(e, n=n):
                    for s in self.loop_sems[n::4]:
                        e.sem_inc(s, START)
                on(_)

    def clear(self):
        with self.nc.Block() as block:
            for n, on in enumerate((block.sync, block.scalar, block.vector, block.tensor, block.gpsimd)):
                def _(e, n=n):
                    for s in self.sems[n::5]:
                        e.sem_clear(s)
                on(_)


def make_constants(nc, m, zeros, zeros_made, cum):
    c = {
        "ident": m.sb("ident", [P, P]),
        "tri_le": m.sb("tri_le", [P, P]),
        "tri_gt": m.sb("tri_gt", [P, P]),
        "ones": m.sb("ones", [P, P]),
        "half_neg": m.sb("half_neg", [P, 2]),
        "eps": m.sb("eps", [P, 2]),
        "prio": m.sb("prio", [P, E]),
        "room": m.sb("room", [P, E]),
        "room_less1": m.sb("room_less1", [P, E]),
        "thresh": m.sb("thresh", [P, NT]),
        "tile_no": m.sb("tile_no", [P, MAXT]),
    }
    ready, filled = m.sem("const_ready"), m.sem("const_filled")
    with nc.Block() as block:

        @block.gpsimd
        def _(g):
            g.memset(c["ident"][:, :], 0.0).then_inc(filled, 1)
            for name in ("tri_le", "tri_gt"):
                g.memset(c[name][:, :], 1.0).then_inc(filled, 1)
            g.memset(c["ones"][:, :], 1.0)
            g.memset(c["half_neg"][:, :], -0.5)
            g.memset(c["eps"][:, :], 1e-5)
            g.memset(zeros[:, :], 0.0).then_inc(zeros_made, 1)
            g.memset(cum[:, :], 0.0)
            for n in range(E):
                g.memset(c["prio"][:, n:n + 1], float(E - n))
                g.memset(c["room"][:, n:n + 1], float(n * ROOM * P))
                g.memset(c["room_less1"][:, n:n + 1], float(n * ROOM * P - 1))
            for t in range(NT):
                g.memset(c["thresh"][:, t:t + 1], float(t * P))
            for t in range(MAXT):
                g.memset(c["tile_no"][:, t:t + 1], float(t))
            g.wait_ge(filled, 3)
            for name, op, row, col, fill in (("ident", ALU.not_equal, 1, -1, 1.0), ("tri_le", ALU.is_ge, -1, 1, 0.0),
                                             ("tri_gt", ALU.is_gt, 1, -1, 0.0)):
                g.affine_select(out=c[name][:, :], in_=c[name][:, :], compare_op=op, fill=fill, base=0,
                                pattern=[[col, P]], channel_multiplier=row).then_inc(ready, 1)
            g.wait_ge(ready, 3)
    return c


def router_stage(m, c, w, x, r, slots_in, tag, bank, x_wait, pe_wait_x, pe_wait_logits, pe_wait_rank):
    ident, tri_le, ones = c["ident"], c["tri_le"], c["ones"]
    sb = m.sb
    stats, mv, rstd, veps = (sb(tag + n, s) for n, s in (
        ("stats", [P, 2, 6]), ("mv", [P, 2, 2]), ("rstd", [P, 2, 1]), ("veps", [P, 2, 1])))
    xs, xsT = sb(tag + "xs", [P, 2, D]), sb(tag + "xsT", [P, KD, ST])
    er, sig, eq, hot, place = (sb(tag + n, [P, 2, E]) for n in "er sig eq hot place".split())
    top, best, pos, pos_i = sb(tag + "top", [P, 2]), sb(tag + "best", [P, 2]), sb(tag + "pos", [P, 2]), sb(tag + "pos_i", [P, 2], U32)
    (stats_done, mv_done, veps_done, rstd_done, xs_done, xsT_ps, xsT_done, logit_ps, er_done, step_done, rank_ps,
     cum_done, noted, scatter_seen) = (m.loop_sem(tag + n) for n in (
         "stats_done mv_done veps_done rstd_done xs_done xsT_ps xsT_done logit_ps er_done step_done rank_ps "
         "cum_done noted scatter_seen").split())
    passed_v, passed_g, scattered = m.sem(tag + "passed_v"), m.sem(tag + "passed_g"), r["scattered"][tag]
    NR, HOT, PLACE = 11, 7, 8
    flat = lambda ap: ap.rearrange("p t e -> p (t e)")
    by_tile = lambda ap: ap.unsqueeze(1).to_broadcast([P, 2, E])
    by_expert = lambda ap: ap.unsqueeze(2).to_broadcast([P, 2, E])

    def pe_R1(pe, s):
        pe_wait_x(pe, s)
        pe.wait_ge(xs_done, at(s, 2))
        for t in range(2):
            for k in range(KD):
                last = pe.transpose(bank[:, k * ST + t * P:k * ST + (t + 1) * P], xs[:, t, k * P:(k + 1) * P], ident[:, :])
        last.then_inc(xsT_ps, 1)

    def pe_R2(pe, s):
        pe_wait_logits(pe, s)
        pe.wait_ge(xsT_done, after(s + 1))
        for t in range(2):
            for k in range(KD):
                last = pe.matmul(bank[:, t * E:(t + 1) * E], xsT[:, k, t * P:(t + 1) * P], w["router"][:, k, :],
                                 start=(k == 0), stop=(k == KD - 1))
        last.then_inc(logit_ps, 1)

    def pe_R3(pe, s):
        pe_wait_rank(pe, s)
        pe.wait_ge(step_done, at(s, NR, HOT))
        pe.wait_ge(er_done, after(s + 1))
        pe.wait_ge(cum_done, after(2 * s))
        pe.matmul(bank[:, 0:2 * E], tri_le[:, :], flat(hot[:, :, :]), start=True, stop=False)
        pe.matmul(bank[:, 0:E], ones[:, :], r["cum"][:, :], start=False, stop=False)
        pe.matmul(bank[:, E:2 * E], ones[:, :], r["cum"][:, :], start=False, stop=False)
        pe.matmul(bank[:, E:2 * E], ones[:, :], hot[:, 0, :], start=False, stop=True).then_inc(rank_ps, 1)

    def act_R1(act, s):
        act.wait_ge(xsT_ps, after(s + 1))
        act.wait_ge(logit_ps, after(s))
        act.activation(xsT[:, :, :].rearrange("p k t -> p (k t)"), bank[:, :], ACT.Copy).then_inc(xsT_done, 1)

    def act_R2(act, s):
        act.wait_ge(logit_ps, after(s + 1))
        act.wait_ge(step_done, after(NR * s))
        act.activation(flat(er[:, :, :]), bank[:, 0:2 * E], ACT.Exp, scale=-1.0).then_inc(er_done, 1)

    def dve_R0(v, s):
        x_wait(v, s)
        wait_apart(v, passed_v, rstd_done, after(s))
        for t in range(2):
            v.bn_stats(stats[:, t, :], x[:, bass.ds(2 * s + t, 1), :].rearrange("p a d -> p (a d)")).then_inc(stats_done, 1)
        for t in range(2):
            wait_apart(v, passed_v, stats_done, at(s, 2, t + 1))
            v.bn_aggr(mv[:, t, :], stats[:, t, :]).then_inc(mv_done, 1)

    def dve_R1(v, s):
        v.wait_ge(rstd_done, after(s + 1))
        v.wait_ge(xsT_ps, after(s))
        v.wait_ge(scatter_seen, after(s))
        for t in range(2):
            v.tensor_scalar(xs[:, t, :], x[:, bass.ds(2 * s + t, 1), :].rearrange("p a d -> p (a d)"),
                            mv[:, t, 0:1], rstd[:, t, :], ALU.subtract, ALU.mult).then_inc(xs_done, 1)

    def stepper(v, s, n):
        def step(instruction):
            n[0] += 1
            instruction.then_inc(step_done, 1)
            v.wait_ge(step_done, at(s, NR, n[0]))
        return step

    def dve_R2(v, s):
        n = [0]
        step = stepper(v, s, n)
        v.wait_ge(er_done, after(s + 1))
        step(v.tensor_scalar(flat(er[:, :, :]), flat(er[:, :, :]), 1.0, None, ALU.add))
        step(v.reciprocal(flat(sig[:, :, :]), flat(er[:, :, :])))
        step(v.tensor_reduce(top[:, :], sig[:, :, :], AX.X, ALU.max))
        step(v.tensor_tensor(eq[:, :, :], sig[:, :, :], by_expert(top[:, :]), ALU.is_equal))
        step(v.tensor_tensor(eq[:, :, :], eq[:, :, :], by_tile(c["prio"][:, :]), ALU.mult))
        step(v.tensor_reduce(best[:, :], eq[:, :, :], AX.X, ALU.max))
        v.wait_ge(cum_done, after(2 * s))
        step(v.tensor_tensor(hot[:, :, :], by_tile(c["prio"][:, :]), by_expert(best[:, :]), ALU.is_equal))
        assert n[0] == HOT
        v.tensor_copy(r["prob"][:, bass.ds(2 * s, 2)], top[:, :]).then_inc(noted, 1)
        v.tensor_copy(r["onehot"][:, bass.ds(2 * s, 2), :], hot[:, :, :]).then_inc(noted, 1)

    def dve_R3(v, s):
        n = [HOT]
        step = stepper(v, s, n)
        v.wait_ge(rank_ps, after(s + 1))
        step(v.tensor_tensor(place[:, :, :], bank[:, 0:2 * E].rearrange("p (t e) -> p t e", e=E), by_tile(c["room_less1"][:, :]), ALU.add))
        assert n[0] == PLACE
        step(v.tensor_tensor(place[:, :, :], place[:, :, :], hot[:, :, :], ALU.mult))
        step(v.tensor_reduce(pos[:, :], place[:, :, :], AX.X, ALU.add))
        step(v.tensor_copy(pos_i[:, :], pos[:, :]))
        assert n[0] == NR
        v.tensor_copy(r["pos"][:, bass.ds(2 * s, 2)], pos[:, :]).then_inc(noted, 1)

    def pool_R0(g, s):
        g.wait_ge(mv_done, at(s, 2))
        g.tensor_tensor(veps[:, :, :], mv[:, :, 1:2], c["eps"][:, :].unsqueeze(2), ALU.add).then_inc(veps_done, 1)
        g.wait_ge(veps_done, after(s + 1))
        g.wait_ge(xs_done, after(2 * s))
        g.tensor_tensor(rstd[:, :, :], veps[:, :, :], c["half_neg"][:, :].unsqueeze(2), ALU.pow).then_inc(rstd_done, 1)

    def pool_R3(g, s):
        g.wait_ge(rank_ps, after(s + 1))
        for t in range(2):
            if t:
                g.wait_ge(cum_done, at(s, 2, t))
            g.tensor_tensor(r["cum"][:, :], r["cum"][:, :], hot[:, t, :], ALU.add).then_inc(cum_done, 1)
        wait_apart(g, passed_g, step_done, at(s, NR))
        for t in range(2):
            g.indirect_dma_start(slots_in[:, :], bass.IndirectOffsetOnAxis(pos_i[:, t:t + 1], 0), xs[:, t, :],
                                 None).then_inc(scattered, 16)

    def pool_R4(g, s):
        g.wait_ge(scattered, 32 * s + 32)
        g.sem_inc(scatter_seen, 1)

    return {"pe": (pe_R1, pe_R2, pe_R3), "act": (act_R1, act_R2), "dve": (dve_R0, dve_R1, dve_R2, dve_R3),
            "pool": (pool_R0, pool_R3, pool_R4), "rows_read": xsT_done, "logits_read": er_done, "ranks_read": step_done,
            "ranks_read_after": lambda s: after(NR * s), "noted": noted}


def mamba_phase(nc, a, c, w, x, r, slots_in, x_loaded, load_router, prefetch):
    ident, tri_le, tri_gt, ones = c["ident"], c["tri_le"], c["tri_gt"], c["ones"]
    with ExitStack() as ctx:
        m = Phase(nc, ctx)
        sb, sem = m.sb, m.sem
        b = m.banks("mb")
        winT = sb("winT", [P, KD, DPROJ])
        woutT = sb("woutT", [P, KI, D])
        conv_w, conv_b = sb("conv_w", [P, CB, TAPS]), sb("conv_b", [P, CB])
        norm_w = sb("norm_w", [P, KI])
        dt_bias, neg_a, d_skip = sb("dt_bias", [P, NH]), sb("neg_a", [P, NH]), sb("d_skip", [P, NH])
        stats, mv, rstd = sb("stats", [P, 2, 6]), sb("mv", [P, 2, 2]), sb("rstd", [P, 2, 1])
        veps = sb("veps", [P, 2, 1])
        xn = sb("xn", [P, 2, D])
        xnT = [sb(f"xnT{q}", [P, KD, ST]) for q in range(2)]
        xpre = sb("xpre", [P, CB, TAPS - 1 + ST])
        h, th = sb("h", [P, CB, ST]), sb("th", [P, 2, 2, ST])
        xc_both = sb("xc", [P, 2, CB, ST])
        xc = [xc_both[:, q, :, :] for q in range(2)]
        dtw = sb("dtw", [P, 8, 2 * NH])
        dt = [sb(f"dt{q}", [P, 2 * NH]) for q in range(2)]
        dA = sb("dA", [P, 2 * NH])
        decay = [sb(f"decay{q}", [P, 2, 2 * NH]) for q in range(2)]
        dA_tri = [sb(f"dA_tri{k}", [P, NH, P]) for k in range(2)]
        L, M = sb("L", [P, NH, P]), sb("M", [P, NH, P])
        cbm, bt = sb("cbm", [P, P]), sb("bt", [P, P])
        xt, xdt, xw, xD = (sb(n, [P, DI]) for n in ("xt", "xdt", "xw", "xD"))
        state = sb("state", [P, DI])
        zs, y, yg = (sb(n, [P, DI]) for n in ("zs", "y", "yg"))
        squares = sb("squares", [P, DI], mybir.dt.bfloat16)
        ygT = sb("ygT", [P, KI, P])
        ms, mse, rs = sb("ms", [P, 1]), sb("mse", [P, 1]), sb("rs", [P, 1])
        win_raw = xc_both[:, :, :, :].rearrange("p q b t -> p (q b t)")[:, 0:11 * D].rearrange("p (r d) -> p r d", d=D)
        wout_raw = L[:, :, :].rearrange("p h t -> p (h t)")[:, 0:2 * DI].rearrange("p (r i) -> p r i", i=DI)

        win_loaded = [sem(f"win_loaded{k}") for k in range(3)]
        win_ps, win_done = sem("win_ps"), sem("win_done")
        wout_loaded, wout_ps, wout_done = sem("wout_loaded"), sem("wout_ps"), sem("wout_done")
        par_loaded, par_done, waits_passed = sem("par_loaded"), sem("par_done"), sem("waits_passed")
        (stats_done, mv_done, veps_done, rstd_done, xn_done, xnT_ps, xnT_done, xbc_ps, xpre_done, tap0_done, conv_step,
         halo_done, tanh_done, xc_done, dt_ps, dt_raw_done, dt_exp_done, dt_step, tri_done, small_ps,
         decay_done) = (m.loop_sem("a_" + n) for n in (
             "stats_done mv_done veps_done rstd_done xn_done xnT_ps xnT_done xbc_ps xpre_done tap0_done conv_step "
             "halo_done tanh_done xc_done dt_ps dt_raw_done dt_exp_done dt_step tri_done small_ps decay_done").split())
        (xt_ps, cb_ps, D_ps, xt_done, bt_done, cbm_done, L_done, M_done, xdt_done, xw_done, xD_done, sdec_done,
         yoff_ps, z_ps, tz_done, zs_done, yd_ps, st_ps, S_done, y1_done, y2_done, y3_done, yg_done, sq_done, mse_done,
         rs_done, ygT_ps, ygT_done, out_ps, x_done) = (m.loop_sem("b_" + n) for n in (
             "xt_ps cb_ps D_ps xt_done bt_done cbm_done L_done M_done xdt_done xw_done xD_done sdec_done "
             "yoff_ps z_ps tz_done zs_done yd_ps st_ps S_done y1_done y2_done y3_done yg_done sq_done mse_done "
             "rs_done ygT_ps ygT_done out_ps x_done").split())
        NDT = 13
        R = router_stage(
            m, c, w, x, r, slots_in, "ra_", b[0],
            x_wait=lambda v, s: v.wait_ge(x_done, at(s, 2)),
            pe_wait_x=lambda pe, s: pe.wait_ge(x_done, at(s, 2) if isinstance(s, int) and s == NS - 1 else at(s, 2, 3)),
            pe_wait_logits=lambda pe, s: None,
            pe_wait_rank=lambda pe, s: None)

        def heads(ap, n):
            return ap.unsqueeze(2).to_broadcast([P, NH, n])

        def pe_setup(pe):
            for g, (r0, r1) in enumerate(((0, 4), (4, 8), (8, 11))):
                pe.wait_ge(win_loaded[g], 16 * (1 + (g == 2)))
                for k in range(KD):
                    for r in range(r0, r1):
                        n = min(P, DPROJ - r * P)
                        t = pe.transpose(b[1 + 2 * g + k][:, (r - r0) * P:(r - r0) * P + n],
                                         win_raw[0:n, r, k * P:(k + 1) * P], ident[0:n, 0:n])
                    t.then_inc(win_ps, 1)
            pe.wait_ge(wout_loaded, 16)
            for g, bank in enumerate((b[0], b[7])):
                for i in range(2):
                    for r in range(2):
                        ib = 2 * g + i
                        t = pe.transpose(bank[:, (2 * i + r) * P:(2 * i + r + 1) * P],
                                         wout_raw[:, r, ib * P:(ib + 1) * P], ident[:, :])
                t.then_inc(wout_ps, 1)
            pe.wait_ge(win_done, 6)
            pe.wait_ge(wout_done, 4)

        def pe_A1(pe, s, q):
            pe.wait_ge(x_done, after(2 * s - 2))
            pe.wait_ge(xn_done, at(s, 2))
            for t in range(2):
                for k in range(KD):
                    last = pe.transpose(b[0][:, k * ST + t * P:k * ST + (t + 1) * P], xn[:, t, k * P:(k + 1) * P],
                                        ident[:, :])
            last.then_inc(xnT_ps, 1)

        def pe_xbc(pe, s, q, g):
            if g == 0:
                pe.wait_ge(xnT_done, at(s, 1))
                pe.wait_ge(tap0_done, at(s, 3, 0))
            elif g == 1:
                pe.wait_ge(decay_done, after(s))
            else:
                pe.wait_ge(tap0_done, at(s, 3, 1))
            bank = b[1 + g % 2]
            for j in range(2):
                col = XBC0 + (2 * g + j) * P
                for k in range(KD):
                    last = pe.matmul(bank[:, j * ST:(j + 1) * ST], winT[:, k, col:col + P], xnT[q][:, k, :],
                                     start=(k == 0), stop=(k == KD - 1))
            last.then_inc(xbc_ps, 1)

        def pe_dt(pe, s, q):
            pe.wait_ge(tap0_done, at(s, 3, 2))
            for t in range(2):
                for k in range(KD):
                    last = pe.matmul(b[2][:, t * NH:(t + 1) * NH], xnT[q][:, k, t * P:(t + 1) * P],
                                     winT[:, k, DT0:DPROJ], start=(k == 0), stop=(k == KD - 1))
            last.then_inc(dt_ps, 1)

        def pe_small(pe, s, q):
            pe.wait_ge(dt_step, at(s, NDT))
            pe.matmul(b[2][:, 32:48], tri_le[:, :], dA[:, :], start=True, stop=True)
            pe.matmul(b[2][:, 48:64], ones[:, :], dA[:, :], start=True, stop=True).then_inc(small_ps, 1)

        def pe_xt(pe, s, q, t):
            g = 2 * s + t
            pe.wait_ge(xc_done, at(s, 3, 2))
            pe.wait_ge(zs_done, after(g))
            for k in range(KI):
                last = pe.transpose(b[5][:, k * P:(k + 1) * P], xc[q][:, k, t * P:(t + 1) * P], ident[:, :])
            last.then_inc(xt_ps, 1)

        def pe_D(pe, s, q, t):
            g = 2 * s + t
            pe.wait_ge(tri_done, after(g + 1))
            pe.wait_ge(y2_done, after(g))
            for k in range(2):
                if k:
                    pe.wait_ge(S_done, after(g + 1))
                last = pe.matmul(b[3 + k][:, :], tri_gt[:, :], dA_tri[t][:, 4 * k:4 * k + 4, :].rearrange("p h t -> p (h t)"),
                                 start=True, stop=True)
            last.then_inc(D_ps, 1)

        def pe_yoff(pe, s, q, t):
            g = 2 * s + t
            pe.wait_ge(xc_done, at(s, 3))
            pe.wait_ge(S_done, after(g + 1))
            pe.wait_ge(y1_done, after(g))
            pe.matmul(b[7][:, :], xc[q][:, KI + 1, t * P:(t + 1) * P], state[:, :], start=True,
                      stop=True).then_inc(yoff_ps, 1)

        def pe_cb(pe, s, q, t):
            g = 2 * s + t
            pe.wait_ge(ygT_done, after(g))
            pe.transpose(b[6][:, 0:P], xc[q][:, KI, t * P:(t + 1) * P], ident[:, :])
            pe.matmul(b[6][:, P:2 * P], xc[q][:, KI, t * P:(t + 1) * P], xc[q][:, KI + 1, t * P:(t + 1) * P],
                      start=True, stop=True).then_inc(cb_ps, 1)

        def pe_z(pe, s, q, t):
            g = 2 * s + t
            pe.wait_ge(xt_done, after(g + 1))
            for k in range(KD):
                last = pe.matmul(b[5][:, :], xnT[q][:, k, t * P:(t + 1) * P], winT[:, k, 0:DI],
                                 start=(k == 0), stop=(k == KD - 1))
            last.then_inc(z_ps, 1)

        def pe_sums(pe, s, q, t):
            g = 2 * s + t
            pe.wait_ge(M_done, after(g + 1))
            pe.wait_ge(xdt_done, after(g + 1))
            for hd in range(NH):
                last = pe.matmul(b[3][:, hd * DH:(hd + 1) * DH], M[:, hd, :], xdt[:, hd * DH:(hd + 1) * DH],
                                 start=True, stop=True)
            last.then_inc(yd_ps, 1)
            pe.wait_ge(xw_done, after(g + 1))
            pe.wait_ge(bt_done, after(g + 1))
            pe.matmul(b[4][:, :], bt[:, :], xw[:, :], start=True, stop=True).then_inc(st_ps, 1)

        def pe_ygT(pe, s, t):
            g = 2 * s + t
            pe.wait_ge(yg_done, after(g + 1))
            pe.wait_ge(cbm_done, after(g + 1))
            for k in range(KI):
                last = pe.transpose(b[6][:, k * P:(k + 1) * P], yg[:, k * P:(k + 1) * P], ident[:, :])
            last.then_inc(ygT_ps, 1)

        def pe_out(pe, s, t):
            g = 2 * s + t
            pe.wait_ge(ygT_done, after(g + 1))
            if t == 0:
                if not (isinstance(s, int) and s == NS - 1):
                    pe.wait_ge(xnT_done, after(s + 2))
            else:
                pe.wait_ge(x_done, after(g))
                pe.wait_ge(R["ranks_read"], R["ranks_read_after"](s))
            for k in range(KI):
                last = pe.matmul(b[0][:, t * D:(t + 1) * D], ygT[:, k, :], woutT[:, k, :], start=(k == 0),
                                 stop=(k == KI - 1))
            last.then_inc(out_ps, 1)

        def pe_tile(pe, s, q, t, first=False):
            before = (s, 0) if t else (s - 1, 1)
            pe_xt(pe, s, q, t)
            pe_D(pe, s, q, t)
            if not first:
                pe_ygT(pe, *before)
            pe_yoff(pe, s, q, t)
            pe_cb(pe, s, q, t)
            if not first:
                pe_out(pe, *before)
            pe_z(pe, s, q, t)

        def pe_body(pe, s, q, ahead=True, behind=True):
            n, nq = s + 1, 1 - q
            R1, R2, R3 = R["pe"]
            pe_tile(pe, s, q, 0, first=not behind)
            if ahead:
                pe_A1(pe, n, nq)
                pe_xbc(pe, n, nq, 0)
                pe_xbc(pe, n, nq, 1)
            pe_sums(pe, s, q, 0)
            pe_tile(pe, s, q, 1)
            if ahead:
                pe_dt(pe, n, nq)
            if behind:
                R1(pe, s - 1)
            if ahead:
                pe_xbc(pe, n, nq, 2)
            if behind:
                R2(pe, s - 1)
            pe_sums(pe, s, q, 1)
            if ahead:
                pe_small(pe, n, nq)
            if behind:
                R3(pe, s - 1)

        def pe_end(pe):
            pe_ygT(pe, NS - 1, 1)
            pe_out(pe, NS - 1, 1)
            for piece in R["pe"]:
                piece(pe, NS - 1)

        def act_setup(act):
            act.wait_ge(par_loaded, 16 * 6)
            act.activation(neg_a[:, :], neg_a[:, :], ACT.Exp).then_inc(par_done, 1)
            for i in (0, 2, 4):
                act.wait_ge(win_ps, i + 1)
                act_copy_win(act, i)
            for g in range(2):
                act.wait_ge(wout_ps, g + 1)
                act.wait_ge(par_done, 2)
                for i in range(2):
                    act.activation(woutT[:, 2 * g + i, :], (b[0], b[7])[g][:, i * D:(i + 1) * D], ACT.Copy,
                                   scale=norm_w[:, 2 * g + i:2 * g + i + 1]).then_inc(wout_done, 1)

        def win_group(i):
            g, k = i // 2, i % 2
            n = (4 * P, 4 * P, DPROJ - 8 * P)[g]
            return winT[:, k, g * 4 * P:g * 4 * P + n], b[1 + i][:, 0:n]

        def act_copy_win(act, i):
            act.activation(*win_group(i), ACT.Copy).then_inc(win_done, 1)

        def act_A1(act, s, q):
            act.wait_ge(xnT_ps, at(s, 1))
            act.wait_ge(z_ps, after(2 * s - 2))
            act.activation(xnT[q][:, :, :].rearrange("p k t -> p (k t)"), b[0][:, :], ACT.Copy).then_inc(xnT_done, 1)

        def act_xbc(act, s, q, g):
            act.wait_ge(xbc_ps, at(s, 3, g + 1))
            act.wait_ge(halo_done, at(s, 3, g + 1))
            act.wait_ge(xc_done, at(s, 3, 0))
            bank = b[1 + g % 2][:, :].rearrange("p (j t) -> p j t", j=2)
            act.activation(xpre[:, 2 * g:2 * g + 2, TAPS - 1:], bank, ACT.Copy).then_inc(xpre_done, 1)
            for j in range(2):
                i = act.activation(h[:, 2 * g + j, :], bank[:, j, :], ACT.Identity,
                                   scale=conv_w[:, 2 * g + j, TAPS - 1:TAPS], bias=conv_b[:, 2 * g + j:2 * g + j + 1])
            i.then_inc(tap0_done, 1)

        def act_tanh(act, s, q, g):
            act.wait_ge(conv_step, at(s, 18, 6 * g + 6))
            act.wait_ge(xc_done, at(s, 3, g - 1) if g else after(3 * s))
            act.activation(th[:, g % 2, :, :], h[:, 2 * g:2 * g + 2, :], ACT.Tanh).then_inc(tanh_done, 1)

        def act_dt(act, s, q):
            act.wait_ge(dt_step, at(s, NDT, 2))
            act.activation(dtw[:, 2, :], dtw[:, 1, :], ACT.Exp).then_inc(dt_exp_done, 1)

        def act_decay(act, s, q):
            act.wait_ge(small_ps, at(s, 1))
            act.wait_ge(y1_done, after(2 * s - 2))
            act.wait_ge(sdec_done, after(2 * s - 2))
            act.activation(decay[q][:, :, :].rearrange("p a b -> p (a b)"), b[2][:, 32:64], ACT.Exp).then_inc(
                decay_done, 1)

        def act_xt_L(act, s, q, t):
            g = 2 * s + t
            act.wait_ge(xt_ps, after(g + 1))
            act.wait_ge(xdt_done, after(g))
            act.wait_ge(xD_done, after(g))
            act.activation(xt[:, :], b[5][:, :], ACT.Copy).then_inc(xt_done, 1)
            act.wait_ge(D_ps, after(g + 1))
            act.wait_ge(M_done, after(g))
            act.wait_ge(xw_done, after(g))
            for k in range(2):
                i = act.activation(L[:, 4 * k:4 * k + 4, :].rearrange("p h t -> p (h t)"), b[3 + k][:, :], ACT.Exp)
            i.then_inc(L_done, 1)

        def act_bt(act, s, q, t):
            g = 2 * s + t
            act.wait_ge(cb_ps, after(g + 1))
            act.wait_ge(st_ps, after(g))
            act.activation(bt[:, :], b[6][:, 0:P], ACT.Copy).then_inc(bt_done, 1)

        def act_z(act, s, q, t):
            g = 2 * s + t
            act.wait_ge(z_ps, after(g + 1))
            act.wait_ge(yg_done, after(g))
            act.activation(zs[:, :], b[5][:, :], ACT.Tanh, scale=0.5).then_inc(tz_done, 1)

        def act_sq(act, s, t):
            g = 2 * s + t
            act.wait_ge(yg_done, after(g + 1))
            act.wait_ge(mse_done, after(g))
            act.activation(squares[:, :], yg[:, :], ACT.Square, scale=0.5 * DI ** -0.5, accum_out=ms[:, :]).then_inc(
                sq_done, 1)

        def act_ygT(act, s, t):
            g = 2 * s + t
            act.wait_ge(ygT_ps, after(g + 1))
            act.wait_ge(out_ps, after(g))
            act.activation(ygT[:, :, :].rearrange("p k t -> p (k t)"), b[6][:, :], ACT.Copy).then_inc(ygT_done, 1)

        def act_tile(act, s, q, t, first=False):
            before = (s, 0) if t else (s - 1, 1)
            act_xt_L(act, s, q, t)
            if not first:
                act_ygT(act, *before)
            act_bt(act, s, q, t)
            if not first:
                act_sq(act, *before)

        def act_body(act, s, q, ahead=True, behind=True):
            n, nq = s + 1, 1 - q
            R1, R2 = R["act"]
            act_tile(act, s, q, 0, first=not behind)
            act_z(act, s, q, 0)
            if ahead:
                act_A1(act, n, nq)
                act_xbc(act, n, nq, 0)
                act_xbc(act, n, nq, 1)
            act_tile(act, s, q, 1)
            if ahead:
                act_tanh(act, n, nq, 0)
                act_tanh(act, n, nq, 1)
            act_z(act, s, q, 1)
            if ahead:
                act_dt(act, n, nq)
            if behind:
                R1(act, s - 1)
            if ahead:
                act_xbc(act, n, nq, 2)
            if behind:
                R2(act, s - 1)
            if ahead:
                act_tanh(act, n, nq, 2)
                act_decay(act, n, nq)

        def act_end(act):
            act_ygT(act, NS - 1, 1)
            act_sq(act, NS - 1, 1)
            for piece in R["act"]:
                piece(act, NS - 1)

        def dve_setup(v):
            v.memset(state[:, :], 0.0).then_inc(S_done, 1)
            v.memset(r["prob"][:, NT:NT + 2], 0.0)
            v.memset(r["pos_i"][:, NT:NT + 2], 0)
            v.memset(xpre[:, :, 0:TAPS - 1], 0.0).then_inc(halo_done, 3)
            v.wait_ge(par_loaded, 16 * 6)
            v.tensor_scalar(conv_w[:, :, :], conv_w[:, :, :], 0.5, None, ALU.mult)
            v.tensor_scalar(conv_b[:, :], conv_b[:, :], 0.5, None, ALU.mult)
            v.tensor_scalar(norm_w[:, :], norm_w[:, :], 0.5, None, ALU.mult).then_inc(par_done, 1)
            v.wait_ge(par_done, 2)
            v.tensor_scalar(neg_a[:, :], neg_a[:, :], -1.0, None, ALU.mult).then_inc(par_done, 1)
            for i in (1, 3, 5):
                v.wait_ge(win_ps, i + 1)
                v.tensor_copy(*win_group(i)).then_inc(win_done, 1)
            v.wait_ge(par_done, 3)

        def dve_stats(v, s, q):
            wait_apart(v, waits_passed, rstd_done, after(s))
            for t in range(2):
                v.bn_stats(stats[:, t, :], x[:, bass.ds(2 * s + t, 1), :].rearrange("p a d -> p (a d)")).then_inc(
                    stats_done, 1)
            for t in range(2):
                wait_apart(v, waits_passed, stats_done, at(s, 2, t + 1))
                v.bn_aggr(mv[:, t, :], stats[:, t, :]).then_inc(mv_done, 1)

        def dve_xn(v, s, q):
            v.wait_ge(rstd_done, after(s + 1))
            v.wait_ge(xnT_ps, after(s))
            for t in range(2):
                v.tensor_scalar(xn[:, t, :], x[:, bass.ds(2 * s + t, 1), :].rearrange("p a d -> p (a d)"),
                                mv[:, t, 0:1], rstd[:, t, :], ALU.subtract, ALU.mult).then_inc(xn_done, 1)

        def dve_conv(v, s, q, g):
            v.wait_ge(tap0_done, at(s, 3, g + 1))
            for n, tap in enumerate((2, 1, 0)):
                for j in range(2):
                    if n:
                        v.wait_ge(conv_step, at(s, 18, 6 * g + 2 * n + j - 1))
                    blk = 2 * g + j
                    v.scalar_tensor_tensor(out=h[:, blk, :], in0=xpre[:, blk, tap:tap + ST], scalar=conv_w[:, blk, tap:tap + 1],
                                           in1=h[:, blk, :], op0=ALU.mult, op1=ALU.add).then_inc(conv_step, 1)
            v.wait_ge(conv_step, at(s, 18, 6 * g + 6))
            v.tensor_copy(xpre[:, 2 * g:2 * g + 2, 0:TAPS - 1], xpre[:, 2 * g:2 * g + 2, ST:ST + TAPS - 1]).then_inc(
                halo_done, 1)

        def dve_silu(v, s, q, g):
            v.wait_ge(tanh_done, at(s, 3, g + 1))
            v.wait_ge(yoff_ps, after(2 * s - 2))
            v.scalar_tensor_tensor(out=xc[q][:, 2 * g:2 * g + 2, :], in0=th[:, g % 2, :, :], scalar=1.0,
                                   in1=h[:, 2 * g:2 * g + 2, :], op0=ALU.add, op1=ALU.mult).then_inc(xc_done, 1)

        def dve_dt(v, s, q):
            vv, nv, e, den, r, z, z2, p = (dtw[:, i, :] for i in range(8))
            k = [0]

            def step(instruction):
                k[0] += 1
                instruction.then_inc(dt_step, 1)
                v.wait_ge(dt_step, at(s, NDT, k[0]))

            v.wait_ge(dt_ps, at(s, 1))
            two = lambda ap: ap.unsqueeze(1).to_broadcast([P, 2, NH])
            split = lambda ap: ap.rearrange("p (a b) -> p a b", a=2)
            step(v.tensor_tensor(split(vv), split(b[2][:, 0:2 * NH]), two(dt_bias[:, :]), ALU.add))
            step(v.scalar_tensor_tensor(out=nv, in0=vv, scalar=-1.0, in1=vv, op0=ALU.mult, op1=ALU.min))
            v.wait_ge(dt_exp_done, at(s, 1))
            step(v.tensor_scalar(den, e, 2.0, None, ALU.add))
            step(v.reciprocal(r, den))
            step(v.tensor_tensor(z, e, r, ALU.mult))
            step(v.tensor_tensor(z2, z, z, ALU.mult))
            step(v.tensor_scalar(p, z2, ATANH[4], ATANH[3], ALU.mult, ALU.add))
            step(v.scalar_tensor_tensor(out=p, in0=p, scalar=0.0, in1=z2, op0=ALU.add, op1=ALU.mult))
            step(v.scalar_tensor_tensor(out=p, in0=p, scalar=ATANH[2], in1=z2, op0=ALU.add, op1=ALU.mult))
            step(v.scalar_tensor_tensor(out=p, in0=p, scalar=ATANH[1], in1=z2, op0=ALU.add, op1=ALU.mult))
            step(v.scalar_tensor_tensor(out=p, in0=p, scalar=ATANH[0], in1=z, op0=ALU.add, op1=ALU.mult))
            v.wait_ge(xdt_done, after(2 * s - 2))
            step(v.scalar_tensor_tensor(out=dt[q][:, :], in0=vv, scalar=0.0, in1=p, op0=ALU.max, op1=ALU.add))
            v.wait_ge(small_ps, after(s))
            v.wait_ge(tri_done, after(2 * s))
            step(v.tensor_tensor(split(dA[:, :]), split(dt[q][:, :]), two(neg_a[:, :]), ALU.mult))

        def dve_cbm(v, s, q, t):
            g = 2 * s + t
            v.wait_ge(bt_done, after(g + 1))
            v.tensor_tensor(cbm[:, :], b[6][:, P:2 * P], tri_le[:, :], ALU.mult).then_inc(cbm_done, 1)

        def dve_M(v, s, q, t):
            g = 2 * s + t
            v.wait_ge(L_done, after(g + 1))
            v.wait_ge(cbm_done, after(g + 1))
            v.wait_ge(yd_ps, after(g))
            v.tensor_tensor(M[:, :, :], L[:, :, :], cbm[:, :].unsqueeze(1).to_broadcast([P, NH, P]),
                            ALU.mult).then_inc(M_done, 1)

        def dve_z(v, s, q, t):
            g = 2 * s + t
            v.wait_ge(tz_done, after(g + 1))
            v.scalar_tensor_tensor(out=zs[:, :], in0=zs[:, :], scalar=1.0, in1=b[5][:, :], op0=ALU.add,
                                   op1=ALU.mult).then_inc(zs_done, 1)

        def dve_y1(v, s, q, t):
            g = 2 * s + t
            byhead = lambda ap: ap.rearrange("p (h d) -> p h d", h=NH)
            v.wait_ge(yoff_ps, after(g + 1))
            v.wait_ge(decay_done, after(s + 1))
            v.tensor_tensor(byhead(y[:, :]), byhead(b[7][:, :]), heads(decay[q][:, 0, t * NH:(t + 1) * NH], DH),
                            ALU.mult).then_inc(y1_done, 1)

        def dve_y(v, s, t):
            g = 2 * s + t
            v.wait_ge(yd_ps, after(g + 1))
            v.wait_ge(y3_done, after(g + 1))
            v.tensor_tensor(y[:, :], y[:, :], b[3][:, :], ALU.add).then_inc(y2_done, 1)
            v.wait_ge(st_ps, after(g + 1))
            v.wait_ge(sdec_done, after(g + 1))
            v.tensor_tensor(state[:, :], state[:, :], b[4][:, :], ALU.add).then_inc(S_done, 1)
            v.wait_ge(y2_done, after(g + 1))
            v.wait_ge(zs_done, after(g + 1))
            v.wait_ge(sq_done, after(g))
            v.wait_ge(ygT_ps, after(g))
            v.tensor_tensor(yg[:, :], y[:, :], zs[:, :], ALU.mult).then_inc(yg_done, 1)

        def dve_x(v, s, t):
            g = 2 * s + t
            v.wait_ge(out_ps, after(g + 1))
            v.wait_ge(rs_done, after(g + 1))
            xs = x[:, bass.ds(g, 1), :].rearrange("p a d -> p (a d)")
            v.scalar_tensor_tensor(out=xs, in0=b[0][:, t * D:(t + 1) * D], scalar=rs[:, :], in1=xs, op0=ALU.mult,
                                   op1=ALU.add).then_inc(x_done, 1)

        def dve_body(v, s, q, ahead=True, behind=True):
            n, nq = s + 1, 1 - q
            R0, R1, R2, R3 = R["dve"]
            if ahead:
                dve_stats(v, n, nq)
            dve_cbm(v, s, q, 0)
            dve_M(v, s, q, 0)
            if ahead:
                dve_xn(v, n, nq)
            dve_y1(v, s, q, 0)
            if behind:
                dve_x(v, s - 1, 1)
            dve_z(v, s, q, 0)
            if behind:
                R0(v, s - 1)
            if ahead:
                dve_conv(v, n, nq, 0)
            dve_y(v, s, 0)
            if ahead:
                dve_conv(v, n, nq, 1)
            dve_cbm(v, s, q, 1)
            dve_M(v, s, q, 1)
            dve_y1(v, s, q, 1)
            dve_x(v, s, 0)
            if behind:
                R1(v, s - 1)
            dve_z(v, s, q, 1)
            if ahead:
                dve_dt(v, n, nq)
                dve_silu(v, n, nq, 0)
                dve_silu(v, n, nq, 1)
                dve_conv(v, n, nq, 2)
            if behind:
                R2(v, s - 1)
            dve_y(v, s, 1)
            if ahead:
                dve_silu(v, n, nq, 2)
            if behind:
                R3(v, s - 1)

        def dve_end(v):
            dve_x(v, NS - 1, 1)
            for piece in R["dve"]:
                piece(v, NS - 1)

        def pool_A1(g_, s, q):
            g_.wait_ge(mv_done, at(s, 2))
            g_.tensor_tensor(veps[:, :, :], mv[:, :, 1:2], c["eps"][:, :].unsqueeze(2), ALU.add).then_inc(veps_done, 1)
            g_.wait_ge(veps_done, after(s + 1))
            g_.wait_ge(xn_done, after(2 * s))
            g_.tensor_tensor(rstd[:, :, :], veps[:, :, :], c["half_neg"][:, :].unsqueeze(2), ALU.pow).then_inc(
                rstd_done, 1)

        def pool_tri(g_, s, q):
            g_.wait_ge(dt_step, at(s, NDT))
            for t in range(2):
                g_.wait_ge(D_ps, after(2 * s - 1 + t))
                g_.tensor_tensor(dA_tri[t][:, :, :], tri_le[:, :].unsqueeze(1).to_broadcast([P, NH, P]),
                                 heads(dA[:, t * NH:(t + 1) * NH], P), ALU.mult).then_inc(tri_done, 1)

        def pool_tile(g_, s, q, t):
            g = 2 * s + t
            byhead = lambda ap: ap.rearrange("p (h d) -> p h d", h=NH)
            g_.wait_ge(L_done, after(g + 1))
            g_.wait_ge(xdt_done, after(g + 1))
            g_.wait_ge(st_ps, after(g))
            g_.tensor_tensor(byhead(xw[:, :]), byhead(xdt[:, :]), L[:, :, P - 1:P].to_broadcast([P, NH, DH]),
                             ALU.mult).then_inc(xw_done, 1)
            g_.wait_ge(S_done, after(g + 1))
            g_.wait_ge(yoff_ps, after(g + 1))
            g_.wait_ge(decay_done, after(s + 1))
            g_.tensor_tensor(byhead(state[:, :]), byhead(state[:, :]), heads(decay[q][:, 1, t * NH:(t + 1) * NH], DH),
                             ALU.mult).then_inc(sdec_done, 1)
            g_.tensor_tensor(byhead(xD[:, :]), byhead(xt[:, :]), heads(d_skip[:, :], DH), ALU.mult).then_inc(
                xD_done, 1)
            g_.wait_ge(xD_done, after(g + 1))
            g_.wait_ge(y1_done, after(g + 1))
            g_.tensor_tensor(y[:, :], y[:, :], xD[:, :], ALU.add).then_inc(y3_done, 1)

        def pool_xdt(g_, s, q, t):
            g = 2 * s + t
            byhead = lambda ap: ap.rearrange("p (h d) -> p h d", h=NH)
            g_.wait_ge(xt_done, after(g + 1))
            g_.wait_ge(dt_step, at(s, NDT))
            g_.wait_ge(yd_ps, after(g))
            g_.tensor_tensor(byhead(xdt[:, :]), byhead(xt[:, :]), heads(dt[q][:, t * NH:(t + 1) * NH], DH),
                             ALU.mult).then_inc(xdt_done, 1)

        def pool_rs(g_, s, t):
            g = 2 * s + t
            g_.wait_ge(sq_done, after(g + 1))
            g_.tensor_tensor(mse[:, :], ms[:, :], c["eps"][:, 0:1], ALU.add).then_inc(mse_done, 1)
            g_.wait_ge(mse_done, after(g + 1))
            g_.wait_ge(x_done, after(g))
            g_.tensor_tensor(rs[:, :], mse[:, :], c["half_neg"][:, 0:1], ALU.pow).then_inc(rs_done, 1)

        def pool_body(g_, s, q, ahead=True, behind=True):
            n, nq = s + 1, 1 - q
            R0, R3, R4 = R["pool"]
            pool_xdt(g_, s, q, 0)
            if ahead:
                pool_A1(g_, n, nq)
            if behind:
                pool_rs(g_, s - 1, 1)
            pool_tile(g_, s, q, 0)
            if behind:
                R0(g_, s - 1)
            pool_xdt(g_, s, q, 1)
            pool_rs(g_, s, 0)
            pool_tile(g_, s, q, 1)
            if ahead:
                pool_tri(g_, n, nq)
            if behind:
                R3(g_, s - 1)
                R4(g_, s - 1)

        def pool_end(g_):
            pool_rs(g_, NS - 1, 1)
            for piece in R["pool"][:2]:
                piece(g_, NS - 1)

        def program(e, stage_a, body, end, before_loop=lambda: None):
            for piece in stage_a:
                piece(e, 0, 0)
            before_loop()
            body(e, 0, 0, behind=False)
            with e.Fori(0, NS // 2 - 1) as i:
                body(e, 2 * i + 1, 1)
                body(e, 2 * i + 2, 0)
            body(e, NS - 1, 1, ahead=False)
            end(e)

        def group(fn, g):
            return lambda e, s, q: fn(e, s, q, g)

        m.start_loop_sems()
        with nc.Block() as block:

            @block.sync
            def _(sp):
                for g, (r0, r1) in ((1, (4, 8)), (2, (8, 10)), (0, (0, 4))):
                    sp.dma_start(win_raw[:, r0:r1, :],
                                 a["W_in"][r0 * P:r1 * P, :].rearrange("(r p) d -> p r d", p=P)).then_inc(win_loaded[g], 16)
                sp.dma_start(win_raw[0:NH, 10, :], a["W_in"][DT0:DPROJ, :]).then_inc(win_loaded[2], 16)
                sp.dma_start(wout_raw, a["W_out"].rearrange("(r p) i -> p r i", p=P)).then_inc(wout_loaded, 16)
                load_router(sp)
                for k in range(3):
                    sp.wait_ge(win_loaded[k], 16 * (1 + (k == 2)))
                sp.wait_ge(wout_loaded, 16)
                for t in range(4):
                    sp.wait_ge(x_loaded[t], 16)
                sp.wait_ge(par_loaded, 16 * 6)
                prefetch(sp)

            @block.tensor
            def _(pe):
                pe_setup(pe)
                pe.wait_ge(w["loaded"][0], 16)
                program(pe, (pe_A1, group(pe_xbc, 0), group(pe_xbc, 1), group(pe_xbc, 2), pe_dt, pe_small), pe_body, pe_end)

            @block.scalar
            def _(act):
                act.dma_start(conv_w[:, :, :], a["conv_w"].rearrange("(r p) w -> p r w", p=P)).then_inc(par_loaded, 16)
                for dst, src in ((conv_b, "conv_b"), (norm_w, "norm_w")):
                    act.dma_start(dst[:, :], a[src].rearrange("(r p) -> p r", p=P), allow_slow_non_contiguous=True).then_inc(par_loaded, 16)
                for dst, src in ((dt_bias, "dt_bias"), (neg_a, "A_log"), (d_skip, "Dp")):
                    act.dma_start(dst[:, :], a[src].partition_broadcast(P)).then_inc(par_loaded, 16)
                for t in range(4):
                    act.dma_start(x[:, 4 * t:4 * t + 4, :], a["u"][0, 4 * t * P:(4 * t + 4) * P, :].rearrange(
                        "(r p) d -> p r d", p=P)).then_inc(x_loaded[t], 16)
                act_setup(act)
                act.wait_ge(par_done, 3)
                program(act, (act_A1, group(act_xbc, 0), group(act_xbc, 1), group(act_tanh, 0), group(act_tanh, 1),
                              group(act_xbc, 2), group(act_tanh, 2), act_dt, act_decay), act_body, act_end)

            @block.vector
            def _(v):
                dve_setup(v)
                v.wait_ge(x_loaded[0], 16)

                def rest_of_x():
                    for t in range(1, 4):
                        v.wait_ge(x_loaded[t], 16)
                program(v, (dve_stats, dve_xn, group(dve_conv, 0), group(dve_conv, 1), group(dve_silu, 0), group(dve_silu, 1),
                            group(dve_conv, 2), group(dve_silu, 2), dve_dt), dve_body, dve_end, rest_of_x)
                v.wait_ge(R["noted"], after(3 * NS))

            @block.gpsimd
            def _(g_):
                g_.wait_ge(par_loaded, 16 * 6)
                program(g_, (pool_A1, pool_tri), pool_body, pool_end)
        m.clear()


def moe_phase(nc, c, w, slots, slots_zeroed, x, r, rows_from, tag, prefetch, prepare):
    ident, ones, zeros = c["ident"], c["ones"], c["zeros"]
    slots_in, slots_out = slots
    with ExitStack() as ctx:
        m = Phase(nc, ctx)
        sb, sem, loop_sem = m.sb, m.sem, m.loop_sem
        b = m.banks(tag + "b")
        over, delta3 = sb(tag + "over", [P, E, NT]), sb(tag + "delta3", [P, NT, E])
        counts, need, spare, ends, first, delta = (sb(tag + n, [P, E]) for n in "counts need spare ends first delta".split())
        last, tile, past = sb(tag + "last", [P, 1]), sb(tag + "tile", [P, MAXT]), sb(tag + "past", [P, MAXT, E])
        expert, skip = sb(tag + "expert", [P, MAXT]), sb(tag + "skip", [P, MAXT])
        pos = sb(tag + "pos", [P, NT])
        table, rows = sb(tag + "table", [1, MAXT], I32), sb(tag + "rows", [1, MAXT], I32)
        tails = sb(tag + "tails", [1, E], I32)
        small_i = sb(tag + "small_i", [1, 3], I32)
        xin, xT = sb(tag + "xin", [P, D]), sb(tag + "xT", [P, KD, P])
        sg, h, yout = (sb(tag + n, [P, s]) for n, s in (("sg", FI), ("h", FI), ("y", D)))
        hT = sb(tag + "hT", [P, KF, P])

        counts_ps, group_step, loose_step, tails_zeroed, waits_passed, waits_passed_a = (sem(tag + n) for n in "counts_ps group_step loose_step tails_zeroed waits_passed waits_passed_a".split())
        xin_loaded, y_stored = loop_sem(tag + "xin_loaded"), loop_sem(tag + "y_stored")
        xT_ps, xT_done, gu_ps, sg_done, h_done, hT_ps, hT_done, y_ps, y_done = (
            loop_sem(tag + n) for n in "xT_ps xT_done gu_ps sg_done h_done hT_ps hT_done y_ps y_done".split())
        NTAILS, NGROUP = 2, 14

        def dve_group(v):
            n = [0]

            def step(instruction):
                n[0] += 1
                instruction.then_inc(group_step, 1)
                v.wait_ge(group_step, n[0])

            wide = lambda ap, k: ap.unsqueeze(2).to_broadcast([P, E, k])
            rep = lambda ap, k: ap.unsqueeze(1).to_broadcast([P, k, E])
            v.wait_ge(counts_ps, 1)
            step(v.tensor_copy(counts[:, :], b[7][:, 0:E]))
            step(v.tensor_tensor(tails[:, :], counts[0:1, :], c["room"][0:1, :], ALU.add))
            assert n[0] == NTAILS
            step(v.tensor_tensor(over[:, :, :], wide(counts[:, :], NT), c["thresh"][:, :].unsqueeze(1).to_broadcast([P, E, NT]), ALU.is_gt))
            step(v.tensor_reduce(need[:, :], over[:, :, :], AX.X, ALU.add))
            step(v.tensor_tensor_scan(ends[:, :], ones[:, 0:E], need[:, :], 0.0, ALU.mult, ALU.add))
            step(v.tensor_scalar(spare[:, :], need[:, :], -1.0, float(ROOM), ALU.mult, ALU.add))
            step(v.tensor_scalar(last[:, :], ends[:, E - 1:E], -1.0, None, ALU.add))
            step(v.tensor_scalar(tile[:, :], c["tile_no"][:, :], last[:, 0:1], None, ALU.min))
            step(v.tensor_tensor(past[:, :, :], tile[:, :].unsqueeze(2).to_broadcast([P, MAXT, E]), rep(ends[:, :], MAXT), ALU.is_ge))
            step(v.tensor_reduce(expert[:, :], past[:, :, :], AX.X, ALU.add))
            step(v.tensor_tensor(past[:, :, :], past[:, :, :], rep(spare[:, :], MAXT), ALU.mult))
            step(v.tensor_reduce(skip[:, :], past[:, :, :], AX.X, ALU.add))
            v.tensor_copy(table[:, :], expert[0:1, :])
            v.tensor_copy(small_i[:, 0:1], ends[0:1, E - 1:E])
            v.tensor_copy(small_i[:, 2:3], last[0:1, :])
            step(v.tensor_tensor(rows[:, :], skip[0:1, :], tile[0:1, :], ALU.add))
            step(v.tensor_scalar(small_i[:, 1:2], ends[0:1, E - 1:E], 16.0, float(START), ALU.mult, ALU.add))
            assert n[0] == NGROUP, n[0]

        def dve_rows_out(v):
            n = [0]

            def step(instruction):
                n[0] += 1
                instruction.then_inc(loose_step, 1)
                v.wait_ge(loose_step, n[0])

            step(v.tensor_tensor(first[:, :], ends[:, :], need[:, :], ALU.subtract))
            step(v.scalar_tensor_tensor(out=delta[:, :], in0=first[:, :], scalar=float(P), in1=c["room"][:, :],
                                        op0=ALU.mult, op1=ALU.subtract))
            step(v.tensor_tensor(delta3[:, :, :], r["onehot"][:, :, :], delta[:, :].unsqueeze(1).to_broadcast([P, NT, E]), ALU.mult))
            step(v.tensor_reduce(pos[:, :], delta3[:, :, :], AX.X, ALU.add))
            step(v.tensor_tensor(pos[:, :], pos[:, :], r["pos"][:, 0:NT], ALU.add))
            step(v.tensor_copy(r["pos_i"][:, 0:NT], pos[:, :]))

        def fill_tails(q, first):
            q.wait_ge(group_step, NTAILS)
            for e in range(first, E, 2):
                tail = q.value_load(tails[0:1, e:e + 1], min_val=e * ROOM * P, max_val=e * ROOM * P + TOKENS)
                q.dma_start(slots_in[bass.ds(tail, P), :], zeros[:, :]).then_inc(tails_zeroed, 16)

        def load_count(e):
            e.wait_ge(group_step, NGROUP)
            return e.value_load(small_i[0:1, 0:1], min_val=NT, max_val=NT + E - 1)

        def tiles(e, up, down):
            up(e, 0)
            count = load_count(e)
            with e.Fori(1, count) as s:
                up(e, s, lambda: down(e, s - 1))
            down(e, e.value_load(small_i[0:1, 2:3], min_val=NT - 1, max_val=NT + E - 2))

        def expert_of(e, s):
            return e.value_load(table[0:1, bass.ds(s, 1)], min_val=0, max_val=E - 1)

        def sp_load(sp, s):
            sp.wait_ge(xT_ps, after(s))
            row = sp.value_load(rows[0:1, bass.ds(s, 1)], min_val=0, max_val=E * ROOM - 1)
            sp.dma_start(xin[:, :], slots_in[bass.ds(row * P, P), :]).then_inc(xin_loaded, 16)

        def pe_x(pe, s):
            pe.wait_ge(xin_loaded, after(s * 16 + 16))
            pe.wait_ge(xT_done, after(s))
            for k in range(KD):
                last = pe.transpose(b[0][:, k * P:(k + 1) * P], xin[:, k * P:(k + 1) * P], ident[:, :])
            last.then_inc(xT_ps, 1)

        def pe_up(pe, s, between=lambda: None):
            ex = expert_of(pe, s)
            pe.wait_ge(xT_done, after(s + 1))
            for bank, name in ((b[1], "gate"), (b[2], "up")):
                for k in range(KD):
                    last = pe.matmul(bank[:, :], xT[:, k, :], w[name][:, bass.ds(ex, 1), k, :].rearrange("p a f -> p (a f)"),
                                     start=(k == 0), stop=(k == KD - 1))
                last.then_inc(gu_ps, 1)
            pe_x(pe, s + 1)
            between()
            pe.wait_ge(h_done, after(s + 1))
            for k in range(KF):
                last = pe.transpose(b[3][:, k * P:(k + 1) * P], h[:, k * P:(k + 1) * P], ident[:, :])
            last.then_inc(hT_ps, 1)

        def pe_down(pe, s):
            ex = expert_of(pe, s)
            pe.wait_ge(hT_done, after(s + 1))
            pe.wait_ge(y_done, after(s))
            for k in range(KF):
                last = pe.matmul(b[4][:, 0:D], hT[:, k, :], w["down"][:, bass.ds(ex, 1), k, :].rearrange("p a f -> p (a f)"),
                                 start=(k == 0), stop=(k == KF - 1))
            last.then_inc(y_ps, 1)

        def act_x(act, s):
            act.wait_ge(xT_ps, after(s + 1))
            act.activation(xT[:, :, :].rearrange("p k t -> p (k t)"), b[0][:, 0:D], ACT.Copy).then_inc(xT_done, 1)

        def act_up(act, s, between=lambda: None):
            act.wait_ge(gu_ps, after(2 * s + 1))
            act.wait_ge(h_done, after(s))
            act.activation(sg[:, :], b[1][:, :], ACT.Silu).then_inc(sg_done, 1)
            act_x(act, s + 1)
            between()

        def act_down(act, s):
            act.wait_ge(y_ps, after(s + 1))
            act.wait_ge(y_stored, after(s * 16))
            act.activation(yout[:, :], b[4][:, 0:D], ACT.Copy).then_inc(y_done, 1)
            wait_apart(act, waits_passed_a, y_done, after(s + 1))
            act.dma_start(slots_out[bass.ds(s * P, P), :], yout[:, :]).then_inc(y_stored, 16)

        def dve_up(v, s, between=lambda: None):
            v.wait_ge(sg_done, after(s + 1))
            v.wait_ge(gu_ps, after(2 * s + 2))
            v.wait_ge(hT_ps, after(s))
            v.tensor_tensor(h[:, :], sg[:, :], b[2][:, :], ALU.mult).then_inc(h_done, 1)
            v.wait_ge(hT_ps, after(s + 1))
            v.tensor_copy(hT[:, :, :].rearrange("p k t -> p (k t)"), b[3][:, :]).then_inc(hT_done, 1)

        m.start_loop_sems()
        with nc.Block() as block:

            @block.tensor
            def _(pe):
                pe.matmul(b[7][:, 0:E], ones[:, :], r["cum"][:, :], start=True, stop=True).then_inc(counts_ps, 1)
                for s in w["loaded"][1:]:
                    pe.wait_ge(s, 16)
                pe.wait_ge(group_step, NGROUP)
                pe_x(pe, 0)
                tiles(pe, pe_up, pe_down)

            @block.scalar
            def _(act):
                act.activation(sg[:, 0:1], c["eps"][:, 0:1], ACT.Silu)
                fill_tails(act, 1)
                act.wait_ge(slots_zeroed, 16)
                act_x(act, 0)
                tiles(act, act_up, act_down)

            @block.vector
            def _(v):
                dve_group(v)
                dve_rows_out(v)
                tiles(v, dve_up, lambda *_: None)

            @block.gpsimd
            def _(g):
                g.wait_ge(counts_ps, 1)
                g.memset(r["cum"][:, :], 0.0)
                prepare(g)

            @block.sync
            def _(sp):
                fill_tails(sp, 0)
                count = load_count(sp)
                sp.wait_ge(r["scattered"][rows_from], 32 * NS)
                sp.wait_ge(tails_zeroed, 16 * E)
                sp_load(sp, 0)
                sp_load(sp, 1)
                prefetch(sp)
                with sp.Fori(0, count) as s:
                    sp_load(sp, s + 2)
                stores = sp.value_load(small_i[0:1, 1:2], min_val=START + 16 * NT, max_val=START + 16 * (NT + E - 1))
                wait_apart(sp, waits_passed, y_stored, stores)
                wait_apart(sp, waits_passed, xin_loaded, stores + 32)
        m.clear()


def griffin_weights(nc, m, a):
    w, loads = {}, []
    for name, rows, cols in (("left_W", D, D), ("right_W", D, D), ("ga_W", D, D), ("gx_W", D, D), ("out_W", D, D),
                             ("up1_W", D, F), ("up2_W", D, F), ("down_W", F, D)):
        w[name] = m.sb("g_" + name, [P, rows // P, cols])
        loads.append((w[name][:, :, :], a[name].rearrange("(k p) f -> p k f", p=P)))
    for name, n in (("norm1_w", KD), ("left_b", KD), ("right_b", KD), ("g_conv_b", KD), ("ga_b", KD), ("gx_b", KD),
                    ("a_param", KD), ("norm2_w", KD), ("up1_b", KU), ("up2_b", KU)):
        w[name] = m.sb("g_" + name, [P, n])
        loads.append((w[name][:, :], a[name].rearrange("(k p) -> p k", p=P)))
    w["g_conv_w"] = m.sb("g_conv_w", [P, TAPS, KD])
    loads.append((w["g_conv_w"][:, :, :], a["g_conv_w"].rearrange("t (k p) -> p t k", p=P)))
    for name in ("out_b", "down_b"):
        w[name] = m.sb("g_" + name, [P, D])
        loads.append((w[name][:, :], a[name].partition_broadcast(P)))
    w["tap_b"] = m.sb("g_tap_b", [P, KD])
    return w, loads


def prepare_griffin_weights(g, w, n_loads, loaded, prepared):
    g.wait_ge(loaded, 16 * n_loads)
    g.tensor_tensor(w["tap_b"][:, :], w["g_conv_w"][:, TAPS - 1, :], w["right_b"][:, :], ALU.mult).then_inc(prepared, 1)
    g.wait_ge(prepared, 1)
    g.tensor_tensor(w["tap_b"][:, :], w["tap_b"][:, :], w["g_conv_b"][:, :], ALU.add).then_inc(prepared, 1)
    for name in ("ga_b", "gx_b"):
        g.tensor_scalar(w[name][:, :], w[name][:, :], 0.5, None, ALU.mult).then_inc(prepared, 1)
    for name, norm in (("left_W", "norm1_w"), ("right_W", "norm1_w"), ("up1_W", "norm2_w"), ("up2_W", "norm2_w")):
        for k in range(KD):
            g.tensor_scalar(w[name][:, k, :], w[name][:, k, :], w[norm][:, k:k + 1], None, ALU.mult).then_inc(prepared, 1)
    g.wait_ge(prepared, 4 + 4 * KD)


def griffin_phase(nc, c, w, experts, x, r, slots):
    ident = c["ident"]
    with ExitStack() as ctx:
        m = Phase(nc, ctx)
        sb, sem, loop_sem = m.sb, m.sem, m.loop_sem
        b = m.banks("gb")
        stats, mv, rstd, veps = (sb("g_" + n, s) for n, s in (
            ("stats", [P, 2, 6]), ("mv", [P, 2, 2]), ("rstd", [P, 2, 1]), ("veps", [P, 2, 1])))
        unit, s1, eps8 = sb("g_unit", [P, 2, 1]), sb("g_s1", [P, 2, 1]), sb("g_eps8", [P, 2])
        xl, xlb = sb("g_xl", [P, 2, D]), [sb(f"g_xlb{q}", [P, 2, D]) for q in range(2)]
        xn, xnT = sb("g_xn", [P, 2, D]), sb("g_xnT", [P, KD, ST])
        left = [sb(f"g_left{q}", [P, KD, ST]) for q in range(2)]
        rpre, xcv = sb("g_rpre", [P, KD, TAPS - 1 + ST]), sb("g_xcv", [P, KD, ST])
        tr, ti, a, tl, a2, u, hs = (sb("g_" + n, [P, KD, ST]) for n in "tr ti a tl a2 u hs".split())
        carry = sb("g_carry", [P, KD])
        prod = [sb(f"g_prod{q}", [P, KD, ST]) for q in range(2)]
        sp4, sp4n, soft = sb("g_sp4", [P, KD]), sb("g_sp4n", [P, KD]), sb("g_soft", [P, 8, KD])
        x1, x1n, x1nT = sb("g_x1", [P, 2, D]), sb("g_x1n", [P, 2, D]), sb("g_x1nT", [P, KD, ST])
        ms, mse, s2 = sb("g_ms", [P, 2]), sb("g_mse", [P, 2]), sb("g_s2", [P, 2])
        sq = sb("g_sq", [P, 2, D], mybir.dt.bfloat16)
        gl = [sb(f"g_gl{j}", [P, ST]) for j in range(3)]
        up_banks = (b[4], b[6], b[7])
        mT = sb("g_mT", [P, KU, ST])

        names = ("stats_done mv_done norm_step xl_done xn_done xlb_done xdb_done xnT_ps xnT_done lr_ps left_done "
                 "rpre_done tap0_done conv_step halo_done gate_ps gates_done a_done tl_done a2_done q_done root_done "
                 "u_done b_done scan_done carry_done prod_done out_ps x1_done sq_done mse_done s2_done x1n_done "
                 "xadd_done x1nT_ps x1nT_done up_ps gl_done m_done down_ps x_done").split()
        S = {n: loop_sem("g_" + n) for n in names}
        gx = [sb(f"g_gx{q}", [P, 2, D]) for q in range(2)]
        now_i, now_p = ([sb(f"g_now_{n}{q}", [P, 2], t) for q in range(2)] for n, t in (("i", U32), ("p", F32)))
        S["now_done"], S["joined"] = loop_sem("g_now_done"), loop_sem("g_joined")
        S["gathered"] = r["gathered"]
        R = router_stage(m, c, experts, x, r, slots[0], "rg_", b[5],
                         x_wait=lambda v, s: v.wait_ge(S["x_done"], after(s + 1)),
                         pe_wait_x=lambda pe, s: None,
                         pe_wait_logits=lambda pe, s: None, pe_wait_rank=lambda pe, s: None)
        setup, exp_done, eps_made, passed_v, passed_g = (sem("g_" + n) for n in "setup exp_done eps_made passed_v passed_g".split())
        N_SETUP = 13
        xt2 = lambda s: x[:, bass.ds(2 * s, 2), :]
        row2 = lambda ap: ap.unsqueeze(1).to_broadcast([P, 2, D])

        def pe_transposes(pe, bank, src, done):
            for t in range(2):
                for k in range(KD):
                    last = pe.transpose(bank[:, k * ST + t * P:k * ST + (t + 1) * P], src[:, t, k * P:(k + 1) * P], ident[:, :])
            last.then_inc(done, 1)

        def pe_features(pe, bank, weight, rhs):
            for j in range(KD):
                for k in range(KD):
                    last = pe.matmul(bank[:, j * ST:(j + 1) * ST], w[weight][:, k, j * P:(j + 1) * P], rhs[:, k, :],
                                     start=(k == 0), stop=(k == KD - 1))
            return last

        def pe_A1(pe, s, q):
            pe.wait_ge(S["xn_done"], at(s, 2))
            pe_transposes(pe, b[0], xn, S["xnT_ps"])
            pe.wait_ge(S["xnT_done"], after(s + 1))
            pe.wait_ge(S["gates_done"], after(4 * s))
            pe_features(pe, b[1], "right_W", xnT).then_inc(S["lr_ps"], 1)
            pe_features(pe, b[2], "left_W", xnT).then_inc(S["lr_ps"], 1)

        def pe_A2(pe, s, q):
            pe.wait_ge(S["conv_step"], at(s, 6))
            pe_features(pe, b[1], "ga_W", xcv).then_inc(S["gate_ps"], 1)
            pe.wait_ge(S["left_done"], at(s, 2))
            pe_features(pe, b[2], "gx_W", xcv).then_inc(S["gate_ps"], 1)

        def pe_out(pe, s, q):
            pe.wait_ge(S["prod_done"], after(s + 1))
            pe.wait_ge(R["ranks_read"], R["ranks_read_after"](s - 1))
            for t in range(2):
                for k in range(KD):
                    last = pe.matmul(b[5][:, t * D:(t + 1) * D], prod[q][:, k, t * P:(t + 1) * P], w["out_W"][:, k, :],
                                     start=(k == 0), stop=(k == KD - 1))
            last.then_inc(S["out_ps"], 1)

        def pe_x1T(pe, s):
            pe.wait_ge(S["x1n_done"], at(s, 2))
            pe_transposes(pe, b[5], x1n, S["x1nT_ps"])
            pe.wait_ge(S["x1nT_done"], after(s + 1))

        def pe_up(pe, s, f0):
            for f in range(f0, f0 + KU // 2):
                pe.wait_ge(S["m_done"], after(KU * s + f - 2))
                for half, name in enumerate(("up1_W", "up2_W")):
                    for k in range(KD):
                        last = pe.matmul(up_banks[f % 3][:, half * ST:(half + 1) * ST], w[name][:, k, f * P:(f + 1) * P],
                                         x1nT[:, k, :], start=(k == 0), stop=(k == KD - 1))
                last.then_inc(S["up_ps"], 1)

        def pe_down(pe, s):
            pe.wait_ge(S["m_done"], at(s, KU))
            pe.wait_ge(S["x_done"], after(s))
            for t in range(2):
                for k in range(KU):
                    last = pe.matmul(b[3][:, t * D:(t + 1) * D], mT[:, k, t * P:(t + 1) * P], w["down_W"][:, k, :],
                                     start=(k == 0), stop=(k == KU - 1))
            last.then_inc(S["down_ps"], 1)

        def pe_body(pe, s, q, ahead, behind):
            R1, R2, R3 = R["pe"]
            pe_out(pe, s, q)
            if behind:
                pe_down(pe, s - 1)
            pe_x1T(pe, s)
            pe_up(pe, s, 0)
            if behind:
                R1(pe, s - 1)
            if ahead:
                pe_A2(pe, s + 1, 1 - q)
            if behind:
                R2(pe, s - 1)
            pe_up(pe, s, KU // 2)
            if ahead > 1:
                pe_A1(pe, s + 2, q)
            if behind:
                R3(pe, s - 1)

        def pe_end(pe):
            pe_down(pe, NS - 1)
            for piece in R["pe"]:
                piece(pe, NS - 1)

        def act_A1(act, s, q):
            act.wait_ge(S["xnT_ps"], after(s + 1))
            act.wait_ge(S["lr_ps"], after(2 * s))
            act.activation(xnT[:, :, :].rearrange("p k t -> p (k t)"), b[0][:, :], ACT.Copy).then_inc(S["xnT_done"], 1)
            act.wait_ge(S["lr_ps"], at(s, 2, 1))
            act.wait_ge(S["halo_done"], after(s + 1))
            act.wait_ge(S["gate_ps"], after(2 * s))
            act.wait_ge(S["u_done"], after(s))
            for j in range(KD):
                act.activation(rpre[:, j, TAPS - 1:], b[1][:, j * ST:(j + 1) * ST], ACT.Identity,
                               bias=w["right_b"][:, j:j + 1]).then_inc(S["rpre_done"], 1)
                act.activation(xcv[:, j, :], b[1][:, j * ST:(j + 1) * ST], ACT.Identity,
                               scale=w["g_conv_w"][:, TAPS - 1, j:j + 1], bias=w["tap_b"][:, j:j + 1]).then_inc(S["tap0_done"], 1)
            act.wait_ge(S["lr_ps"], at(s, 2, 2))
            act.wait_ge(S["prod_done"], after(s - 1))
            for j in range(KD):
                act.activation(left[q][:, j, :], b[2][:, j * ST:(j + 1) * ST], ACT.Gelu, bias=w["left_b"][:, j:j + 1]).then_inc(
                    S["left_done"], 1)

        def act_A2(act, s, q):
            act.wait_ge(S["tl_done"], after(2 * s))
            act.wait_ge(S["u_done"], after(s))
            for n, (dst, bias) in enumerate(((tr, "ga_b"), (ti, "gx_b"))):
                act.wait_ge(S["gate_ps"], at(s, 2, n + 1))
                for j in range(KD):
                    act.activation(dst[:, j, :], b[1 + n][:, j * ST:(j + 1) * ST], ACT.Tanh, scale=0.5,
                                   bias=w[bias][:, j:j + 1]).then_inc(S["gates_done"], 1)

        def act_A3(act, s, q):
            act.wait_ge(S["gates_done"], at(s, 4, 2))
            act.wait_ge(S["scan_done"], after(s))
            act.wait_ge(S["b_done"], after(s))
            for dst, func, by, done in ((a, ACT.Exp, sp4, "a_done"), (tl, ACT.Tanh, sp4n, "tl_done")):
                for j in range(KD):
                    act.activation(dst[:, j, :], tr[:, j, :], func, scale=by[:, j:j + 1], bias=by[:, j:j + 1]).then_inc(
                        S[done], 1)

        def act_root(act, s, q):
            act.wait_ge(S["q_done"], after(s + 1))
            act.activation(tl[:, :, :], a2[:, :, :], ACT.Sqrt, scale=0.25).then_inc(S["root_done"], 1)

        def act_sq(act, s):
            act.wait_ge(S["x1_done"], after(s + 1))
            act.wait_ge(S["mse_done"], after(s))
            for t in range(2):
                act.activation(sq[:, t, :], x1[:, t, :], ACT.Square, scale=D ** -0.5, accum_out=ms[:, t:t + 1]).then_inc(
                    S["sq_done"], 1)

        def act_x1T(act, s):
            act.wait_ge(S["x1nT_ps"], after(s + 1))
            act.wait_ge(S["up_ps"], after(KU * s))
            act.activation(x1nT[:, :, :].rearrange("p k t -> p (k t)"), b[5][:, :], ACT.Copy).then_inc(S["x1nT_done"], 1)

        def act_up(act, s, f0):
            for f in range(f0, f0 + KU // 2):
                act.wait_ge(S["up_ps"], at(s, KU, f + 1))
                act.wait_ge(S["m_done"], after(KU * s + f - 2))
                act.activation(gl[f % 3][:, :], up_banks[f % 3][:, 0:ST], ACT.Gelu, bias=w["up1_b"][:, f:f + 1]).then_inc(
                    S["gl_done"], 1)

        def act_body(act, s, q, ahead, behind):
            R1, R2 = R["act"]
            act_sq(act, s)
            act_x1T(act, s)
            act_up(act, s, 0)
            if behind:
                R1(act, s - 1)
            if ahead:
                act_A2(act, s + 1, 1 - q)
                act_A3(act, s + 1, 1 - q)
            if behind:
                R2(act, s - 1)
            if ahead:
                act_root(act, s + 1, 1 - q)
            act_up(act, s, KU // 2)
            if ahead > 1:
                act_A1(act, s + 2, q)

        def act_end(act):
            for piece in R["act"]:
                piece(act, NS - 1)

        def dve_setup(v):
            n = [0]

            def step(instruction):
                n[0] += 1
                instruction.then_inc(setup, 1)
                v.wait_ge(setup, n[0])

            v.memset(carry[:, :], 0.0).then_inc(S["carry_done"], 1)
            v.memset(rpre[:, :, 0:TAPS - 1], 0.0).then_inc(S["halo_done"], 1)
            vv, nv, e, den, r, z, z2, p = (soft[:, i, :] for i in range(8))
            vv = w["a_param"][:, :]
            step(v.scalar_tensor_tensor(out=nv, in0=vv, scalar=-1.0, in1=vv, op0=ALU.mult, op1=ALU.min))
            v.wait_ge(exp_done, 1)
            step(v.tensor_scalar(den, e, 2.0, None, ALU.add))
            step(v.reciprocal(r, den))
            step(v.tensor_tensor(z, e, r, ALU.mult))
            step(v.tensor_tensor(z2, z, z, ALU.mult))
            step(v.tensor_scalar(p, z2, ATANH[4], ATANH[3], ALU.mult, ALU.add))
            step(v.scalar_tensor_tensor(out=p, in0=p, scalar=0.0, in1=z2, op0=ALU.add, op1=ALU.mult))
            step(v.scalar_tensor_tensor(out=p, in0=p, scalar=ATANH[2], in1=z2, op0=ALU.add, op1=ALU.mult))
            step(v.scalar_tensor_tensor(out=p, in0=p, scalar=ATANH[1], in1=z2, op0=ALU.add, op1=ALU.mult))
            step(v.scalar_tensor_tensor(out=p, in0=p, scalar=ATANH[0], in1=z, op0=ALU.add, op1=ALU.mult))
            step(v.scalar_tensor_tensor(out=p, in0=vv, scalar=0.0, in1=p, op0=ALU.max, op1=ALU.add))
            step(v.tensor_scalar(sp4[:, :], p, -C_RGLRU / 2, None, ALU.mult))
            step(v.tensor_scalar(sp4n[:, :], p, C_RGLRU / 2, None, ALU.mult))
            assert n[0] == N_SETUP, n[0]

        def dve_rows(v, s, q):
            v.wait_ge(S["joined"], after(2 * s - 2))
            v.tensor_copy(now_i[q][:, :], r["pos_i"][:, bass.ds(2 * s, 2)]).then_inc(S["now_done"], 1)
            v.tensor_copy(now_p[q][:, :], r["prob"][:, bass.ds(2 * s, 2)]).then_inc(S["now_done"], 1)

        def dve_join(v, s, q):
            v.wait_ge(S["now_done"], at(s, 2))
            v.wait_ge(S["gathered"][q], 16 * (s - q) + 32)
            for t in range(2):
                xs = x[:, bass.ds(2 * s + t, 1), :].rearrange("p a d -> p (a d)")
                v.scalar_tensor_tensor(out=xs, in0=gx[q][:, t, :], scalar=now_p[q][:, t:t + 1], in1=xs, op0=ALU.mult,
                                       op1=ALU.add).then_inc(S["joined"], 1)
            v.wait_ge(S["joined"], at(s, 2))

        def dve_stats(v, s, q):
            dve_join(v, s, q)
            dve_rows(v, s + 1, 1 - q)
            wait_apart(v, passed_v, S["norm_step"], at(s, 6, 0))
            for t in range(2):
                v.bn_stats(stats[:, t, :], x[:, bass.ds(2 * s + t, 1), :].rearrange("p a d -> p (a d)")).then_inc(
                    S["stats_done"], 1)
            for t in range(2):
                wait_apart(v, passed_v, S["stats_done"], at(s, 2, t + 1))
                v.bn_aggr(mv[:, t, :], stats[:, t, :]).then_inc(S["mv_done"], 1)

        def dve_xl(v, s, q):
            v.wait_ge(S["norm_step"], at(s, 6, 2))
            v.wait_ge(S["xlb_done"], after(s))
            for t in range(2):
                v.tensor_scalar(xl[:, t, :], x[:, bass.ds(2 * s + t, 1), :].rearrange("p a d -> p (a d)"),
                                mv[:, t, 0:1], rstd[:, t, :], ALU.subtract, ALU.mult).then_inc(S["xl_done"], 1)

        def dve_xn(v, s, q):
            v.wait_ge(S["xl_done"], at(s, 2))
            v.wait_ge(S["norm_step"], at(s, 6, 6))
            v.wait_ge(S["xnT_ps"], after(s))
            for t in range(2):
                v.tensor_scalar(xn[:, t, :], xl[:, t, :], s1[:, t, :], None, ALU.mult).then_inc(S["xn_done"], 1)

        def dve_conv(v, s, q):
            for n, tap in enumerate((2, 1, 0)):
                for j in range(KD):
                    if n:
                        v.wait_ge(S["conv_step"], at(s, 6, 2 * n + j - 1))
                    else:
                        v.wait_ge(S["tap0_done"], at(s, 2, j + 1))
                    v.scalar_tensor_tensor(out=xcv[:, j, :], in0=rpre[:, j, tap:tap + ST], scalar=w["g_conv_w"][:, tap, j:j + 1],
                                           in1=xcv[:, j, :], op0=ALU.mult, op1=ALU.add).then_inc(S["conv_step"], 1)
            v.wait_ge(S["conv_step"], at(s, 6))
            v.tensor_copy(rpre[:, :, 0:TAPS - 1], rpre[:, :, ST:ST + TAPS - 1]).then_inc(S["halo_done"], 1)

        def dve_q(v, s, q):
            v.wait_ge(S["gates_done"], at(s, 4))
            v.wait_ge(S["b_done"], after(s))
            v.scalar_tensor_tensor(out=u[:, :, :], in0=ti[:, :, :], scalar=1.0, in1=xcv[:, :, :], op0=ALU.add,
                                   op1=ALU.mult).then_inc(S["u_done"], 1)
            v.wait_ge(S["a_done"], at(s, 2))
            v.wait_ge(S["root_done"], after(s))
            v.tensor_tensor(a2[:, :, :], a[:, :, :], a[:, :, :], ALU.mult).then_inc(S["a2_done"], 1)
            v.wait_ge(S["a2_done"], after(s + 1))
            v.wait_ge(S["tl_done"], at(s, 2))
            v.scalar_tensor_tensor(out=a2[:, :, :], in0=a2[:, :, :], scalar=1.0, in1=tl[:, :, :], op0=ALU.add,
                                   op1=ALU.mult).then_inc(S["q_done"], 1)

        def dve_scan(v, s, q):
            v.wait_ge(S["root_done"], after(s + 1))
            v.tensor_tensor(u[:, :, :], u[:, :, :], tl[:, :, :], ALU.mult).then_inc(S["b_done"], 1)
            v.wait_ge(S["b_done"], after(s + 1))
            v.wait_ge(S["carry_done"], after(s + 1))
            for j in range(KD):
                last = v.tensor_tensor_scan(hs[:, j, :], a[:, j, :], u[:, j, :], carry[:, j:j + 1], ALU.mult, ALU.add)
            last.then_inc(S["scan_done"], 1)
            v.wait_ge(S["scan_done"], after(s + 1))
            v.wait_ge(S["left_done"], at(s, 2))
            v.wait_ge(S["out_ps"], after(s - 1))
            v.tensor_tensor(prod[q][:, :, :], left[q][:, :, :], hs[:, :, :], ALU.mult).then_inc(S["prod_done"], 1)
            v.tensor_copy(carry[:, :], hs[:, :, ST - 1]).then_inc(S["carry_done"], 1)

        def dve_x1(v, s, q):
            v.wait_ge(S["out_ps"], after(s + 1))
            v.wait_ge(S["xlb_done"], after(s + 1))
            v.wait_ge(S["xadd_done"], after(s))
            v.tensor_tensor(x1[:, :, :].rearrange("p t d -> p (t d)"), b[5][:, :], xlb[q][:, :, :].rearrange("p t d -> p (t d)"),
                            ALU.add).then_inc(S["x1_done"], 1)

        def dve_x1n(v, s):
            v.wait_ge(S["s2_done"], after(s + 1))
            v.wait_ge(S["x1_done"], after(s + 1))
            v.wait_ge(S["x1nT_ps"], after(s))
            for t in range(2):
                v.tensor_scalar(x1n[:, t, :], x1[:, t, :], s2[:, t:t + 1], None, ALU.mult).then_inc(S["x1n_done"], 1)

        def dve_m(v, s, f0, f1):
            for f in range(f0, f1):
                v.wait_ge(S["gl_done"], at(s, KU, f + 1))
                v.wait_ge(S["down_ps"], after(s))
                v.scalar_tensor_tensor(out=mT[:, f, :], in0=up_banks[f % 3][:, ST:2 * ST], scalar=w["up2_b"][:, f:f + 1],
                                       in1=gl[f % 3][:, :], op0=ALU.add, op1=ALU.mult).then_inc(S["m_done"], 1)

        def dve_x(v, s):
            v.wait_ge(S["down_ps"], after(s + 1))
            v.wait_ge(S["xadd_done"], after(s + 1))
            v.tensor_tensor(xt2(s).rearrange("p t d -> p (t d)"), b[3][:, :], xt2(s).rearrange("p t d -> p (t d)"),
                            ALU.add).then_inc(S["x_done"], 1)

        def dve_body(v, s, q, ahead, behind):
            R0, R1, R2, R3 = R["dve"]
            dve_x1(v, s, q)
            if ahead > 1:
                dve_stats(v, s + 2, q)
            dve_x1n(v, s)
            if ahead:
                dve_conv(v, s + 1, 1 - q)
            if behind:
                dve_x(v, s - 1)
                R0(v, s - 1)
            if ahead > 1:
                dve_xl(v, s + 2, q)
            dve_m(v, s, 0, 1)
            if behind:
                R1(v, s - 1)
            dve_m(v, s, 1, 3)
            if ahead > 1:
                dve_xn(v, s + 2, q)
            if ahead:
                dve_q(v, s + 1, 1 - q)
            if behind:
                R2(v, s - 1)
            dve_m(v, s, 3, 5)
            if ahead:
                dve_scan(v, s + 1, 1 - q)
            dve_m(v, s, 5, 6)
            if behind:
                R3(v, s - 1)

        def dve_end(v):
            dve_x(v, NS - 1)
            for piece in R["dve"]:
                piece(v, NS - 1)

        def pool_gather(g, s, q):
            wait_apart(g, passed_g, S["now_done"], at(s, 2))
            for t in range(2):
                g.indirect_dma_start(gx[q][:, t, :], None, slots[1][:, :],
                                     bass.IndirectOffsetOnAxis(now_i[q][:, t:t + 1], 0)).then_inc(S["gathered"][q], 16)

        def pool_norm(g, s, q):
            half_neg = c["half_neg"][:, :].unsqueeze(2)
            g.wait_ge(S["mv_done"], at(s, 2))
            g.wait_ge(S["xn_done"], after(2 * s))
            for n, (out, in0, in1, op) in enumerate((
                    (veps, mv[:, :, 1:2], c["eps"][:, :].unsqueeze(2), ALU.add),
                    (rstd, veps[:, :, :], half_neg, ALU.pow),
                    (unit, rstd[:, :, :], rstd[:, :, :], ALU.mult),
                    (unit, unit[:, :, :], mv[:, :, 1:2], ALU.mult),
                    (unit, unit[:, :, :], eps8[:, :].unsqueeze(2), ALU.add),
                    (s1, unit[:, :, :], half_neg, ALU.pow))):
                if n:
                    g.wait_ge(S["norm_step"], at(s, 6, n))
                g.tensor_tensor(out[:, :, :], in0, in1, op).then_inc(S["norm_step"], 1)

        def pool_biases(g, s, q):
            g.wait_ge(S["xl_done"], at(s, 2))
            g.wait_ge(S["x1_done"], after(s - 1))
            g.tensor_tensor(xlb[q][:, :, :], xl[:, :, :], row2(w["out_b"][:, :]), ALU.add).then_inc(S["xlb_done"], 1)
            wait_apart(g, passed_g, S["xl_done"], at(s, 2))
            g.tensor_tensor(xt2(s), xt2(s), row2(w["down_b"][:, :]), ALU.add).then_inc(S["xdb_done"], 1)

        def pool_s2(g, s):
            g.wait_ge(S["sq_done"], at(s, 2))
            g.tensor_tensor(mse[:, :], ms[:, :], eps8[:, :], ALU.add).then_inc(S["mse_done"], 1)
            g.wait_ge(S["mse_done"], after(s + 1))
            g.wait_ge(S["x1n_done"], after(2 * s))
            g.tensor_tensor(s2[:, :], mse[:, :], c["half_neg"][:, :], ALU.pow).then_inc(S["s2_done"], 1)

        def pool_xadd(g, s):
            wait_apart(g, passed_g, S["xdb_done"], after(s + 1))
            g.tensor_tensor(xt2(s), xt2(s), x1[:, :, :], ALU.add).then_inc(S["xadd_done"], 1)

        def pool_body(g, s, q, ahead, behind):
            R0, R3, R4 = R["pool"]
            pool_s2(g, s)
            if ahead > 1:
                pool_norm(g, s + 2, q)
            pool_xadd(g, s)
            if behind:
                R0(g, s - 1)
            if ahead > 1:
                pool_gather(g, s + 3, 1 - q)
                pool_biases(g, s + 2, q)
            if behind:
                R3(g, s - 1)
                R4(g, s - 1)

        def pool_end(g):
            for piece in R["pool"][:2]:
                piece(g, NS - 1)

        def program(e, stage_1, stage_2, body, end):
            stage_1(e, 0, 0)
            stage_2(e, 0, 0)
            stage_1(e, 1, 1)
            body(e, 0, 0, 2, False)
            with e.Fori(0, NS // 2 - 2) as i:
                body(e, 2 * i + 1, 1, 2, True)
                body(e, 2 * i + 2, 0, 2, True)
            for s in range(NS - 3, NS):
                body(e, s, s % 2, min(2, NS - 1 - s), True)
            end(e)

        def all_of(*pieces):
            def run(*args):
                for piece in pieces:
                    piece(*args)
            return run

        m.start_loop_sems()
        with nc.Block() as block:

            @block.tensor
            def _(pe):
                program(pe, pe_A1, pe_A2, pe_body, pe_end)

            @block.scalar
            def _(act):
                act.wait_ge(setup, 1)
                act.activation(soft[:, 2, :], soft[:, 1, :], ACT.Exp).then_inc(exp_done, 1)
                act.wait_ge(setup, N_SETUP)
                program(act, act_A1, all_of(act_A2, act_A3, act_root), act_body, act_end)

            @block.vector
            def _(v):
                dve_rows(v, 0, 0)
                dve_setup(v)
                program(v, all_of(dve_stats, dve_xl, dve_xn), all_of(dve_conv, dve_q, dve_scan), dve_body, dve_end)
                v.wait_ge(R["noted"], after(3 * NS))

            @block.gpsimd
            def _(g):
                g.memset(eps8[:, :], 1e-8).then_inc(eps_made, 1)
                g.wait_ge(eps_made, 1)
                pool_gather(g, 0, 0)
                program(g, all_of(lambda e, s, q: pool_gather(e, s + 1, 1 - q), pool_norm, pool_biases), lambda *_: None,
                        pool_body, pool_end)
                g.wait_ge(S["gathered"][0], 16 * NS + 32)
        m.clear()


_PARTS = {"u": "L0_attn_a_u", "W_in": "L0_attn_a_W_in", "conv_w": "L0_attn_a_conv_w", "conv_b": "L0_attn_a_conv_b",
          "dt_bias": "L0_attn_a_dt_bias", "A_log": "L0_attn_a_A_log", "Dp": "L0_attn_a_Dp",
          "norm_w": "L0_attn_a_norm_w", "W_out": "L0_attn_a_W_out",
          "router": "L0_ffn_router_w", "gate": "L0_ffn_gate_w", "up": "L0_ffn_up_w", "down": "L0_ffn_down_w", "g_conv_w": "L0_attn_b_conv_w", "g_conv_b": "L0_attn_b_conv_b"}
_PARTS.update({n: "L0_attn_b_" + n for n in (
    "norm1_w left_W left_b right_W right_b ga_W ga_b gx_W gx_b a_param out_W out_b norm2_w up1_W up1_b up2_W up2_b "
    "down_W down_b").split()})


def build(nc, a, out):
    with ExitStack() as ctx:
        m = Memory(nc, ctx)
        x = m.sb("x", [P, NT, D])
        x_loaded = [m.sem(f"x_loaded{t}") for t in range(4)]
        zeros, zeros_made, slots_zeroed = m.sb("zeros", [P, D]), m.sem("zeros_made"), m.sem("slots_zeroed")
        r = {"prob": m.sb("prob", [P, NT + 2]), "onehot": m.sb("onehot", [P, NT, E]), "pos": m.sb("pos", [P, NT]),
             "pos_i": m.sb("pos_i", [P, NT + 2], U32), "cum": m.sb("cum", [P, E]),
             "scattered": {tag: m.sem(tag + "scattered") for tag in ("ra_", "rg_")},
             "gathered": [m.sem(f"gathered{q}") for q in range(2)], "gathered_last": [m.sem(f"gathered_last{s}") for s in range(NS)]}
        c = make_constants(nc, m, zeros, zeros_made, r["cum"])
        c["zeros"] = zeros
        w = {"router": m.sb("router", [P, KD, E]), "gate": m.sb("gate", [P, E, KD, FI]), "up": m.sb("up", [P, E, KD, FI]),
             "down": m.sb("down", [P, E, KF, D]), "loaded": [m.sem(f"experts_loaded{k}") for k in range(4)]}
        slots = [nc.dram_tensor(n, (k * P, D), F32).ap() for n, k in (("slots_in", E * ROOM), ("slots_out", MAXT))]

        def load_experts(sp):
            sp.dma_start(slots[1].rearrange("(t p) d -> p t d", p=P), zeros[:, :].unsqueeze(1).to_broadcast([P, MAXT, D])).then_inc(
                slots_zeroed, 16)
            for k, name in enumerate(("gate", "up", "down")):
                sp.dma_start(w[name][:, :, :, :], a[name].rearrange("e (k p) f -> p e k f", p=P)).then_inc(w["loaded"][k + 1], 16)

        def load_router(sp):
            sp.dma_start(w["router"][:, :, :], a["router"].rearrange("(k p) e -> p k e", p=P)).then_inc(w["loaded"][0], 16)

        mamba_phase(nc, a, c, w, x, r, slots[0], x_loaded, load_router, load_experts)
        gw, loads = griffin_weights(nc, m, a)
        griffin_loaded = m.sem("griffin_loaded")

        def load_griffin(sp):
            for dst, src in loads:
                sp.dma_start(dst, src, allow_slow_non_contiguous=True).then_inc(griffin_loaded, 16)

        griffin_prepared = m.sem("griffin_prepared")

        def prepare_griffin(g):
            prepare_griffin_weights(g, gw, len(loads), griffin_loaded, griffin_prepared)

        moe_phase(nc, c, w, slots, slots_zeroed, x, r, "ra_", "f1_", load_griffin, prepare_griffin)
        griffin_phase(nc, c, gw, w, x, r, slots)
        moe_phase(nc, c, w, slots, slots_zeroed, x, r, "rg_", "f2_", lambda sp: None, lambda g: None)
        finish(nc, m, x, r, slots[1], out)


def finish(nc, m, x, r, slots_out, out):
    gx = m.sb("gx", [P, NT, D])
    gathered, joined, stored = r["gathered_last"], m.sem("joined"), m.sem("stored")
    with nc.Block() as block:

        @block.gpsimd
        def _(g):
            for t in range(NT):
                g.indirect_dma_start(gx[:, t, :], None, slots_out[:, :],
                                     bass.IndirectOffsetOnAxis(r["pos_i"][:, t:t + 1], 0)).then_inc(gathered[t // 2], 16)

        @block.vector
        def _(v):
            for t in range(NT):
                v.wait_ge(gathered[t // 2], 32)
                v.scalar_tensor_tensor(out=x[:, t, :], in0=gx[:, t, :], scalar=r["prob"][:, t:t + 1], in1=x[:, t, :],
                                       op0=ALU.mult, op1=ALU.add).then_inc(joined, 1)

        @block.sync
        def _(sp):
            for s in range(NS):
                sp.wait_ge(joined, 2 * s + 2)
                sp.dma_start(out[0, s * ST:(s + 1) * ST, :].rearrange("(r p) d -> p r d", p=P),
                             x[:, 2 * s:2 * s + 2, :]).then_inc(stored, 16)
            sp.wait_ge(stored, 16 * NS)


def kernel(**inputs):
    import numpy as _np
    import concourse.bacc as _bacc
    from concourse import mybir as _mybir
    from concourse.bass_utils import run_bass_kernel_spmd as _run

    nc = _bacc.Bacc("TRN2", target_bir_lowering=False, num_devices=1)
    arrays, args = {}, {}
    for short, name in _PARTS.items():
        v = _np.ascontiguousarray(inputs[name])
        arrays[f"in_{name}_dram"] = v
        args[short] = nc.dram_tensor(f"in_{name}_dram", v.shape, _mybir.dt.from_np(v.dtype), kind="ExternalInput").ap()
    out = nc.dram_tensor("out_0_dram", (1, TOKENS, D), _mybir.dt.float32, kind="ExternalOutput").ap()
    build(nc, args, out)
    r = _run(nc, [arrays], core_ids=[0])
    return r.results[0]["out_0_dram"]
```

```python
from contextlib import ExitStack

import numpy as np

import concourse.bass as bass
from concourse import mybir

F32 = mybir.dt.float32
I32 = mybir.dt.int32
U32 = mybir.dt.uint32
ALU = mybir.AluOpType
ACT = mybir.ActivationFunctionType
AX = mybir.AxisListType

P = 128
TOKENS, D = 2048, 256
KD = D // P
NT = TOKENS // P
NS = NT // 2
ST = 2 * P

DI, DS, NH, DH, TAPS = 512, 128, 8, 64, 4
KI = DI // P
CB = (DI + 2 * DS) // P
XBC0 = DI
DT0 = DI + CB * P
DPROJ = DT0 + NH
ATANH = (2.000000007877749, 0.6666631593507903, 0.40024853723562315, 0.2796141883332212, 0.28174657270344106)

E, FI = 8, 512
KF = FI // P
F, KU = 768, 768 // P
C_RGLRU = 8.0
MAXT = NT + E + 1
ROOM = NT + 1


START = 2


def after(n):
    return START + (max(n, 0) if isinstance(n, int) else n)


def at(s, per, k=None):
    return after(s * per + (per if k is None else k))


def wait_apart(e, passed, sem, value):
    e.wait_ge(sem, value)
    e.sem_inc(passed, 1)


class Memory:

    def __init__(self, nc, ctx):
        self.nc, self.ctx = nc, ctx

    def sb(self, name, shape, dt=F32):
        return self.ctx.enter_context(self.nc.sbuf_tensor(name, shape, dt))

    def banks(self, name):
        return [self.ctx.enter_context(self.nc.psum_tensor(f"{name}{i}", [P, 512], F32)) for i in range(8)]

    def sem(self, name):
        return self.ctx.enter_context(self.nc.semaphore(name))


class Phase(Memory):

    def __init__(self, nc, ctx):
        super().__init__(nc, ctx)
        self.sems, self.loop_sems = [], []

    def sem(self, name):
        self.sems.append(super().sem(name))
        return self.sems[-1]

    def loop_sem(self, name):
        self.loop_sems.append(self.sem(name))
        return self.loop_sems[-1]

    def start_loop_sems(self, more=()):
        loop_sems = [*self.loop_sems, *more]
        with self.nc.Block() as block:
            for n, on in enumerate((block.sync, block.scalar, block.vector, block.tensor)):
                def _(e, n=n):
                    for s in loop_sems[n::4]:
                        e.sem_inc(s, START)
                on(_)

    def clear(self, e):
        for s in self.sems:
            e.sem_clear(s)


def make_constants(m, zeros, zeros_made, cum):
    c = {
        "ident": m.sb("ident", [P, P]),
        "tri_le": m.sb("tri_le", [P, P]),
        "tri_gt": m.sb("tri_gt", [P, P]),
        "ones": m.sb("ones", [P, P]),
        "half_neg": m.sb("half_neg", [P, 2]),
        "eps": m.sb("eps", [P, 2]),
        "prio": m.sb("prio", [P, E]),
        "room": m.sb("room", [P, E]),
        "room_less1": m.sb("room_less1", [P, E]),
        "thresh": m.sb("thresh", [P, NT]),
        "tile_no": m.sb("tile_no", [P, MAXT]),
    }
    ready, filled = m.sem("const_ready"), m.sem("const_filled")

    def fill(g):
        g.memset(zeros[:, :], 0.0).then_inc(zeros_made, 1)
        g.memset(c["ident"][:, :], 0.0).then_inc(filled, 1)
        for name in ("tri_le", "tri_gt"):
            g.memset(c[name][:, :], 1.0).then_inc(filled, 1)
        g.memset(c["ones"][:, :], 1.0)
        g.memset(c["half_neg"][:, :], -0.5)
        g.memset(c["eps"][:, :], 1e-5)
        g.memset(cum[:, :, :], 0.0)
        for n in range(E):
            g.memset(c["prio"][:, n:n + 1], float(E - n))
            g.memset(c["room"][:, n:n + 1], float(n * ROOM * P))
            g.memset(c["room_less1"][:, n:n + 1], float(n * ROOM * P - 1))
        for t in range(NT):
            g.memset(c["thresh"][:, t:t + 1], float(t * P))
        for t in range(MAXT):
            g.memset(c["tile_no"][:, t:t + 1], float(t))
        g.wait_ge(filled, 3)
        for name, op, row, col, fill in (("ident", ALU.not_equal, 1, -1, 1.0), ("tri_le", ALU.is_ge, -1, 1, 0.0),
                                         ("tri_gt", ALU.is_gt, 1, -1, 0.0)):
            g.affine_select(out=c[name][:, :], in_=c[name][:, :], compare_op=op, fill=fill, base=0,
                            pattern=[[col, P]], channel_multiplier=row).then_inc(ready, 1)
        g.wait_ge(ready, 3)

    c["fill"], c["ready"] = fill, ready
    return c


def router_stage(m, c, w, x, r, slots_in, tag, bank, x_wait, pe_wait_x, pe_wait_rank,
                 last_rows, last_rows_free, rank_bank=None):
    ident, tri_le, ones = c["ident"], c["tri_le"], c["ones"]
    rank_bank = rank_bank or bank
    is_last = lambda s: isinstance(s, int) and s == NS - 1
    rows = lambda s: last_rows if is_last(s) else xs
    sb = m.sb
    stats, mv, rstd, veps = (sb(tag + n, s) for n, s in (
        ("stats", [P, 2, 6]), ("mv", [P, 2, 2]), ("rstd", [P, 2, 1]), ("veps", [P, 2, 1])))
    xs, xsT = sb(tag + "xs", [P, 2, D]), sb(tag + "xsT", [P, KD, ST])
    er, sig, eq, hot, place = (sb(tag + n, [P, 2, E]) for n in "er sig eq hot place".split())
    top, best, pos, pos_i = sb(tag + "top", [P, 2]), sb(tag + "best", [P, 2]), sb(tag + "pos", [P, 2]), sb(tag + "pos_i", [P, 2], U32)
    (stats_done, mv_done, veps_done, rstd_done, xs_done, xsT_ps, xsT_done, logit_ps, er_done, step_done, rank_ps,
     cum_done, noted, scatter_seen) = (m.loop_sem(tag + n) for n in (
         "stats_done mv_done veps_done rstd_done xs_done xsT_ps xsT_done logit_ps er_done step_done rank_ps "
         "cum_done noted scatter_seen").split())
    passed_v, passed_g, scattered = m.sem(tag + "passed_v"), m.sem(tag + "passed_g"), r["scattered"][tag]
    NR, HOT, PLACE = 11, 7, 8
    flat = lambda ap: ap.rearrange("p t e -> p (t e)")
    by_tile = lambda ap: ap.unsqueeze(1).to_broadcast([P, 2, E])
    by_expert = lambda ap: ap.unsqueeze(2).to_broadcast([P, 2, E])

    def pe_R1(pe, s):
        pe_wait_x(pe, s)
        pe.wait_ge(xs_done, at(s, 2))
        for t in range(2):
            for k in range(KD):
                last = pe.transpose(bank[:, k * ST + t * P:k * ST + (t + 1) * P], rows(s)[:, t, k * P:(k + 1) * P], ident[:, :])
        last.then_inc(xsT_ps, 1)

    def pe_R2(pe, s):
        pe.wait_ge(xsT_done, after(s + 1))
        for t in range(2):
            for k in range(KD):
                last = pe.matmul(bank[:, t * E:(t + 1) * E], xsT[:, k, t * P:(t + 1) * P], w["router"][:, k, :],
                                 start=(k == 0), stop=(k == KD - 1))
        last.then_inc(logit_ps, 1)

    def pe_R3(pe, s):
        pe_wait_rank(pe, s)
        pe.wait_ge(step_done, at(s, NR, HOT))
        pe.wait_ge(er_done, after(s + 1))
        pe.wait_ge(cum_done, at(s, 2, 1))
        pe.matmul(rank_bank[:, 0:2 * E], tri_le[:, :], flat(hot[:, :, :]), start=True, stop=False)
        pe.matmul(rank_bank[:, 0:2 * E], ones[:, :], flat(r["cum"][:, :, :]), start=False, stop=True).then_inc(rank_ps, 1)

    def act_R1(act, s):
        act.wait_ge(xsT_ps, after(s + 1))
        act.wait_ge(logit_ps, after(s))
        act.activation(xsT[:, :, :].rearrange("p k t -> p (k t)"), bank[:, :], ACT.Copy).then_inc(xsT_done, 1)

    def act_R2(act, s):
        act.wait_ge(logit_ps, after(s + 1))
        act.wait_ge(step_done, after(NR * s))
        act.activation(flat(er[:, :, :]), bank[:, 0:2 * E], ACT.Exp, scale=-1.0).then_inc(er_done, 1)

    def dve_R0(v, s):
        x_wait(v, s)
        wait_apart(v, passed_v, rstd_done, after(s))
        for t in range(2):
            v.bn_stats(stats[:, t, :], x[:, bass.ds(2 * s + t, 1), :].rearrange("p a d -> p (a d)")).then_inc(stats_done, 1)
        for t in range(2):
            wait_apart(v, passed_v, stats_done, at(s, 2, t + 1))
            v.bn_aggr(mv[:, t, :], stats[:, t, :]).then_inc(mv_done, 1)

    def dve_R1(v, s):
        v.wait_ge(rstd_done, after(s + 1))
        if is_last(s):
            last_rows_free(v)
        else:
            v.wait_ge(xsT_ps, after(s))
            v.wait_ge(scatter_seen, after(s))
        for t in range(2):
            v.tensor_scalar(rows(s)[:, t, :], x[:, bass.ds(2 * s + t, 1), :].rearrange("p a d -> p (a d)"),
                            mv[:, t, 0:1], rstd[:, t, :], ALU.subtract, ALU.mult).then_inc(xs_done, 1)

    def stepper(v, s, n):
        def step(instruction):
            n[0] += 1
            instruction.then_inc(step_done, 1)
            v.wait_ge(step_done, at(s, NR, n[0]))
        return step

    def dve_R2(v, s):
        n = [0]
        step = stepper(v, s, n)
        v.wait_ge(er_done, after(s + 1))
        step(v.tensor_scalar(flat(er[:, :, :]), flat(er[:, :, :]), 1.0, None, ALU.add))
        step(v.reciprocal(flat(sig[:, :, :]), flat(er[:, :, :])))
        step(v.tensor_reduce(top[:, :], sig[:, :, :], AX.X, ALU.max))
        step(v.tensor_tensor(eq[:, :, :], sig[:, :, :], by_expert(top[:, :]), ALU.is_equal))
        step(v.tensor_tensor(eq[:, :, :], eq[:, :, :], by_tile(c["prio"][:, :]), ALU.mult))
        step(v.tensor_reduce(best[:, :], eq[:, :, :], AX.X, ALU.max))
        v.wait_ge(cum_done, after(2 * s))
        step(v.tensor_tensor(hot[:, :, :], by_tile(c["prio"][:, :]), by_expert(best[:, :]), ALU.is_equal))
        assert n[0] == HOT
        v.tensor_copy(r["prob"][:, bass.ds(2 * s, 2)], top[:, :]).then_inc(noted, 1)
        v.tensor_copy(r["onehot"][:, bass.ds(2 * s, 2), :], hot[:, :, :]).then_inc(noted, 1)

    def dve_R3(v, s):
        n = [HOT]
        step = stepper(v, s, n)
        v.wait_ge(rank_ps, after(s + 1))
        step(v.tensor_tensor(place[:, :, :], rank_bank[:, 0:2 * E].rearrange("p (t e) -> p t e", e=E), by_tile(c["room_less1"][:, :]), ALU.add))
        assert n[0] == PLACE
        step(v.tensor_tensor(place[:, :, :], place[:, :, :], hot[:, :, :], ALU.mult))
        step(v.tensor_reduce(pos[:, :], place[:, :, :], AX.X, ALU.add))
        v.wait_ge(scatter_seen, after(s))
        step(v.tensor_copy(pos_i[:, :], pos[:, :]))
        assert n[0] == NR
        v.tensor_copy(r["pos"][:, bass.ds(2 * s, 2)], pos[:, :]).then_inc(noted, 1)

    def pool_R0(g, s):
        g.wait_ge(mv_done, at(s, 2))
        g.tensor_tensor(veps[:, :, :], mv[:, :, 1:2], c["eps"][:, :].unsqueeze(2), ALU.add).then_inc(veps_done, 1)
        g.wait_ge(veps_done, after(s + 1))
        g.wait_ge(xs_done, after(2 * s))
        g.tensor_tensor(rstd[:, :, :], veps[:, :, :], c["half_neg"][:, :].unsqueeze(2), ALU.pow).then_inc(rstd_done, 1)

    def pool_R2(g, s):
        g.wait_ge(step_done, at(s, NR, HOT))
        g.wait_ge(cum_done, after(2 * s))
        g.tensor_tensor(r["cum"][:, 1, :], r["cum"][:, 0, :], hot[:, 0, :], ALU.add).then_inc(cum_done, 1)

    def pool_R3(g, s):
        g.wait_ge(rank_ps, after(s + 1))
        g.tensor_tensor(r["cum"][:, 0, :], r["cum"][:, 1, :], hot[:, 1, :], ALU.add).then_inc(cum_done, 1)
        wait_apart(g, passed_g, step_done, at(s, NR))
        for t in range(2):
            g.indirect_dma_start(slots_in[:, :], bass.IndirectOffsetOnAxis(pos_i[:, t:t + 1], 0), rows(s)[:, t, :],
                                 None).then_inc(scattered, 16)

    def pool_R4(g, s):
        g.wait_ge(scattered, 32 * s + 32)
        g.sem_inc(scatter_seen, 1)

    return {"pe": (pe_R1, pe_R2, pe_R3), "act": (act_R1, act_R2), "dve": (dve_R0, dve_R1, dve_R2, dve_R3),
            "pool": (pool_R0, pool_R2, pool_R3, pool_R4), "rows_read": xsT_done, "cum_done": cum_done,
            "scratch": xsT[:, :, :].rearrange("p k t -> p (k t)"), "logits_read": er_done, "ranks_read": step_done,
            "ranks_read_after": lambda s: after(NR * s), "noted": noted}


def group_stage(m, c, r, R, slots_in, tag, bank, pe_wait_bank):
    scratch, used = R["scratch"], [0]

    def room(*shape):
        n = int(np.prod(shape))
        ap = scratch[:, used[0]:used[0] + n]
        used[0] += n
        return ap.rearrange("p (a b) -> p a b", b=shape[1]) if len(shape) == 2 else ap

    over, past = room(E, NT), room(MAXT, E)
    counts, spare, last, tile, expert, skip = room(E), room(E), room(1), room(MAXT), room(MAXT), room(MAXT)
    need, ends, table, rows, small_i, tails = (r[n] for n in "need ends table rows small_i tails".split())
    counts_ps, group_step = m.sem(tag + "counts_ps"), m.sem(tag + "group_step")
    NTAILS, NGROUP = 2, 14
    wide = lambda ap, k: ap.unsqueeze(2).to_broadcast([P, E, k])
    rep = lambda ap, k: ap.unsqueeze(1).to_broadcast([P, k, E])

    def pe_group(pe):
        pe.wait_ge(R["cum_done"], after(2 * NS))
        pe_wait_bank(pe)
        pe.matmul(bank[:, 0:E], c["ones"][:, :], r["cum"][:, 0, :], start=True, stop=True).then_inc(counts_ps, 1)

    def dve_group(v):
        n = [0]

        def step(instruction):
            n[0] += 1
            instruction.then_inc(group_step, 1)
            v.wait_ge(group_step, n[0])

        v.wait_ge(counts_ps, 1)
        step(v.tensor_copy(counts, bank[:, 0:E]))
        step(v.tensor_tensor(tails[:, :], counts[0:1, :], c["room"][0:1, :], ALU.add))
        assert n[0] == NTAILS
        step(v.tensor_tensor(over, wide(counts, NT), c["thresh"][:, :].unsqueeze(1).to_broadcast([P, E, NT]), ALU.is_gt))
        step(v.tensor_reduce(need[:, :], over, AX.X, ALU.add))
        step(v.tensor_tensor_scan(ends[:, :], c["ones"][:, 0:E], need[:, :], 0.0, ALU.mult, ALU.add))
        step(v.tensor_scalar(spare, need[:, :], -1.0, float(ROOM), ALU.mult, ALU.add))
        step(v.tensor_scalar(last, ends[:, E - 1:E], -1.0, None, ALU.add))
        step(v.tensor_scalar(tile, c["tile_no"][:, :], last, None, ALU.min))
        step(v.tensor_tensor(past, tile.unsqueeze(2).to_broadcast([P, MAXT, E]), rep(ends[:, :], MAXT), ALU.is_ge))
        step(v.tensor_reduce(expert, past, AX.X, ALU.add))
        step(v.tensor_tensor(past, past, rep(spare, MAXT), ALU.mult))
        step(v.tensor_reduce(skip, past, AX.X, ALU.add))
        v.tensor_copy(table[:, :], expert[0:1, :])
        v.tensor_copy(small_i[:, 0:1], ends[0:1, E - 1:E])
        v.tensor_copy(small_i[:, 2:3], last[0:1, :])
        step(v.tensor_tensor(rows[:, :], skip[0:1, :], tile[0:1, :], ALU.add))
        step(v.tensor_scalar(small_i[:, 1:2], ends[0:1, E - 1:E], 16.0, float(START), ALU.mult, ALU.add))
        assert n[0] == NGROUP, n[0]

    def fill_tails(q, first):
        q.wait_ge(group_step, NTAILS)
        for e in range(first, E, 2):
            tail = q.value_load(tails[0:1, e:e + 1], min_val=e * ROOM * P, max_val=e * ROOM * P + TOKENS)
            q.dma_start(slots_in[bass.ds(tail, P), :], c["zeros"][:, :]).then_inc(r["tails_zeroed"][tag], 16)

    return pe_group, dve_group, fill_tails


def mamba_phase(nc, a, c, w, x, r, slots_in, x_loaded, load_router, load_experts, later_loop_sems):
    ident, tri_le, tri_gt, ones = c["ident"], c["tri_le"], c["tri_gt"], c["ones"]
    with ExitStack() as ctx:
        m = Phase(nc, ctx)
        sb, sem = m.sb, m.sem
        b = m.banks("mb")
        winT = sb("winT", [P, KD, DPROJ])
        woutT = sb("woutT", [P, KI, D])
        conv_w, conv_b = sb("conv_w", [P, CB, TAPS]), sb("conv_b", [P, CB])
        norm_w = sb("norm_w", [P, KI])
        dt_bias, neg_a, d_skip = sb("dt_bias", [P, NH]), sb("neg_a", [P, NH]), sb("d_skip", [P, NH])
        stats, mv, rstd = sb("stats", [P, 2, 6]), sb("mv", [P, 2, 2]), sb("rstd", [P, 2, 1])
        veps = sb("veps", [P, 2, 1])
        xn = sb("xn", [P, 2, D])
        xnT = [sb(f"xnT{q}", [P, KD, ST]) for q in range(2)]
        xpre = sb("xpre", [P, CB, TAPS - 1 + ST])
        h, th = sb("h", [P, CB, ST]), sb("th", [P, 2, 2, ST])
        xc_both = sb("xc", [P, 2, CB, ST])
        xc = [xc_both[:, q, :, :] for q in range(2)]
        dtw = sb("dtw", [P, 8, 2 * NH])
        dt = [sb(f"dt{q}", [P, 2 * NH]) for q in range(2)]
        dA = sb("dA", [P, 2 * NH])
        decay = [sb(f"decay{q}", [P, 2, 2 * NH]) for q in range(2)]
        dA_tri = [sb(f"dA_tri{k}", [P, NH, P]) for k in range(2)]
        L, M = sb("L", [P, NH, P]), sb("M", [P, NH, P])
        cbm, bt = sb("cbm", [P, P]), sb("bt", [P, P])
        xt, xdt, xw, xD = (sb(n, [P, DI]) for n in ("xt", "xdt", "xw", "xD"))
        state = sb("state", [P, DI])
        zs, y, yg = (sb(n, [P, DI]) for n in ("zs", "y", "yg"))
        squares = sb("squares", [P, DI], mybir.dt.bfloat16)
        ygT = sb("ygT", [P, KI, P])
        ms, mse, rs = sb("ms", [P, 1]), sb("mse", [P, 1]), sb("rs", [P, 1])
        win_raw = xc_both[:, :, :, :].rearrange("p q b t -> p (q b t)")[:, 0:11 * D].rearrange("p (r d) -> p r d", d=D)
        wout_raw = L[:, :, :].rearrange("p h t -> p (h t)")[:, 0:2 * DI].rearrange("p (r i) -> p r i", i=DI)

        win_loaded = [sem(f"win_loaded{k}") for k in range(3)]
        win_ps, win_done = sem("win_ps"), sem("win_done")
        wout_loaded, wout_ps, wout_done = sem("wout_loaded"), sem("wout_ps"), sem("wout_done")
        par_loaded, par_done, waits_passed = sem("par_loaded"), sem("par_done"), sem("waits_passed")
        (stats_done, mv_done, veps_done, rstd_done, xn_done, xnT_ps, xnT_done, xbc_ps, xpre_done, tap0_done, conv_step,
         halo_done, tanh_done, xc_done, dt_ps, dt_exp_done, dt_step, tri_done, small_ps,
         decay_done) = (m.loop_sem("a_" + n) for n in (
             "stats_done mv_done veps_done rstd_done xn_done xnT_ps xnT_done xbc_ps xpre_done tap0_done conv_step "
             "halo_done tanh_done xc_done dt_ps dt_exp_done dt_step tri_done small_ps decay_done").split())
        (xt_ps, cb_ps, D_ps, xt_done, bt_done, cbm_done, L_done, M_done, xdt_done, xw_done, xD_done, sdec_done,
         yoff_ps, z_ps, tz_done, zs_done, yd_ps, st_ps, S_done, y1_done, y2_done, y3_done, yg_done, sq_done, mse_done,
         rs_done, ygT_ps, ygT_done, out_ps, x_done) = (m.loop_sem("b_" + n) for n in (
             "xt_ps cb_ps D_ps xt_done bt_done cbm_done L_done M_done xdt_done xw_done xD_done sdec_done "
             "yoff_ps z_ps tz_done zs_done yd_ps st_ps S_done y1_done y2_done y3_done yg_done sq_done mse_done "
             "rs_done ygT_ps ygT_done out_ps x_done").split())
        NDT = 13
        R = router_stage(
            m, c, w, x, r, slots_in, "ra_", b[0], last_rows=xn, last_rows_free=lambda v: v.wait_ge(xnT_ps, after(NS)),
            x_wait=lambda v, s: v.wait_ge(x_done, at(s, 2)),
            pe_wait_x=lambda pe, s: pe.wait_ge(x_done, at(s, 2) if isinstance(s, int) and s == NS - 1 else at(s, 2, 3)),
            pe_wait_rank=lambda pe, s: pe.wait_ge(*(
                (x_done, at(s, 2) if s == NS - 1 else at(s, 2, 4)) if isinstance(s, int) and s > NS - 4 else
                (xnT_done, after(s + 4)))))

        pe_group, dve_group, fill_tails = group_stage(m, c, r, R, slots_in, "ra_", b[1],
                                                      lambda pe: pe.wait_ge(tap0_done, after(3 * NS)))

        def heads(ap, n):
            return ap.unsqueeze(2).to_broadcast([P, NH, n])

        def pe_setup(pe):
            for g, (r0, r1) in enumerate(((0, 4), (4, 8), (8, 11))):
                pe.wait_ge(win_loaded[g], 16 * (1 + (g == 2)))
                for k in range(KD):
                    for r in range(r0, r1):
                        n = min(P, DPROJ - r * P)
                        t = pe.transpose(b[1 + 2 * g + k][:, (r - r0) * P:(r - r0) * P + n],
                                         win_raw[0:n, r, k * P:(k + 1) * P], ident[0:n, 0:n])
                    t.then_inc(win_ps, 1)
            pe.wait_ge(wout_loaded, 16)
            for g, bank in enumerate((b[0], b[7])):
                for i in range(2):
                    for r in range(2):
                        ib = 2 * g + i
                        t = pe.transpose(bank[:, (2 * i + r) * P:(2 * i + r + 1) * P],
                                         wout_raw[:, r, ib * P:(ib + 1) * P], ident[:, :])
                t.then_inc(wout_ps, 1)
            pe.wait_ge(win_done, 6)
            pe.wait_ge(wout_done, 4)

        def pe_A1(pe, s, q):
            pe.wait_ge(x_done, after(2 * s - 2))
            pe.wait_ge(R["ranks_read"], R["ranks_read_after"](s - 3))
            pe.wait_ge(xn_done, at(s, 2))
            for t in range(2):
                for k in range(KD):
                    last = pe.transpose(b[0][:, k * ST + t * P:k * ST + (t + 1) * P], xn[:, t, k * P:(k + 1) * P],
                                        ident[:, :])
            last.then_inc(xnT_ps, 1)

        def pe_xbc(pe, s, q, g):
            if g == 0:
                pe.wait_ge(xnT_done, at(s, 1))
                pe.wait_ge(tap0_done, at(s, 3, 0))
            elif g == 1:
                pe.wait_ge(decay_done, after(s))
            else:
                pe.wait_ge(tap0_done, at(s, 3, 1))
            bank = b[1 + g % 2]
            for j in range(2):
                col = XBC0 + (2 * g + j) * P
                for k in range(KD):
                    last = pe.matmul(bank[:, j * ST:(j + 1) * ST], winT[:, k, col:col + P], xnT[q][:, k, :],
                                     start=(k == 0), stop=(k == KD - 1))
            last.then_inc(xbc_ps, 1)

        def pe_dt(pe, s, q):
            pe.wait_ge(tap0_done, at(s, 3, 2))
            for t in range(2):
                for k in range(KD):
                    last = pe.matmul(b[2][:, t * NH:(t + 1) * NH], xnT[q][:, k, t * P:(t + 1) * P],
                                     winT[:, k, DT0:DPROJ], start=(k == 0), stop=(k == KD - 1))
            last.then_inc(dt_ps, 1)

        def pe_small(pe, s, q):
            pe.wait_ge(dt_step, at(s, NDT))
            pe.matmul(b[2][:, 32:48], tri_le[:, :], dA[:, :], start=True, stop=True)
            pe.matmul(b[2][:, 48:64], ones[:, :], dA[:, :], start=True, stop=True).then_inc(small_ps, 1)

        def pe_xt(pe, s, q, t):
            g = 2 * s + t
            pe.wait_ge(xc_done, at(s, 3, 2))
            pe.wait_ge(zs_done, after(g))
            for k in range(KI):
                last = pe.transpose(b[5][:, k * P:(k + 1) * P], xc[q][:, k, t * P:(t + 1) * P], ident[:, :])
            last.then_inc(xt_ps, 1)

        def pe_D(pe, s, q, t):
            g = 2 * s + t
            pe.wait_ge(tri_done, after(g + 1))
            pe.wait_ge(y2_done, after(g))
            for k in range(2):
                if k:
                    pe.wait_ge(S_done, after(g + 1))
                last = pe.matmul(b[3 + k][:, :], tri_gt[:, :], dA_tri[t][:, 4 * k:4 * k + 4, :].rearrange("p h t -> p (h t)"),
                                 start=True, stop=True)
            last.then_inc(D_ps, 1)

        def pe_yoff(pe, s, q, t):
            g = 2 * s + t
            pe.wait_ge(xc_done, at(s, 3))
            pe.wait_ge(S_done, after(g + 1))
            pe.wait_ge(y1_done, after(g))
            pe.matmul(b[7][:, :], xc[q][:, KI + 1, t * P:(t + 1) * P], state[:, :], start=True,
                      stop=True).then_inc(yoff_ps, 1)

        def pe_cb(pe, s, q, t):
            g = 2 * s + t
            pe.wait_ge(xc_done, at(s, 3))
            pe.wait_ge(ygT_done, after(g))
            pe.transpose(b[6][:, 0:P], xc[q][:, KI, t * P:(t + 1) * P], ident[:, :])
            pe.matmul(b[6][:, P:2 * P], xc[q][:, KI, t * P:(t + 1) * P], xc[q][:, KI + 1, t * P:(t + 1) * P],
                      start=True, stop=True).then_inc(cb_ps, 1)

        def pe_z(pe, s, q, t):
            g = 2 * s + t
            pe.wait_ge(xt_done, after(g + 1))
            for k in range(KD):
                last = pe.matmul(b[5][:, :], xnT[q][:, k, t * P:(t + 1) * P], winT[:, k, 0:DI],
                                 start=(k == 0), stop=(k == KD - 1))
            last.then_inc(z_ps, 1)

        def pe_sums(pe, s, q, t):
            g = 2 * s + t
            pe.wait_ge(M_done, after(g + 1))
            pe.wait_ge(xdt_done, after(g + 1))
            for hd in range(NH):
                last = pe.matmul(b[3][:, hd * DH:(hd + 1) * DH], M[:, hd, :], xdt[:, hd * DH:(hd + 1) * DH],
                                 start=True, stop=True)
            last.then_inc(yd_ps, 1)
            pe.wait_ge(xw_done, after(g + 1))
            pe.wait_ge(bt_done, after(g + 1))
            pe.matmul(b[4][:, :], bt[:, :], xw[:, :], start=True, stop=True).then_inc(st_ps, 1)

        def pe_ygT(pe, s, t):
            g = 2 * s + t
            pe.wait_ge(yg_done, after(g + 1))
            pe.wait_ge(cbm_done, after(g + 1))
            for k in range(KI):
                last = pe.transpose(b[6][:, k * P:(k + 1) * P], yg[:, k * P:(k + 1) * P], ident[:, :])
            last.then_inc(ygT_ps, 1)

        def pe_out(pe, s, t):
            g = 2 * s + t
            pe.wait_ge(ygT_done, after(g + 1))
            if t == 0:
                pe.wait_ge(R["ranks_read"], R["ranks_read_after"](s - 1))
                if not (isinstance(s, int) and s == NS - 1):
                    pe.wait_ge(xnT_done, after(s + 2))
            else:
                pe.wait_ge(x_done, after(g))
                pe.wait_ge(R["logits_read"], after(s))
            for k in range(KI):
                last = pe.matmul(b[0][:, t * D:(t + 1) * D], ygT[:, k, :], woutT[:, k, :], start=(k == 0),
                                 stop=(k == KI - 1))
            last.then_inc(out_ps, 1)

        def pe_tile(pe, s, q, t, first=False, between=lambda: None):
            before = (s, 0) if t else (s - 1, 1)
            if t == 0:
                pe_D(pe, s, q, t)
                pe_small(pe, s, q)
                pe_xt(pe, s, q, t)
            else:
                pe_xt(pe, s, q, t)
                pe_D(pe, s, q, t)
            if not first:
                pe_ygT(pe, *before)
            pe_z(pe, s, q, t)
            if t:
                pe_cb(pe, s, q, t)
            if not first:
                pe_out(pe, *before)
            if t == 0:
                pe_cb(pe, s, q, t)
            between()
            pe_yoff(pe, s, q, t)

        def pe_body(pe, s, q, ahead=True, behind=2):
            n, nq = s + 1, 1 - q
            R1, R2, R3 = R["pe"]
            pe_tile(pe, s, q, 0, first=not behind, between=(lambda: pe_A1(pe, n, nq)) if ahead else lambda: None)
            if ahead:
                pe_xbc(pe, n, nq, 0)
            if behind > 1:
                R3(pe, s - 2)
            if ahead:
                pe_xbc(pe, n, nq, 1)
                pe_xbc(pe, n, nq, 2)
            pe_sums(pe, s, q, 0)
            if ahead:
                pe_dt(pe, n, nq)
            pe_tile(pe, s, q, 1)
            if behind:
                R1(pe, s - 1)
            pe_sums(pe, s, q, 1)
            if behind:
                R2(pe, s - 1)

        def pe_end(pe):
            pe_ygT(pe, NS - 1, 1)
            pe_out(pe, NS - 1, 1)
            R["pe"][2](pe, NS - 2)
            for piece in R["pe"]:
                piece(pe, NS - 1)
            pe_group(pe)

        def act_setup(act):
            act.wait_ge(par_loaded, 16 * 6)
            act.activation(neg_a[:, :], neg_a[:, :], ACT.Exp).then_inc(par_done, 1)
            for i in (0, 2, 4):
                act.wait_ge(win_ps, i + 1)
                act_copy_win(act, i)
            for g in range(2):
                act.wait_ge(wout_ps, g + 1)
                act.wait_ge(par_done, 2)
                for i in range(2):
                    act.activation(woutT[:, 2 * g + i, :], (b[0], b[7])[g][:, i * D:(i + 1) * D], ACT.Copy,
                                   scale=norm_w[:, 2 * g + i:2 * g + i + 1]).then_inc(wout_done, 1)

        def win_group(i):
            g, k = i // 2, i % 2
            n = (4 * P, 4 * P, DPROJ - 8 * P)[g]
            return winT[:, k, g * 4 * P:g * 4 * P + n], b[1 + i][:, 0:n]

        def act_copy_win(act, i):
            act.activation(*win_group(i), ACT.Copy).then_inc(win_done, 1)

        def act_A1(act, s, q):
            act.wait_ge(xnT_ps, at(s, 1))
            act.wait_ge(z_ps, after(2 * s - 2))
            act.activation(xnT[q][:, :, :].rearrange("p k t -> p (k t)"), b[0][:, :], ACT.Copy).then_inc(xnT_done, 1)

        def act_xbc(act, s, q, g):
            act.wait_ge(xbc_ps, at(s, 3, g + 1))
            act.wait_ge(halo_done, at(s, 3, g + 1))
            act.wait_ge(xc_done, at(s, 3, 0))
            bank = b[1 + g % 2][:, :].rearrange("p (j t) -> p j t", j=2)
            blk = 2 * g
            act.activation(xpre[:, blk:blk + 2, TAPS - 1:], bank, ACT.Copy).then_inc(xpre_done, 1)
            for j in range(2):
                i = act.activation(h[:, blk + j, :], bank[:, j, :], ACT.Identity,
                                   scale=conv_w[:, blk + j, TAPS - 1:TAPS], bias=conv_b[:, blk + j:blk + j + 1])
            i.then_inc(tap0_done, 1)

        def act_tanh(act, s, q, g):
            blk = 2 * g
            act.wait_ge(conv_step, at(s, 18, 6 * g + 6))
            act.wait_ge(xc_done, at(s, 3, g - 1) if g else after(3 * s))
            act.activation(th[:, g % 2, :, :], h[:, blk:blk + 2, :], ACT.Tanh).then_inc(tanh_done, 1)

        def act_dt(act, s, q):
            act.wait_ge(dt_step, at(s, NDT, 2))
            act.activation(dtw[:, 2, :], dtw[:, 1, :], ACT.Exp).then_inc(dt_exp_done, 1)

        def act_decay(act, s, q):
            act.wait_ge(small_ps, at(s, 1))
            act.wait_ge(y1_done, after(2 * s - 2))
            act.wait_ge(sdec_done, after(2 * s - 2))
            act.activation(decay[q][:, :, :].rearrange("p a b -> p (a b)"), b[2][:, 32:64], ACT.Exp).then_inc(
                decay_done, 1)

        def act_xt(act, s, q, t):
            g = 2 * s + t
            act.wait_ge(xt_ps, after(g + 1))
            act.wait_ge(xdt_done, after(g))
            act.wait_ge(xD_done, after(g))
            act.activation(xt[:, :], b[5][:, :], ACT.Copy).then_inc(xt_done, 1)

        def act_L(act, s, q, t):
            g = 2 * s + t
            act.wait_ge(D_ps, after(g + 1))
            act.wait_ge(M_done, after(g))
            act.wait_ge(xw_done, after(g))
            for k in range(2):
                i = act.activation(L[:, 4 * k:4 * k + 4, :].rearrange("p h t -> p (h t)"), b[3 + k][:, :], ACT.Exp)
            i.then_inc(L_done, 1)

        def act_bt(act, s, q, t):
            g = 2 * s + t
            act.wait_ge(cb_ps, after(g + 1))
            act.wait_ge(st_ps, after(g))
            act.activation(bt[:, :], b[6][:, 0:P], ACT.Copy).then_inc(bt_done, 1)

        def act_z(act, s, q, t):
            g = 2 * s + t
            act.wait_ge(z_ps, after(g + 1))
            act.wait_ge(yg_done, after(g))
            act.activation(zs[:, :], b[5][:, :], ACT.Tanh, scale=0.5).then_inc(tz_done, 1)

        def act_sq(act, s, t):
            g = 2 * s + t
            act.wait_ge(yg_done, after(g + 1))
            act.wait_ge(mse_done, after(g))
            act.activation(squares[:, :], yg[:, :], ACT.Square, scale=0.5 * DI ** -0.5, accum_out=ms[:, :]).then_inc(
                sq_done, 1)

        def act_ygT(act, s, t):
            g = 2 * s + t
            act.wait_ge(ygT_ps, after(g + 1))
            act.wait_ge(out_ps, after(g))
            act.activation(ygT[:, :, :].rearrange("p k t -> p (k t)"), b[6][:, :], ACT.Copy).then_inc(ygT_done, 1)

        def act_body(act, s, q, ahead=True, behind=2):
            n, nq = s + 1, 1 - q
            R1, R2 = R["act"]
            act_L(act, s, q, 0)
            act_decay(act, s, q)
            act_xt(act, s, q, 0)
            if behind:
                act_ygT(act, s - 1, 1)
            act_tanh(act, s, q, 2)
            if behind:
                act_sq(act, s - 1, 1)
            act_z(act, s, q, 0)
            act_bt(act, s, q, 0)
            if ahead:
                act_A1(act, n, nq)
                for g in range(3):
                    act_xbc(act, n, nq, g)
            act_xt(act, s, q, 1)
            if ahead:
                act_dt(act, n, nq)
            act_L(act, s, q, 1)
            act_ygT(act, s, 0)
            if ahead:
                act_tanh(act, n, nq, 0)
            act_bt(act, s, q, 1)
            act_sq(act, s, 0)
            act_z(act, s, q, 1)
            if behind:
                R1(act, s - 1)
            if ahead:
                act_tanh(act, n, nq, 1)
            if behind:
                R2(act, s - 1)

        def act_end(act):
            act_ygT(act, NS - 1, 1)
            act_sq(act, NS - 1, 1)
            for piece in R["act"]:
                piece(act, NS - 1)
            fill_tails(act, 1)

        def dve_setup(v):
            v.memset(state[:, :], 0.0).then_inc(S_done, 1)
            v.memset(r["prob"][:, NT:NT + 2], 0.0)
            v.memset(r["pos_i"][:, NT:NT + 2], 0)
            v.memset(xpre[:, :, 0:TAPS - 1], 0.0).then_inc(halo_done, 3)
            v.wait_ge(par_loaded, 16 * 6)
            v.tensor_scalar(conv_w[:, :, :], conv_w[:, :, :], 0.5, None, ALU.mult)
            v.tensor_scalar(conv_b[:, :], conv_b[:, :], 0.5, None, ALU.mult)
            v.tensor_scalar(norm_w[:, :], norm_w[:, :], 0.5, None, ALU.mult).then_inc(par_done, 1)
            v.wait_ge(par_done, 2)
            v.tensor_scalar(neg_a[:, :], neg_a[:, :], -1.0, None, ALU.mult).then_inc(par_done, 1)
            for i in (1, 3, 5):
                v.wait_ge(win_ps, i + 1)
                v.tensor_copy(*win_group(i)).then_inc(win_done, 1)
            v.wait_ge(par_done, 3)

        def dve_stats(v, s, q):
            wait_apart(v, waits_passed, rstd_done, after(s))
            for t in range(2):
                v.bn_stats(stats[:, t, :], x[:, bass.ds(2 * s + t, 1), :].rearrange("p a d -> p (a d)")).then_inc(
                    stats_done, 1)
            for t in range(2):
                wait_apart(v, waits_passed, stats_done, at(s, 2, t + 1))
                v.bn_aggr(mv[:, t, :], stats[:, t, :]).then_inc(mv_done, 1)

        def dve_xn(v, s, q):
            v.wait_ge(rstd_done, after(s + 1))
            v.wait_ge(xnT_ps, after(s))
            for t in range(2):
                v.tensor_scalar(xn[:, t, :], x[:, bass.ds(2 * s + t, 1), :].rearrange("p a d -> p (a d)"),
                                mv[:, t, 0:1], rstd[:, t, :], ALU.subtract, ALU.mult).then_inc(xn_done, 1)

        def dve_conv(v, s, q, g):
            v.wait_ge(tap0_done, at(s, 3, g + 1))
            for n, tap in enumerate((2, 1, 0)):
                for j in range(2):
                    if n:
                        v.wait_ge(conv_step, at(s, 18, 6 * g + 2 * n + j - 1))
                    blk = 2 * g + j
                    v.scalar_tensor_tensor(out=h[:, blk, :], in0=xpre[:, blk, tap:tap + ST], scalar=conv_w[:, blk, tap:tap + 1],
                                           in1=h[:, blk, :], op0=ALU.mult, op1=ALU.add).then_inc(conv_step, 1)
            v.wait_ge(conv_step, at(s, 18, 6 * g + 6))
            blk = 2 * g
            v.tensor_copy(xpre[:, blk:blk + 2, 0:TAPS - 1], xpre[:, blk:blk + 2, ST:ST + TAPS - 1]).then_inc(
                halo_done, 1)

        def dve_silu(v, s, q, g):
            blk = 2 * g
            v.wait_ge(tanh_done, at(s, 3, g + 1))
            v.wait_ge(yoff_ps, after(2 * s - 2))
            v.scalar_tensor_tensor(out=xc[q][:, blk:blk + 2, :], in0=th[:, g % 2, :, :], scalar=1.0,
                                   in1=h[:, blk:blk + 2, :], op0=ALU.add, op1=ALU.mult).then_inc(xc_done, 1)

        def dve_dt(v, s, q):
            vv, nv, e, den, r, z, z2, p = (dtw[:, i, :] for i in range(8))
            k = [0]

            def step(instruction):
                k[0] += 1
                instruction.then_inc(dt_step, 1)
                v.wait_ge(dt_step, at(s, NDT, k[0]))

            v.wait_ge(dt_ps, at(s, 1))
            two = lambda ap: ap.unsqueeze(1).to_broadcast([P, 2, NH])
            split = lambda ap: ap.rearrange("p (a b) -> p a b", a=2)
            step(v.tensor_tensor(split(vv), split(b[2][:, 0:2 * NH]), two(dt_bias[:, :]), ALU.add))
            step(v.scalar_tensor_tensor(out=nv, in0=vv, scalar=-1.0, in1=vv, op0=ALU.mult, op1=ALU.min))
            v.wait_ge(dt_exp_done, at(s, 1))
            step(v.tensor_scalar(den, e, 2.0, None, ALU.add))
            step(v.reciprocal(r, den))
            step(v.tensor_tensor(z, e, r, ALU.mult))
            step(v.tensor_tensor(z2, z, z, ALU.mult))
            step(v.tensor_scalar(p, z2, ATANH[4], ATANH[3], ALU.mult, ALU.add))
            step(v.scalar_tensor_tensor(out=p, in0=p, scalar=0.0, in1=z2, op0=ALU.add, op1=ALU.mult))
            step(v.scalar_tensor_tensor(out=p, in0=p, scalar=ATANH[2], in1=z2, op0=ALU.add, op1=ALU.mult))
            step(v.scalar_tensor_tensor(out=p, in0=p, scalar=ATANH[1], in1=z2, op0=ALU.add, op1=ALU.mult))
            step(v.scalar_tensor_tensor(out=p, in0=p, scalar=ATANH[0], in1=z, op0=ALU.add, op1=ALU.mult))
            v.wait_ge(xdt_done, after(2 * s - 2))
            step(v.scalar_tensor_tensor(out=dt[q][:, :], in0=vv, scalar=0.0, in1=p, op0=ALU.max, op1=ALU.add))
            v.wait_ge(small_ps, after(s))
            v.wait_ge(tri_done, after(2 * s))
            step(v.tensor_tensor(split(dA[:, :]), split(dt[q][:, :]), two(neg_a[:, :]), ALU.mult))

        def dve_cbm(v, s, q, t):
            g = 2 * s + t
            v.wait_ge(bt_done, after(g + 1))
            v.tensor_tensor(cbm[:, :], b[6][:, P:2 * P], tri_le[:, :], ALU.mult).then_inc(cbm_done, 1)

        def dve_M(v, s, q, t):
            g = 2 * s + t
            v.wait_ge(L_done, after(g + 1))
            v.wait_ge(cbm_done, after(g + 1))
            v.wait_ge(yd_ps, after(g))
            v.tensor_tensor(M[:, :, :], L[:, :, :], cbm[:, :].unsqueeze(1).to_broadcast([P, NH, P]),
                            ALU.mult).then_inc(M_done, 1)

        def dve_z(v, s, q, t):
            g = 2 * s + t
            v.wait_ge(tz_done, after(g + 1))
            v.scalar_tensor_tensor(out=zs[:, :], in0=zs[:, :], scalar=1.0, in1=b[5][:, :], op0=ALU.add,
                                   op1=ALU.mult).then_inc(zs_done, 1)

        def dve_y1(v, s, q, t):
            g = 2 * s + t
            byhead = lambda ap: ap.rearrange("p (h d) -> p h d", h=NH)
            v.wait_ge(yoff_ps, after(g + 1))
            v.wait_ge(decay_done, after(s + 1))
            v.tensor_tensor(byhead(y[:, :]), byhead(b[7][:, :]), heads(decay[q][:, 0, t * NH:(t + 1) * NH], DH),
                            ALU.mult).then_inc(y1_done, 1)

        def dve_y(v, s, t):
            g = 2 * s + t
            v.wait_ge(yd_ps, after(g + 1))
            v.wait_ge(y3_done, after(g + 1))
            v.tensor_tensor(y[:, :], y[:, :], b[3][:, :], ALU.add).then_inc(y2_done, 1)
            v.wait_ge(st_ps, after(g + 1))
            v.wait_ge(sdec_done, after(g + 1))
            v.tensor_tensor(state[:, :], state[:, :], b[4][:, :], ALU.add).then_inc(S_done, 1)
            v.wait_ge(y2_done, after(g + 1))
            v.wait_ge(zs_done, after(g + 1))
            v.wait_ge(sq_done, after(g))
            v.wait_ge(ygT_ps, after(g))
            v.tensor_tensor(yg[:, :], y[:, :], zs[:, :], ALU.mult).then_inc(yg_done, 1)

        def dve_x(v, s, t):
            g = 2 * s + t
            v.wait_ge(out_ps, after(g + 1))
            v.wait_ge(rs_done, after(g + 1))
            xs = x[:, bass.ds(g, 1), :].rearrange("p a d -> p (a d)")
            v.scalar_tensor_tensor(out=xs, in0=b[0][:, t * D:(t + 1) * D], scalar=rs[:, :], in1=xs, op0=ALU.mult,
                                   op1=ALU.add).then_inc(x_done, 1)

        def dve_body(v, s, q, ahead=True, behind=2):
            n, nq = s + 1, 1 - q
            R0, R1, R2, R3 = R["dve"]
            if ahead:
                dve_stats(v, n, nq)
            dve_silu(v, s, q, 2)
            if ahead:
                dve_xn(v, n, nq)
            if behind:
                dve_x(v, s - 1, 1)
            if behind > 1:
                R2(v, s - 2)
            dve_cbm(v, s, q, 0)
            dve_M(v, s, q, 0)
            dve_z(v, s, q, 0)
            dve_y1(v, s, q, 0)
            if behind:
                R0(v, s - 1)
            if behind > 1:
                R3(v, s - 2)
            if ahead:
                dve_conv(v, n, nq, 0)
            dve_y(v, s, 0)
            if ahead:
                dve_dt(v, n, nq)
            if behind:
                R1(v, s - 1)
            dve_cbm(v, s, q, 1)
            dve_M(v, s, q, 1)
            dve_x(v, s, 0)
            dve_z(v, s, q, 1)
            dve_y1(v, s, q, 1)
            if ahead:
                dve_conv(v, n, nq, 1)
            dve_y(v, s, 1)
            if ahead:
                dve_silu(v, n, nq, 0)
                dve_silu(v, n, nq, 1)
                dve_conv(v, n, nq, 2)

        def dve_end(v):
            R0, R1, R2, R3 = R["dve"]
            R2(v, NS - 2)
            dve_x(v, NS - 1, 1)
            R0(v, NS - 1)
            R3(v, NS - 2)
            for piece in (R1, R2, R3):
                piece(v, NS - 1)
            dve_group(v)

        def pool_A1(g_, s, q):
            g_.wait_ge(mv_done, at(s, 2))
            g_.tensor_tensor(veps[:, :, :], mv[:, :, 1:2], c["eps"][:, :].unsqueeze(2), ALU.add).then_inc(veps_done, 1)
            g_.wait_ge(veps_done, after(s + 1))
            g_.wait_ge(xn_done, after(2 * s))
            g_.tensor_tensor(rstd[:, :, :], veps[:, :, :], c["half_neg"][:, :].unsqueeze(2), ALU.pow).then_inc(
                rstd_done, 1)

        def pool_tri(g_, s, q, tiles=(0, 1)):
            g_.wait_ge(dt_step, at(s, NDT))
            for t in tiles:
                g_.wait_ge(D_ps, after(2 * s - 1 + t))
                g_.tensor_tensor(dA_tri[t][:, :, :], tri_le[:, :].unsqueeze(1).to_broadcast([P, NH, P]),
                                 heads(dA[:, t * NH:(t + 1) * NH], P), ALU.mult).then_inc(tri_done, 1)

        def pool_tile(g_, s, q, t):
            g = 2 * s + t
            byhead = lambda ap: ap.rearrange("p (h d) -> p h d", h=NH)
            g_.wait_ge(L_done, after(g + 1))
            g_.wait_ge(xdt_done, after(g + 1))
            g_.wait_ge(st_ps, after(g))
            g_.tensor_tensor(byhead(xw[:, :]), byhead(xdt[:, :]), L[:, :, P - 1:P].to_broadcast([P, NH, DH]),
                             ALU.mult).then_inc(xw_done, 1)
            g_.wait_ge(S_done, after(g + 1))
            g_.wait_ge(yoff_ps, after(g + 1))
            g_.wait_ge(decay_done, after(s + 1))
            g_.tensor_tensor(byhead(state[:, :]), byhead(state[:, :]), heads(decay[q][:, 1, t * NH:(t + 1) * NH], DH),
                             ALU.mult).then_inc(sdec_done, 1)
            g_.wait_ge(xD_done, after(g + 1))
            g_.wait_ge(y1_done, after(g + 1))
            g_.tensor_tensor(y[:, :], y[:, :], xD[:, :], ALU.add).then_inc(y3_done, 1)

        def pool_xdt(g_, s, q, t):
            g = 2 * s + t
            byhead = lambda ap: ap.rearrange("p (h d) -> p h d", h=NH)
            g_.wait_ge(xt_done, after(g + 1))
            g_.wait_ge(dt_step, at(s, NDT))
            g_.wait_ge(yd_ps, after(g))
            g_.tensor_tensor(byhead(xdt[:, :]), byhead(xt[:, :]), heads(dt[q][:, t * NH:(t + 1) * NH], DH),
                             ALU.mult).then_inc(xdt_done, 1)
            g_.wait_ge(y3_done, after(g))
            g_.tensor_tensor(byhead(xD[:, :]), byhead(xt[:, :]), heads(d_skip[:, :], DH), ALU.mult).then_inc(
                xD_done, 1)

        def pool_rs(g_, s, t):
            g = 2 * s + t
            g_.wait_ge(sq_done, after(g + 1))
            g_.tensor_tensor(mse[:, :], ms[:, :], c["eps"][:, 0:1], ALU.add).then_inc(mse_done, 1)
            g_.wait_ge(mse_done, after(g + 1))
            g_.wait_ge(x_done, after(g))
            g_.tensor_tensor(rs[:, :], mse[:, :], c["half_neg"][:, 0:1], ALU.pow).then_inc(rs_done, 1)

        def pool_body(g_, s, q, ahead=True, behind=2):
            n, nq = s + 1, 1 - q
            R0, R2, R3, R4 = R["pool"]
            if ahead:
                pool_A1(g_, n, nq)
            if behind:
                pool_rs(g_, s - 1, 1)
            pool_xdt(g_, s, q, 0)
            if behind > 1:
                R2(g_, s - 2)
            pool_tile(g_, s, q, 0)
            if behind:
                R0(g_, s - 1)
            if behind > 1:
                R3(g_, s - 2)
            pool_xdt(g_, s, q, 1)
            if behind > 1:
                R4(g_, s - 2)
            if ahead:
                pool_tri(g_, n, nq, (0,))
            pool_rs(g_, s, 0)
            pool_tile(g_, s, q, 1)
            if ahead:
                pool_tri(g_, n, nq, (1,))

        def pool_end(g_):
            R0, R2, R3, R4 = R["pool"]
            R2(g_, NS - 2)
            pool_rs(g_, NS - 1, 1)
            R0(g_, NS - 1)
            R3(g_, NS - 2)
            R4(g_, NS - 2)
            for piece in (R2, R3):
                piece(g_, NS - 1)

        def program(e, stage_a, body, end, before_loop=lambda: None):
            for piece in stage_a:
                piece(e, 0, 0)
            before_loop()
            body(e, 0, 0, behind=0)
            body(e, 1, 1, behind=1)
            with e.Fori(1, NS // 2 - 1) as i:
                body(e, 2 * i, 0)
                body(e, 2 * i + 1, 1)
            body(e, NS - 2, 0)
            body(e, NS - 1, 1, ahead=False)
            end(e)

        def group(fn, g):
            return lambda e, s, q: fn(e, s, q, g)

        m.start_loop_sems(later_loop_sems)
        with nc.Block() as block:

            @block.sync
            def _(sp):
                for g, (r0, r1) in ((1, (4, 8)), (2, (8, 10)), (0, (0, 4))):
                    sp.dma_start(win_raw[:, r0:r1, :],
                                 a["W_in"][r0 * P:r1 * P, :].rearrange("(r p) d -> p r d", p=P)).then_inc(win_loaded[g], 16)
                sp.dma_start(win_raw[0:NH, 10, :], a["W_in"][DT0:DPROJ, :]).then_inc(win_loaded[2], 16)
                sp.dma_start(wout_raw, a["W_out"].rearrange("(r p) i -> p r i", p=P)).then_inc(wout_loaded, 16)
                load_router(sp)
                for k in range(3):
                    sp.wait_ge(win_loaded[k], 16 * (1 + (k == 2)))
                sp.wait_ge(wout_loaded, 16)
                for t in range(4):
                    sp.wait_ge(x_loaded[t], 16)
                sp.wait_ge(par_loaded, 16 * 6)
                load_experts(sp)
                fill_tails(sp, 0)

            @block.tensor
            def _(pe):
                pe.wait_ge(c["ready"], 3)
                pe_setup(pe)
                pe.wait_ge(w["loaded"][0], 16)
                program(pe, (pe_A1, group(pe_xbc, 0), group(pe_xbc, 1), group(pe_xbc, 2), pe_dt), pe_body, pe_end)

            @block.scalar
            def _(act):
                act.dma_start(conv_w[:, :, :], a["conv_w"].rearrange("(r p) w -> p r w", p=P)).then_inc(par_loaded, 16)
                for dst, src in ((conv_b, "conv_b"), (norm_w, "norm_w")):
                    act.dma_start(dst[:, :], a[src].rearrange("(r p) -> p r", p=P), allow_slow_non_contiguous=True).then_inc(par_loaded, 16)
                for dst, src in ((dt_bias, "dt_bias"), (neg_a, "A_log"), (d_skip, "Dp")):
                    act.dma_start(dst[:, :], a[src].partition_broadcast(P)).then_inc(par_loaded, 16)
                for t in range(4):
                    act.dma_start(x[:, 4 * t:4 * t + 4, :], a["u"][0, 4 * t * P:(4 * t + 4) * P, :].rearrange(
                        "(r p) d -> p r d", p=P)).then_inc(x_loaded[t], 16)
                act_setup(act)
                act.wait_ge(par_done, 3)
                program(act, (act_A1, group(act_xbc, 0), group(act_xbc, 1), group(act_xbc, 2), group(act_tanh, 0),
                              group(act_tanh, 1), act_dt), act_body, act_end)

            @block.vector
            def _(v):
                dve_setup(v)
                v.wait_ge(c["ready"], 3)
                v.wait_ge(x_loaded[0], 16)

                def rest_of_x():
                    for t in range(1, 4):
                        v.wait_ge(x_loaded[t], 16)
                program(v, (dve_stats, dve_xn, group(dve_conv, 0), group(dve_conv, 1), group(dve_silu, 0), group(dve_silu, 1),
                            dve_dt, group(dve_conv, 2)), dve_body, dve_end, rest_of_x)
                v.wait_ge(R["noted"], after(3 * NS))

            @block.gpsimd
            def _(g_):
                c["fill"](g_)
                g_.wait_ge(par_loaded, 16 * 6)
                program(g_, (pool_A1, pool_tri), pool_body, pool_end)

    return m


class MoeSems:

    def __init__(self, m, tag):
        self.loop_sems = [m.sem(tag + n) for n in (
            "xin_loaded y_stored xT_ps xT_done gu_ps sg_done h_done hT_ps hT_done y_ps y_done").split()]
        self.loose_step, self.waits_passed, self.waits_passed_a, self.waits_passed_g = (
            m.sem(tag + n) for n in "loose_step waits_passed waits_passed_a waits_passed_g".split())


def moe_phase(nc, c, w, slots, slots_zeroed, r, rows_from, tag, sems, load_ahead=None, prepare=None, last=None):
    ident = c["ident"]
    slots_in, slots_out = slots
    with ExitStack() as ctx:
        m = Phase(nc, ctx)
        sb = m.sb
        b = m.banks(tag + "b")
        delta3, first, delta = sb(tag + "delta3", [P, NT, E]), sb(tag + "first", [P, E]), sb(tag + "delta", [P, E])
        pos = sb(tag + "pos", [P, NT])
        table, rows, small_i = r["table"], r["rows"], r["small_i"]
        xin, xT = sb(tag + "xin", [P, D]), sb(tag + "xT", [P, KD, P])
        sg, h, yout = (sb(tag + n, [P, s]) for n, s in (("sg", FI), ("h", FI), ("y", D)))
        hT = sb(tag + "hT", [P, KF, P])

        loose_step, waits_passed, waits_passed_a, waits_passed_g = (
            sems.loose_step, sems.waits_passed, sems.waits_passed_a, sems.waits_passed_g)
        if last:
            last_pool, last_dve, last_sync = last(m)
        xin_loaded, y_stored, xT_ps, xT_done, gu_ps, sg_done, h_done, hT_ps, hT_done, y_ps, y_done = sems.loop_sems

        def dve_rows_out(v):
            n = [0]

            def step(instruction):
                n[0] += 1
                instruction.then_inc(loose_step, 1)
                v.wait_ge(loose_step, n[0])

            step(v.tensor_tensor(first[:, :], r["ends"][:, :], r["need"][:, :], ALU.subtract))
            step(v.scalar_tensor_tensor(out=delta[:, :], in0=first[:, :], scalar=float(P), in1=c["room"][:, :],
                                        op0=ALU.mult, op1=ALU.subtract))
            step(v.tensor_tensor(delta3[:, :, :], r["onehot"][:, :, :], delta[:, :].unsqueeze(1).to_broadcast([P, NT, E]), ALU.mult))
            step(v.tensor_reduce(pos[:, :], delta3[:, :, :], AX.X, ALU.add))
            step(v.tensor_tensor(pos[:, :], pos[:, :], r["pos"][:, 0:NT], ALU.add))
            step(v.tensor_copy(r["pos_i"][:, 0:NT], pos[:, :]))

        def load_count(e):
            return e.value_load(small_i[0:1, 0:1], min_val=NT, max_val=NT + E - 1)

        def tiles(e, up, down):
            up(e, 0)
            count = load_count(e)
            with e.Fori(1, count) as s:
                up(e, s, lambda: down(e, s - 1))
            down(e, e.value_load(small_i[0:1, 2:3], min_val=NT - 1, max_val=NT + E - 2))

        def expert_of(e, s):
            return e.value_load(table[0:1, bass.ds(s, 1)], min_val=0, max_val=E - 1)

        def sp_load(sp, s):
            sp.wait_ge(xT_ps, after(s))
            row = sp.value_load(rows[0:1, bass.ds(s, 1)], min_val=0, max_val=E * ROOM - 1)
            sp.dma_start(xin[:, :], slots_in[bass.ds(row * P, P), :]).then_inc(xin_loaded, 16)

        def pe_x(pe, s):
            pe.wait_ge(xin_loaded, after(s * 16 + 16))
            pe.wait_ge(xT_done, after(s))
            for k in range(KD):
                last = pe.transpose(b[0][:, k * P:(k + 1) * P], xin[:, k * P:(k + 1) * P], ident[:, :])
            last.then_inc(xT_ps, 1)

        def pe_up(pe, s, between=lambda: None):
            ex = expert_of(pe, s)
            pe.wait_ge(xT_done, after(s + 1))
            for bank, name in ((b[1], "gate"), (b[2], "up")):
                for k in range(KD):
                    last = pe.matmul(bank[:, :], xT[:, k, :], w[name][:, bass.ds(ex, 1), k, :].rearrange("p a f -> p (a f)"),
                                     start=(k == 0), stop=(k == KD - 1))
                last.then_inc(gu_ps, 1)
            pe_x(pe, s + 1)
            between()
            pe.wait_ge(h_done, after(s + 1))
            for k in range(KF):
                last = pe.transpose(b[3][:, k * P:(k + 1) * P], h[:, k * P:(k + 1) * P], ident[:, :])
            last.then_inc(hT_ps, 1)

        def pe_down(pe, s):
            ex = expert_of(pe, s)
            pe.wait_ge(hT_done, after(s + 1))
            pe.wait_ge(y_done, after(s))
            for k in range(KF):
                last = pe.matmul(b[4][:, 0:D], hT[:, k, :], w["down"][:, bass.ds(ex, 1), k, :].rearrange("p a f -> p (a f)"),
                                 start=(k == 0), stop=(k == KF - 1))
            last.then_inc(y_ps, 1)

        def act_x(act, s):
            act.wait_ge(xT_ps, after(s + 1))
            act.activation(xT[:, :, :].rearrange("p k t -> p (k t)"), b[0][:, 0:D], ACT.Copy).then_inc(xT_done, 1)

        def act_up(act, s, between=lambda: None):
            act.wait_ge(gu_ps, after(2 * s + 1))
            act.wait_ge(h_done, after(s))
            act.activation(sg[:, :], b[1][:, :], ACT.Silu).then_inc(sg_done, 1)
            act_x(act, s + 1)
            between()

        def act_down(act, s):
            act.wait_ge(y_ps, after(s + 1))
            act.wait_ge(y_stored, after(s * 16))
            act.activation(yout[:, :], b[4][:, 0:D], ACT.Copy).then_inc(y_done, 1)
            wait_apart(act, waits_passed_a, y_done, after(s + 1))
            act.dma_start(slots_out[bass.ds(s * P, P), :], yout[:, :]).then_inc(y_stored, 16)

        def dve_up(v, s, between=lambda: None):
            v.wait_ge(sg_done, after(s + 1))
            v.wait_ge(gu_ps, after(2 * s + 2))
            v.wait_ge(hT_ps, after(s))
            v.tensor_tensor(h[:, :], sg[:, :], b[2][:, :], ALU.mult).then_inc(h_done, 1)
            v.wait_ge(hT_ps, after(s + 1))
            v.tensor_copy(hT[:, :, :].rearrange("p k t -> p (k t)"), b[3][:, :]).then_inc(hT_done, 1)

        with nc.Block() as block:

            @block.tensor
            def _(pe):
                for s in w["loaded"][1:]:
                    pe.wait_ge(s, 16)
                pe_x(pe, 0)
                tiles(pe, pe_up, pe_down)

            @block.scalar
            def _(act):
                act.activation(sg[:, 0:1], c["eps"][:, 0:1], ACT.Silu)
                act.wait_ge(slots_zeroed, 16)
                act_x(act, 0)
                tiles(act, act_up, act_down)

            @block.vector
            def _(v):
                dve_rows_out(v)
                tiles(v, dve_up, lambda *_: None)
                if last:
                    last_dve(v)

            @block.gpsimd
            def _(g):
                g.memset(r["cum"][:, :, :], 0.0)
                if prepare:
                    prepare(g)
                if last:
                    g.wait_ge(loose_step, 6)
                    wait_apart(g, waits_passed_g, y_stored, g.value_load(
                        small_i[0:1, 1:2], min_val=START + 16 * NT, max_val=START + 16 * (NT + E - 1)))
                    last_pool(g)

            @block.sync
            def _(sp):
                count = load_count(sp)
                sp.wait_ge(r["scattered"][rows_from], 32 * NS)
                sp.wait_ge(r["tails_zeroed"][rows_from], 16 * E)
                sp_load(sp, 0)
                sp_load(sp, 1)
                if load_ahead:
                    load_ahead(sp)
                with sp.Fori(0, count) as s:
                    sp_load(sp, s + 2)
                stores = sp.value_load(small_i[0:1, 1:2], min_val=START + 16 * NT, max_val=START + 16 * (NT + E - 1))
                wait_apart(sp, waits_passed, y_stored, stores)
                wait_apart(sp, waits_passed, xin_loaded, stores + 32)
                if last:
                    last_sync(sp)


def griffin_weights(m, a):
    w, loads = {}, []
    for name, rows, cols in (("left_W", D, D), ("right_W", D, D), ("ga_W", D, D), ("gx_W", D, D), ("out_W", D, D),
                             ("up1_W", D, F), ("up2_W", D, F), ("down_W", F, D)):
        w[name] = m.sb("g_" + name, [P, rows // P, cols])
        loads.append((w[name][:, :, :], a[name].rearrange("(k p) f -> p k f", p=P)))
    for name, n in (("norm1_w", KD), ("left_b", KD), ("right_b", KD), ("g_conv_b", KD), ("ga_b", KD), ("gx_b", KD),
                    ("a_param", KD), ("norm2_w", KD), ("up1_b", KU), ("up2_b", KU)):
        w[name] = m.sb("g_" + name, [P, n])
        loads.append((w[name][:, :], a[name].rearrange("(k p) -> p k", p=P)))
    w["g_conv_w"] = m.sb("g_conv_w", [P, TAPS, KD])
    loads.append((w["g_conv_w"][:, :, :], a["g_conv_w"].rearrange("t (k p) -> p t k", p=P)))
    for name in ("out_b", "down_b"):
        w[name] = m.sb("g_" + name, [P, D])
        loads.append((w[name][:, :], a[name].partition_broadcast(P)))
    w["tap_b"] = m.sb("g_tap_b", [P, KD])
    return w, loads


def prepare_griffin_weights(g, w, n_loads, loaded, prepared):
    g.wait_ge(loaded, 16 * n_loads)
    g.tensor_tensor(w["tap_b"][:, :], w["g_conv_w"][:, TAPS - 1, :], w["right_b"][:, :], ALU.mult).then_inc(prepared, 1)
    g.wait_ge(prepared, 1)
    g.tensor_tensor(w["tap_b"][:, :], w["tap_b"][:, :], w["g_conv_b"][:, :], ALU.add).then_inc(prepared, 1)
    for name in ("ga_b", "gx_b"):
        g.tensor_scalar(w[name][:, :], w[name][:, :], 0.5, None, ALU.mult).then_inc(prepared, 1)
    for name, norm in (("left_W", "norm1_w"), ("right_W", "norm1_w"), ("up1_W", "norm2_w"), ("up2_W", "norm2_w")):
        for k in range(KD):
            g.tensor_scalar(w[name][:, k, :], w[name][:, k, :], w[norm][:, k:k + 1], None, ALU.mult).then_inc(prepared, 1)
    g.wait_ge(prepared, 4 + 4 * KD)


def griffin_phase(nc, c, w, experts, x, r, slots):
    ident = c["ident"]
    with ExitStack() as ctx:
        m = Phase(nc, ctx)
        sb, sem, loop_sem = m.sb, m.sem, m.loop_sem
        b = m.banks("gb")
        stats, mv, rstd, veps = (sb("g_" + n, s) for n, s in (
            ("stats", [P, 2, 6]), ("mv", [P, 2, 2]), ("rstd", [P, 2, 1]), ("veps", [P, 2, 1])))
        unit, s1, eps8 = sb("g_unit", [P, 2, 1]), sb("g_s1", [P, 2, 1]), sb("g_eps8", [P, 2])
        xl, xlb = sb("g_xl", [P, 2, D]), [sb(f"g_xlb{q}", [P, 2, D]) for q in range(2)]
        xn, xnT = sb("g_xn", [P, 2, D]), sb("g_xnT", [P, KD, ST])
        left = [sb(f"g_left{q}", [P, KD, ST]) for q in range(2)]
        rpre, xcv = sb("g_rpre", [P, KD, TAPS - 1 + ST]), sb("g_xcv", [P, KD, ST])
        tr, ti, a, tl, a2, u = (sb("g_" + n, [P, KD, ST]) for n in "tr ti a tl a2 u".split())
        carry = sb("g_carry", [P, KD])
        prod = [sb(f"g_prod{q}", [P, KD, ST]) for q in range(2)]
        sp4, sp4n, soft = sb("g_sp4", [P, KD]), sb("g_sp4n", [P, KD]), sb("g_soft", [P, 8, KD])
        x1, x1n, x1nT = sb("g_x1", [P, 2, D]), sb("g_x1n", [P, 2, D]), sb("g_x1nT", [P, KD, ST])
        ms, mse, s2 = sb("g_ms", [P, 2]), sb("g_mse", [P, 2]), sb("g_s2", [P, 2])
        sq = sb("g_sq", [P, 2, D], mybir.dt.bfloat16)
        gl = [sb(f"g_gl{j}", [P, ST]) for j in range(3)]
        up_banks = (b[4], b[6], b[7])
        mT = sb("g_mT", [P, KU, ST])

        names = ("stats_done mv_done norm_step xl_done xn_done xlb_done xdb_done xnT_ps xnT_done lr_ps left_done "
                 "rpre_done tap0_done conv_step halo_done gate_ps gates_done a_done tl_done a2_done q_done root_done "
                 "u_done b_done scan_done carry_done prod_done out_ps x1_done sq_done mse_done s2_done x1n_done "
                 "xadd_done x1nT_ps x1nT_done up_ps gl_done m_done down_ps x_done").split()
        S = {n: loop_sem("g_" + n) for n in names}
        gx = [sb(f"g_gx{q}", [P, 2, D]) for q in range(2)]
        now_i, now_p = ([sb(f"g_now_{n}{q}", [P, 2], t) for q in range(2)] for n, t in (("i", U32), ("p", F32)))
        S["now_done"], S["joined"] = loop_sem("g_now_done"), loop_sem("g_joined")
        S["gathered"] = r["gathered"]
        R = router_stage(m, c, experts, x, r, slots[0], "rg_", b[5],
                         x_wait=lambda v, s: v.wait_ge(S["x_done"], after(s + 1)),
                         pe_wait_x=lambda pe, s: None,
                         pe_wait_rank=lambda pe, s: None, rank_bank=b[0],
                         last_rows=xn, last_rows_free=lambda v: v.wait_ge(S["xnT_ps"], after(NS)))
        pe_group, dve_group, fill_tails = group_stage(m, c, r, R, slots[0], "rg_", b[3],
                                                      lambda pe: pe.wait_ge(S["x_done"], after(NS)))
        setup, exp_done, eps_made, passed_v, passed_g = (sem("g_" + n) for n in "setup exp_done eps_made passed_v passed_g".split())
        N_SETUP = 13
        xt2 = lambda s: x[:, bass.ds(2 * s, 2), :]
        row2 = lambda ap: ap.unsqueeze(1).to_broadcast([P, 2, D])

        def pe_transposes(pe, bank, src, done):
            for t in range(2):
                for k in range(KD):
                    last = pe.transpose(bank[:, k * ST + t * P:k * ST + (t + 1) * P], src[:, t, k * P:(k + 1) * P], ident[:, :])
            last.then_inc(done, 1)

        def pe_features(pe, bank, weight, rhs):
            for j in range(KD):
                for k in range(KD):
                    last = pe.matmul(bank[:, j * ST:(j + 1) * ST], w[weight][:, k, j * P:(j + 1) * P], rhs[:, k, :],
                                     start=(k == 0), stop=(k == KD - 1))
            return last

        def pe_A0(pe, s, q):
            pe.wait_ge(S["xn_done"], at(s, 2))
            pe.wait_ge(R["ranks_read"], R["ranks_read_after"](s - 3))
            pe_transposes(pe, b[0], xn, S["xnT_ps"])

        def pe_A1(pe, s, q):
            pe.wait_ge(S["xnT_done"], after(s + 1))
            pe.wait_ge(S["gates_done"], after(4 * s))
            pe_features(pe, b[1], "right_W", xnT).then_inc(S["lr_ps"], 1)
            pe_features(pe, b[2], "left_W", xnT).then_inc(S["lr_ps"], 1)

        def pe_A2(pe, s, q):
            pe.wait_ge(S["conv_step"], at(s, 6))
            pe_features(pe, b[1], "ga_W", xcv).then_inc(S["gate_ps"], 1)
            pe.wait_ge(S["left_done"], at(s, 2))
            pe_features(pe, b[2], "gx_W", xcv).then_inc(S["gate_ps"], 1)

        def pe_out(pe, s, q):
            pe.wait_ge(S["prod_done"], after(s + 1))
            pe.wait_ge(R["logits_read"], after(s - 1))
            for t in range(2):
                for k in range(KD):
                    last = pe.matmul(b[5][:, t * D:(t + 1) * D], prod[q][:, k, t * P:(t + 1) * P], w["out_W"][:, k, :],
                                     start=(k == 0), stop=(k == KD - 1))
            last.then_inc(S["out_ps"], 1)

        def pe_x1T(pe, s):
            pe.wait_ge(S["x1n_done"], at(s, 2))
            pe_transposes(pe, b[5], x1n, S["x1nT_ps"])
            pe.wait_ge(S["x1nT_done"], after(s + 1))

        def pe_up(pe, s, f0):
            for f in range(f0, f0 + KU // 2):
                pe.wait_ge(S["m_done"], after(KU * s + f - 2))
                for half, name in enumerate(("up1_W", "up2_W")):
                    for k in range(KD):
                        last = pe.matmul(up_banks[f % 3][:, half * ST:(half + 1) * ST], w[name][:, k, f * P:(f + 1) * P],
                                         x1nT[:, k, :], start=(k == 0), stop=(k == KD - 1))
                last.then_inc(S["up_ps"], 1)

        def pe_down(pe, s):
            pe.wait_ge(S["m_done"], at(s, KU))
            pe.wait_ge(S["x_done"], after(s))
            for t in range(2):
                for k in range(KU):
                    last = pe.matmul(b[3][:, t * D:(t + 1) * D], mT[:, k, t * P:(t + 1) * P], w["down_W"][:, k, :],
                                     start=(k == 0), stop=(k == KU - 1))
            last.then_inc(S["down_ps"], 1)

        def pe_body(pe, s, q, ahead, behind):
            R1, R2, R3 = R["pe"]
            pe_out(pe, s, q)
            if behind:
                pe_down(pe, s - 1)
            pe_x1T(pe, s)
            pe_up(pe, s, 0)
            if behind:
                R1(pe, s - 1)
            if ahead:
                pe_A2(pe, s + 1, 1 - q)
            if behind:
                R2(pe, s - 1)
            if ahead > 1:
                pe_A0(pe, s + 2, q)
            pe_up(pe, s, KU // 2)
            if ahead > 1:
                pe_A1(pe, s + 2, q)
            if behind:
                R3(pe, s - 1)

        def pe_end(pe):
            pe_down(pe, NS - 1)
            for piece in R["pe"]:
                piece(pe, NS - 1)
            pe_group(pe)

        def act_A0(act, s, q):
            act.wait_ge(S["xnT_ps"], after(s + 1))
            act.wait_ge(S["lr_ps"], after(2 * s))
            act.activation(xnT[:, :, :].rearrange("p k t -> p (k t)"), b[0][:, :], ACT.Copy).then_inc(S["xnT_done"], 1)

        def act_A1(act, s, q):
            act.wait_ge(S["lr_ps"], at(s, 2, 1))
            act.wait_ge(S["halo_done"], after(s + 1))
            act.wait_ge(S["gate_ps"], after(2 * s))
            act.wait_ge(S["u_done"], after(s))
            for j in range(KD):
                act.activation(rpre[:, j, TAPS - 1:], b[1][:, j * ST:(j + 1) * ST], ACT.Identity,
                               bias=w["right_b"][:, j:j + 1]).then_inc(S["rpre_done"], 1)
                act.activation(xcv[:, j, :], b[1][:, j * ST:(j + 1) * ST], ACT.Identity,
                               scale=w["g_conv_w"][:, TAPS - 1, j:j + 1], bias=w["tap_b"][:, j:j + 1]).then_inc(S["tap0_done"], 1)
            act.wait_ge(S["lr_ps"], at(s, 2, 2))
            act.wait_ge(S["prod_done"], after(s - 1))
            for j in range(KD):
                act.activation(left[q][:, j, :], b[2][:, j * ST:(j + 1) * ST], ACT.Gelu, bias=w["left_b"][:, j:j + 1]).then_inc(
                    S["left_done"], 1)

        def act_A2(act, s, q):
            act.wait_ge(S["tl_done"], after(2 * s))
            act.wait_ge(S["u_done"], after(s))
            for n, (dst, bias) in enumerate(((tr, "ga_b"), (ti, "gx_b"))):
                act.wait_ge(S["gate_ps"], at(s, 2, n + 1))
                for j in range(KD):
                    act.activation(dst[:, j, :], b[1 + n][:, j * ST:(j + 1) * ST], ACT.Tanh, scale=0.5,
                                   bias=w[bias][:, j:j + 1]).then_inc(S["gates_done"], 1)

        def act_A3(act, s, q):
            act.wait_ge(S["gates_done"], at(s, 4, 2))
            act.wait_ge(S["scan_done"], after(s))
            act.wait_ge(S["b_done"], after(s))
            for dst, func, by, done in ((a, ACT.Exp, sp4, "a_done"), (tl, ACT.Tanh, sp4n, "tl_done")):
                for j in range(KD):
                    act.activation(dst[:, j, :], tr[:, j, :], func, scale=by[:, j:j + 1], bias=by[:, j:j + 1]).then_inc(
                        S[done], 1)

        def act_root(act, s, q):
            act.wait_ge(S["q_done"], after(s + 1))
            act.activation(tl[:, :, :], a2[:, :, :], ACT.Sqrt, scale=0.25).then_inc(S["root_done"], 1)

        def act_sq(act, s):
            act.wait_ge(S["x1_done"], after(s + 1))
            act.wait_ge(S["mse_done"], after(s))
            for t in range(2):
                act.activation(sq[:, t, :], x1[:, t, :], ACT.Square, scale=D ** -0.5, accum_out=ms[:, t:t + 1]).then_inc(
                    S["sq_done"], 1)

        def act_x1T(act, s):
            act.wait_ge(S["x1nT_ps"], after(s + 1))
            act.wait_ge(S["up_ps"], after(KU * s))
            act.activation(x1nT[:, :, :].rearrange("p k t -> p (k t)"), b[5][:, :], ACT.Copy).then_inc(S["x1nT_done"], 1)

        def act_up(act, s, f0):
            for f in range(f0, f0 + KU // 2):
                act.wait_ge(S["up_ps"], at(s, KU, f + 1))
                act.wait_ge(S["m_done"], after(KU * s + f - 2))
                act.activation(gl[f % 3][:, :], up_banks[f % 3][:, 0:ST], ACT.Gelu, bias=w["up1_b"][:, f:f + 1]).then_inc(
                    S["gl_done"], 1)

        def act_body(act, s, q, ahead, behind):
            R1, R2 = R["act"]
            act_sq(act, s)
            act_x1T(act, s)
            act_up(act, s, 0)
            if behind:
                R1(act, s - 1)
            if ahead:
                act_A2(act, s + 1, 1 - q)
                act_A3(act, s + 1, 1 - q)
            if behind:
                R2(act, s - 1)
            if ahead:
                act_root(act, s + 1, 1 - q)
            if ahead > 1:
                act_A0(act, s + 2, q)
            act_up(act, s, KU // 2)
            if ahead > 1:
                act_A1(act, s + 2, q)

        def act_end(act):
            for piece in R["act"]:
                piece(act, NS - 1)
            fill_tails(act, 1)

        def dve_setup(v):
            n = [0]

            def step(instruction):
                n[0] += 1
                instruction.then_inc(setup, 1)
                v.wait_ge(setup, n[0])

            v.memset(carry[:, :], 0.0).then_inc(S["carry_done"], 1)
            v.memset(rpre[:, :, 0:TAPS - 1], 0.0).then_inc(S["halo_done"], 1)
            vv, nv, e, den, r, z, z2, p = (soft[:, i, :] for i in range(8))
            vv = w["a_param"][:, :]
            step(v.scalar_tensor_tensor(out=nv, in0=vv, scalar=-1.0, in1=vv, op0=ALU.mult, op1=ALU.min))
            v.wait_ge(exp_done, 1)
            step(v.tensor_scalar(den, e, 2.0, None, ALU.add))
            step(v.reciprocal(r, den))
            step(v.tensor_tensor(z, e, r, ALU.mult))
            step(v.tensor_tensor(z2, z, z, ALU.mult))
            step(v.tensor_scalar(p, z2, ATANH[4], ATANH[3], ALU.mult, ALU.add))
            step(v.scalar_tensor_tensor(out=p, in0=p, scalar=0.0, in1=z2, op0=ALU.add, op1=ALU.mult))
            step(v.scalar_tensor_tensor(out=p, in0=p, scalar=ATANH[2], in1=z2, op0=ALU.add, op1=ALU.mult))
            step(v.scalar_tensor_tensor(out=p, in0=p, scalar=ATANH[1], in1=z2, op0=ALU.add, op1=ALU.mult))
            step(v.scalar_tensor_tensor(out=p, in0=p, scalar=ATANH[0], in1=z, op0=ALU.add, op1=ALU.mult))
            step(v.scalar_tensor_tensor(out=p, in0=vv, scalar=0.0, in1=p, op0=ALU.max, op1=ALU.add))
            step(v.tensor_scalar(sp4[:, :], p, -C_RGLRU / 2, None, ALU.mult))
            step(v.tensor_scalar(sp4n[:, :], p, C_RGLRU / 2, None, ALU.mult))
            assert n[0] == N_SETUP, n[0]

        def dve_rows(v, s, q):
            v.wait_ge(S["joined"], after(2 * s - 2))
            v.tensor_copy(now_i[q][:, :], r["pos_i"][:, bass.ds(2 * s, 2)]).then_inc(S["now_done"], 1)
            v.tensor_copy(now_p[q][:, :], r["prob"][:, bass.ds(2 * s, 2)]).then_inc(S["now_done"], 1)

        def dve_join(v, s, q):
            v.wait_ge(S["now_done"], at(s, 2))
            v.wait_ge(S["gathered"][q], 16 * (s - q) + 32)
            for t in range(2):
                xs = x[:, bass.ds(2 * s + t, 1), :].rearrange("p a d -> p (a d)")
                v.scalar_tensor_tensor(out=xs, in0=gx[q][:, t, :], scalar=now_p[q][:, t:t + 1], in1=xs, op0=ALU.mult,
                                       op1=ALU.add).then_inc(S["joined"], 1)
            v.wait_ge(S["joined"], at(s, 2))

        def dve_stats(v, s, q):
            dve_join(v, s, q)
            dve_rows(v, s + 1, 1 - q)
            wait_apart(v, passed_v, S["norm_step"], at(s, 6, 0))
            for t in range(2):
                v.bn_stats(stats[:, t, :], x[:, bass.ds(2 * s + t, 1), :].rearrange("p a d -> p (a d)")).then_inc(
                    S["stats_done"], 1)
            for t in range(2):
                wait_apart(v, passed_v, S["stats_done"], at(s, 2, t + 1))
                v.bn_aggr(mv[:, t, :], stats[:, t, :]).then_inc(S["mv_done"], 1)

        def dve_xl(v, s, q):
            v.wait_ge(S["norm_step"], at(s, 6, 2))
            v.wait_ge(S["xlb_done"], after(s))
            for t in range(2):
                v.tensor_scalar(xl[:, t, :], x[:, bass.ds(2 * s + t, 1), :].rearrange("p a d -> p (a d)"),
                                mv[:, t, 0:1], rstd[:, t, :], ALU.subtract, ALU.mult).then_inc(S["xl_done"], 1)

        def dve_xn(v, s, q):
            v.wait_ge(S["xl_done"], at(s, 2))
            v.wait_ge(S["norm_step"], at(s, 6, 6))
            v.wait_ge(S["xnT_ps"], after(s))
            for t in range(2):
                v.tensor_scalar(xn[:, t, :], xl[:, t, :], s1[:, t, :], None, ALU.mult).then_inc(S["xn_done"], 1)

        def dve_conv(v, s, q):
            for n, tap in enumerate((2, 1, 0)):
                for j in range(KD):
                    if n:
                        v.wait_ge(S["conv_step"], at(s, 6, 2 * n + j - 1))
                    else:
                        v.wait_ge(S["tap0_done"], at(s, 2, j + 1))
                    v.scalar_tensor_tensor(out=xcv[:, j, :], in0=rpre[:, j, tap:tap + ST], scalar=w["g_conv_w"][:, tap, j:j + 1],
                                           in1=xcv[:, j, :], op0=ALU.mult, op1=ALU.add).then_inc(S["conv_step"], 1)
            v.wait_ge(S["conv_step"], at(s, 6))
            v.tensor_copy(rpre[:, :, 0:TAPS - 1], rpre[:, :, ST:ST + TAPS - 1]).then_inc(S["halo_done"], 1)

        def dve_q(v, s, q):
            v.wait_ge(S["gates_done"], at(s, 4))
            v.wait_ge(S["carry_done"], after(s + 1))
            v.wait_ge(S["prod_done"], after(s))
            v.scalar_tensor_tensor(out=u[:, :, :], in0=ti[:, :, :], scalar=1.0, in1=xcv[:, :, :], op0=ALU.add,
                                   op1=ALU.mult).then_inc(S["u_done"], 1)
            v.wait_ge(S["a_done"], at(s, 2))
            v.wait_ge(S["root_done"], after(s))
            v.tensor_tensor(a2[:, :, :], a[:, :, :], a[:, :, :], ALU.mult).then_inc(S["a2_done"], 1)
            v.wait_ge(S["a2_done"], after(s + 1))
            v.wait_ge(S["tl_done"], at(s, 2))
            v.scalar_tensor_tensor(out=a2[:, :, :], in0=a2[:, :, :], scalar=1.0, in1=tl[:, :, :], op0=ALU.add,
                                   op1=ALU.mult).then_inc(S["q_done"], 1)

        def dve_scan(v, s, q):
            v.wait_ge(S["root_done"], after(s + 1))
            v.tensor_tensor(u[:, :, :], u[:, :, :], tl[:, :, :], ALU.mult).then_inc(S["b_done"], 1)
            v.wait_ge(S["b_done"], after(s + 1))
            v.wait_ge(S["carry_done"], after(s + 1))
            for j in range(KD):
                last = v.tensor_tensor_scan(u[:, j, :], a[:, j, :], u[:, j, :], carry[:, j:j + 1], ALU.mult, ALU.add)
            last.then_inc(S["scan_done"], 1)
            v.wait_ge(S["scan_done"], after(s + 1))
            v.wait_ge(S["left_done"], at(s, 2))
            v.wait_ge(S["out_ps"], after(s - 1))
            v.tensor_tensor(prod[q][:, :, :], left[q][:, :, :], u[:, :, :], ALU.mult).then_inc(S["prod_done"], 1)
            v.tensor_copy(carry[:, :], u[:, :, ST - 1]).then_inc(S["carry_done"], 1)

        def dve_x1(v, s, q):
            v.wait_ge(S["out_ps"], after(s + 1))
            v.wait_ge(S["xlb_done"], after(s + 1))
            v.wait_ge(S["xadd_done"], after(s))
            v.tensor_tensor(x1[:, :, :].rearrange("p t d -> p (t d)"), b[5][:, :], xlb[q][:, :, :].rearrange("p t d -> p (t d)"),
                            ALU.add).then_inc(S["x1_done"], 1)

        def dve_x1n(v, s):
            v.wait_ge(S["s2_done"], after(s + 1))
            v.wait_ge(S["x1_done"], after(s + 1))
            v.wait_ge(S["x1nT_ps"], after(s))
            for t in range(2):
                v.tensor_scalar(x1n[:, t, :], x1[:, t, :], s2[:, t:t + 1], None, ALU.mult).then_inc(S["x1n_done"], 1)

        def dve_m(v, s, f0, f1):
            for f in range(f0, f1):
                v.wait_ge(S["gl_done"], at(s, KU, f + 1))
                v.wait_ge(S["down_ps"], after(s))
                v.scalar_tensor_tensor(out=mT[:, f, :], in0=up_banks[f % 3][:, ST:2 * ST], scalar=w["up2_b"][:, f:f + 1],
                                       in1=gl[f % 3][:, :], op0=ALU.add, op1=ALU.mult).then_inc(S["m_done"], 1)

        def dve_x(v, s):
            v.wait_ge(S["down_ps"], after(s + 1))
            v.wait_ge(S["xadd_done"], after(s + 1))
            v.tensor_tensor(xt2(s).rearrange("p t d -> p (t d)"), b[3][:, :], xt2(s).rearrange("p t d -> p (t d)"),
                            ALU.add).then_inc(S["x_done"], 1)

        def dve_body(v, s, q, ahead, behind):
            R0, R1, R2, R3 = R["dve"]
            dve_x1(v, s, q)
            if ahead > 1:
                dve_stats(v, s + 2, q)
            dve_x1n(v, s)
            if ahead:
                dve_conv(v, s + 1, 1 - q)
            if behind:
                dve_x(v, s - 1)
                R0(v, s - 1)
            if ahead > 1:
                dve_xl(v, s + 2, q)
            dve_m(v, s, 0, 1)
            if behind:
                R1(v, s - 1)
            dve_m(v, s, 1, 3)
            if ahead > 1:
                dve_xn(v, s + 2, q)
            if ahead:
                dve_q(v, s + 1, 1 - q)
            if behind:
                R2(v, s - 1)
            dve_m(v, s, 3, 5)
            if ahead:
                dve_scan(v, s + 1, 1 - q)
            dve_m(v, s, 5, 6)
            if behind:
                R3(v, s - 1)

        def dve_end(v):
            dve_x(v, NS - 1)
            for piece in R["dve"]:
                piece(v, NS - 1)
            dve_group(v)

        def pool_gather(g, s, q):
            wait_apart(g, passed_g, S["now_done"], at(s, 2))
            for t in range(2):
                g.indirect_dma_start(gx[q][:, t, :], None, slots[1][:, :],
                                     bass.IndirectOffsetOnAxis(now_i[q][:, t:t + 1], 0)).then_inc(S["gathered"][q], 16)

        def pool_norm(g, s, q):
            half_neg = c["half_neg"][:, :].unsqueeze(2)
            g.wait_ge(S["mv_done"], at(s, 2))
            g.wait_ge(S["xn_done"], after(2 * s))
            for n, (out, in0, in1, op) in enumerate((
                    (veps, mv[:, :, 1:2], c["eps"][:, :].unsqueeze(2), ALU.add),
                    (rstd, veps[:, :, :], half_neg, ALU.pow),
                    (unit, rstd[:, :, :], rstd[:, :, :], ALU.mult),
                    (unit, unit[:, :, :], mv[:, :, 1:2], ALU.mult),
                    (unit, unit[:, :, :], eps8[:, :].unsqueeze(2), ALU.add),
                    (s1, unit[:, :, :], half_neg, ALU.pow))):
                if n:
                    g.wait_ge(S["norm_step"], at(s, 6, n))
                g.tensor_tensor(out[:, :, :], in0, in1, op).then_inc(S["norm_step"], 1)

        def pool_biases(g, s, q):
            g.wait_ge(S["xl_done"], at(s, 2))
            g.wait_ge(S["x1_done"], after(s - 1))
            g.tensor_tensor(xlb[q][:, :, :], xl[:, :, :], row2(w["out_b"][:, :]), ALU.add).then_inc(S["xlb_done"], 1)
            wait_apart(g, passed_g, S["xl_done"], at(s, 2))
            g.tensor_tensor(xt2(s), xt2(s), row2(w["down_b"][:, :]), ALU.add).then_inc(S["xdb_done"], 1)

        def pool_s2(g, s):
            g.wait_ge(S["sq_done"], at(s, 2))
            g.tensor_tensor(mse[:, :], ms[:, :], eps8[:, :], ALU.add).then_inc(S["mse_done"], 1)
            g.wait_ge(S["mse_done"], after(s + 1))
            g.wait_ge(S["x1n_done"], after(2 * s))
            g.tensor_tensor(s2[:, :], mse[:, :], c["half_neg"][:, :], ALU.pow).then_inc(S["s2_done"], 1)

        def pool_xadd(g, s):
            wait_apart(g, passed_g, S["xdb_done"], after(s + 1))
            g.tensor_tensor(xt2(s), xt2(s), x1[:, :, :], ALU.add).then_inc(S["xadd_done"], 1)

        def pool_body(g, s, q, ahead, behind):
            R0, R2, R3, R4 = R["pool"]
            pool_s2(g, s)
            if ahead > 1:
                pool_norm(g, s + 2, q)
            pool_xadd(g, s)
            if behind:
                R0(g, s - 1)
            if ahead > 1:
                pool_gather(g, s + 3, 1 - q)
                pool_biases(g, s + 2, q)
            if behind:
                R2(g, s - 1)
                R3(g, s - 1)
                R4(g, s - 1)

        def pool_end(g):
            for piece in R["pool"][:3]:
                piece(g, NS - 1)

        def program(e, stage_1, stage_2, body, end):
            stage_1(e, 0, 0)
            stage_2(e, 0, 0)
            stage_1(e, 1, 1)
            body(e, 0, 0, 2, False)
            with e.Fori(0, NS // 2 - 2) as i:
                body(e, 2 * i + 1, 1, 2, True)
                body(e, 2 * i + 2, 0, 2, True)
            for s in range(NS - 3, NS):
                body(e, s, s % 2, min(2, NS - 1 - s), True)
            end(e)

        def all_of(*pieces):
            def run(*args):
                for piece in pieces:
                    piece(*args)
            return run

        m.start_loop_sems()
        with nc.Block() as block:

            @block.sync
            def _(sp):
                fill_tails(sp, 0)

            @block.tensor
            def _(pe):
                program(pe, all_of(pe_A0, pe_A1), pe_A2, pe_body, pe_end)

            @block.scalar
            def _(act):
                act.wait_ge(setup, 1)
                act.activation(soft[:, 2, :], soft[:, 1, :], ACT.Exp).then_inc(exp_done, 1)
                act.wait_ge(setup, N_SETUP)
                program(act, all_of(act_A0, act_A1), all_of(act_A2, act_A3, act_root), act_body, act_end)

            @block.vector
            def _(v):
                dve_rows(v, 0, 0)
                dve_setup(v)
                program(v, all_of(dve_stats, dve_xl, dve_xn), all_of(dve_conv, dve_q, dve_scan), dve_body, dve_end)
                v.wait_ge(R["noted"], after(3 * NS))

            @block.gpsimd
            def _(g):
                g.memset(eps8[:, :], 1e-8).then_inc(eps_made, 1)
                g.wait_ge(eps_made, 1)
                pool_gather(g, 0, 0)
                program(g, all_of(pool_norm, lambda e, s, q: pool_gather(e, s + 1, 1 - q), pool_biases), lambda *_: None,
                        pool_body, pool_end)
                g.wait_ge(S["gathered"][0], 16 * NS + 32)


_PARTS = {"u": "L0_attn_a_u", "W_in": "L0_attn_a_W_in", "conv_w": "L0_attn_a_conv_w", "conv_b": "L0_attn_a_conv_b",
          "dt_bias": "L0_attn_a_dt_bias", "A_log": "L0_attn_a_A_log", "Dp": "L0_attn_a_Dp",
          "norm_w": "L0_attn_a_norm_w", "W_out": "L0_attn_a_W_out",
          "router": "L0_ffn_router_w", "gate": "L0_ffn_gate_w", "up": "L0_ffn_up_w", "down": "L0_ffn_down_w",
          "g_conv_w": "L0_attn_b_conv_w", "g_conv_b": "L0_attn_b_conv_b"}
_PARTS.update({n: "L0_attn_b_" + n for n in (
    "norm1_w left_W left_b right_W right_b ga_W ga_b gx_W gx_b a_param out_W out_b norm2_w up1_W up1_b up2_W up2_b "
    "down_W down_b").split()})


def build(nc, a, out):
    with ExitStack() as ctx:
        m = Memory(nc, ctx)
        x = m.sb("x", [P, NT, D])
        x_loaded = [m.sem(f"x_loaded{t}") for t in range(4)]
        zeros, zeros_made, slots_zeroed = m.sb("zeros", [P, D]), m.sem("zeros_made"), m.sem("slots_zeroed")
        r = {"prob": m.sb("prob", [P, NT + 2]), "onehot": m.sb("onehot", [P, NT, E]), "pos": m.sb("pos", [P, NT]),
             "pos_i": m.sb("pos_i", [P, NT + 2], U32), "cum": m.sb("cum", [P, 2, E]),
             "need": m.sb("need", [P, E]), "ends": m.sb("ends", [P, E]), "table": m.sb("table", [1, MAXT], I32),
             "rows": m.sb("rows", [1, MAXT], I32), "small_i": m.sb("small_i", [1, 3], I32), "tails": m.sb("tails", [1, E], I32),
             "tails_zeroed": {tag: m.sem(tag + "tails_zeroed") for tag in ("ra_", "rg_")},
             "scattered": {tag: m.sem(tag + "scattered") for tag in ("ra_", "rg_")},
             "gathered": [m.sem(f"gathered{q}") for q in range(2)], "gathered_last": [m.sem(f"gathered_last{s}") for s in range(NS)]}
        c = make_constants(m, zeros, zeros_made, r["cum"])
        c["zeros"] = zeros
        w = {"router": m.sb("router", [P, KD, E]), "gate": m.sb("gate", [P, E, KD, FI]), "up": m.sb("up", [P, E, KD, FI]),
             "down": m.sb("down", [P, E, KF, D]), "loaded": [m.sem(f"experts_loaded{k}") for k in range(4)]}
        slots = [nc.dram_tensor(n, (k * P, D), F32).ap() for n, k in (("slots_in", E * ROOM), ("slots_out", MAXT))]

        def load_experts(sp):
            sp.wait_ge(zeros_made, 1)
            sp.dma_start(slots[1].rearrange("(t p) d -> p t d", p=P), zeros[:, :].unsqueeze(1).to_broadcast([P, MAXT, D])).then_inc(
                slots_zeroed, 16)
            for k, name in enumerate(("gate", "up", "down")):
                sp.dma_start(w[name][:, :, :, :], a[name].rearrange("e (k p) f -> p e k f", p=P)).then_inc(w["loaded"][k + 1], 16)

        def load_router(sp):
            sp.dma_start(w["router"][:, :, :], a["router"].rearrange("(k p) e -> p k e", p=P)).then_inc(w["loaded"][0], 16)

        moe_sems = {tag: MoeSems(m, tag) for tag in ("f1_", "f2_")}
        mamba = mamba_phase(nc, a, c, w, x, r, slots[0], x_loaded, load_router, load_experts,
                            [s for sems in moe_sems.values() for s in sems.loop_sems])
        gw, loads = griffin_weights(m, a)
        griffin_loaded = m.sem("griffin_loaded")

        def load_griffin(sp):
            for dst, src in loads:
                sp.dma_start(dst, src, allow_slow_non_contiguous=True).then_inc(griffin_loaded, 16)

        griffin_prepared = m.sem("griffin_prepared")

        def prepare_griffin(g):
            mamba.clear(g)
            prepare_griffin_weights(g, gw, len(loads), griffin_loaded, griffin_prepared)

        moe_phase(nc, c, w, slots, slots_zeroed, r, "ra_", "f1_", moe_sems["f1_"],
                  load_ahead=load_griffin, prepare=prepare_griffin)
        griffin_phase(nc, c, gw, w, x, r, slots)
        moe_phase(nc, c, w, slots, slots_zeroed, r, "rg_", "f2_", moe_sems["f2_"],
                  last=lambda m: finish(m, x, r, slots[1], out))


def finish(m, x, r, slots_out, out):
    gx = m.sb("gx", [P, NT, D])
    gathered, joined, stored = r["gathered_last"], m.sem("joined"), m.sem("stored")

    def pool(g):
        for t in range(NT):
            g.indirect_dma_start(gx[:, t, :], None, slots_out[:, :],
                                 bass.IndirectOffsetOnAxis(r["pos_i"][:, t:t + 1], 0)).then_inc(gathered[t // 2], 16)

    def dve(v):
        for t in range(NT):
            v.wait_ge(gathered[t // 2], 32)
            v.scalar_tensor_tensor(out=x[:, t, :], in0=gx[:, t, :], scalar=r["prob"][:, t:t + 1], in1=x[:, t, :],
                                   op0=ALU.mult, op1=ALU.add).then_inc(joined, 1)

    def sync(sp):
        for s in range(NS):
            sp.wait_ge(joined, 2 * s + 2)
            sp.dma_start(out[0, s * ST:(s + 1) * ST, :].rearrange("(r p) d -> p r d", p=P),
                         x[:, 2 * s:2 * s + 2, :]).then_inc(stored, 16)
        sp.wait_ge(stored, 16 * NS)

    return pool, dve, sync


def kernel(**inputs):
    import numpy as _np
    import concourse.bacc as _bacc
    from concourse import mybir as _mybir
    from concourse.bass_utils import run_bass_kernel_spmd as _run

    nc = _bacc.Bacc("TRN2", target_bir_lowering=False, num_devices=1)
    arrays, args = {}, {}
    for short, name in _PARTS.items():
        v = _np.ascontiguousarray(inputs[name])
        arrays[f"in_{name}_dram"] = v
        args[short] = nc.dram_tensor(f"in_{name}_dram", v.shape, _mybir.dt.from_np(v.dtype), kind="ExternalInput").ap()
    out = nc.dram_tensor("out_0_dram", (1, TOKENS, D), _mybir.dt.float32, kind="ExternalOutput").ap()
    build(nc, args, out)
    r = _run(nc, [arrays], core_ids=[0])
    return r.results[0]["out_0_dram"]
```
